# Optimizing a Trainium2 kernel written in Bass

```python
import numpy as np
import jax
import jax.numpy as jnp

def _softmax(x, axis=-1):
    return jax.nn.softmax(x, axis=axis)

def _gelu(x):
    return jax.nn.gelu(x, approximate=True)

def _silu(x):
    return jax.nn.silu(x)

def _sigmoid(x):
    return jax.nn.sigmoid(x)

def _layernorm(x, axis=-1, eps=1e-05):
    m = jnp.mean(x, axis=axis, keepdims=True)
    v = jnp.var(x, axis=axis, keepdims=True)
    return (x - m) / jnp.sqrt(v + eps)

def _scatter_add(tgt, idx, src, axis=0):
    return tgt.at[idx].add(src)

def _segment_sum(src, seg, n):
    return jax.ops.segment_sum(src, seg, n)
kernel_name = 'mk_decoder_postln_d2_seqx_r8_c8c1a5'

def setup_inputs(seed: int=0):
    np.random.seed(seed)
    _w = jnp.asarray

    def _rec_inputs():
        import jax
        import jax.numpy as jnp
        _rk = jax.random.key(seed)
        x = -0.0003929 + 0.9999 * jax.random.normal(jax.random.fold_in(_rk, 1), (8, 128, 128), jnp.float32)
        _lenS = 128 - jax.random.randint(jax.random.fold_in(_rk, 7), (8,), 0, max(1, 128 // 4) + 1, jnp.int32)
        _lenS2 = 120 - jax.random.randint(jax.random.fold_in(_rk, 8), (8,), 0, max(1, 120 // 4) + 1, jnp.int32)
        _ctx_768P = jax.random.normal(jax.random.fold_in(_rk, 11), (8, 16, 96), jnp.float32)
        _ctx_768c = jax.random.dirichlet(jax.random.fold_in(_rk, 511), 0.3 * jnp.ones((16,), jnp.float32), (8, 120))
        _ctx_768t = jnp.einsum('bsk,bkd->bsd', _ctx_768c, _ctx_768P)
        _ctx_768t = _ctx_768t * jax.lax.rsqrt(jnp.mean(jnp.square(_ctx_768t)) + 1e-12) * 0.953939
        ctx_768 = -7.36909e-05 + 0.999899 * (_ctx_768t + 0.3 * jax.random.normal(jax.random.fold_in(_rk, 611), (8, 120, 96), jnp.float32))
        return (x, ctx_768)
    x, ctx_768 = _rec_inputs()

    def _L0_attn_setup():
        import jax, jax.numpy as jnp
        import numpy as np
        NUM_HEADS = 16
        DEPTH = 0

        def rotate_half(x):
            x1, x2 = jnp.split(x, 2, axis=-1)
            return jnp.concatenate((-x2, x1), axis=-1)

        def rotary_tables(seq_len, rot_dim, dtype):
            inv_freq = 1.0 / 10000.0 ** (jnp.arange(0, rot_dim, 2, dtype=jnp.float32) / rot_dim)
            freqs = jnp.arange(seq_len, dtype=jnp.float32)[:, None] * inv_freq[None, :]
            emb = jnp.concatenate((freqs, freqs), axis=-1)
            return (emb.astype(dtype), jnp.cos(emb).astype(dtype), jnp.sin(emb).astype(dtype))
        key = jax.random.key(seed)
        ks = jax.random.split(key, 7)
        B, N, C = (1, 256, 128)
        hd = C // NUM_HEADS
        std_qkv = (1.0 / C) ** 0.5
        std_proj = (1.0 / (2 * C)) ** 0.5
        return {'x': jax.random.normal(ks[0], (B, N, C), dtype=jnp.float32), 'W_qkv': jax.random.normal(ks[1], (6 * C, C), dtype=jnp.float32) * std_qkv, 'W_proj': jax.random.normal(ks[2], (C, 2 * C), dtype=jnp.float32) * std_proj, 'lambda_q1': jax.random.normal(ks[3], (hd,), dtype=jnp.float32) * 0.1, 'lambda_q2': jax.random.normal(ks[4], (hd,), dtype=jnp.float32) * 0.1, 'lambda_k1': jax.random.normal(ks[5], (hd,), dtype=jnp.float32) * 0.1, 'lambda_k2': jax.random.normal(ks[6], (hd,), dtype=jnp.float32) * 0.1}
    _L0_attn_all = _L0_attn_setup()
    _L0_attn_in = {k: v for k, v in _L0_attn_all.items() if k in ('W_qkv', 'W_proj', 'lambda_q1', 'lambda_q2', 'lambda_k1', 'lambda_k2')}
    del _L0_attn_all

    def _L0_xattn_setup():
        import jax, jax.numpy as jnp
        import numpy as np
        IMG_DIM, TXT_DIM, HID = (128, 96, 128)
        B, LQ, LK = (8, 256, 256)
        key = jax.random.key(seed)
        ks = jax.random.split(key, 8)
        s_img = 1.0 / np.sqrt(IMG_DIM)
        s_txt = 1.0 / np.sqrt(TXT_DIM)
        return {'image_features': jax.random.normal(ks[0], (B, LQ, IMG_DIM), jnp.float32), 'text_features': jax.random.normal(ks[1], (B, LK, TXT_DIM), jnp.float32), 'Wq': jax.random.uniform(ks[2], (IMG_DIM, HID), jnp.float32, -s_img, s_img), 'bq': jax.random.uniform(ks[3], (HID,), jnp.float32, -s_img, s_img), 'Wk': jax.random.uniform(ks[4], (TXT_DIM, HID), jnp.float32, -s_txt, s_txt), 'bk': jax.random.uniform(ks[5], (HID,), jnp.float32, -s_txt, s_txt), 'Wv': jax.random.uniform(ks[6], (TXT_DIM, HID), jnp.float32, -s_txt, s_txt), 'bv': jax.random.uniform(ks[7], (HID,), jnp.float32, -s_txt, s_txt)}
    _L0_xattn_all = _L0_xattn_setup()
    _L0_xattn_in = {k: v for k, v in _L0_xattn_all.items() if k in ('Wq', 'bq', 'Wk', 'bk', 'Wv', 'bv')}
    del _L0_xattn_all

    def _L0_ffn_setup():
        import jax, jax.numpy as jnp
        import numpy as np
        NUM_EXPERTS = 8
        CAPACITY_FACTOR = 1.0
        key = jax.random.key(seed)
        k1, k2, k3, k4 = jax.random.split(key, 4)
        B, S, D, E, F = (8, 256, 128, NUM_EXPERTS, 512)
        x = jax.random.normal(k1, (B, S, D), dtype=jnp.float32)
        router_w = jax.random.normal(k2, (D, E), dtype=jnp.float32) * D ** (-0.5)
        w1 = jax.random.normal(k3, (E, D, F), dtype=jnp.float32) * D ** (-0.5)
        w2 = jax.random.normal(k4, (E, F, D), dtype=jnp.float32) * F ** (-0.5)
        return {'x': x, 'router_w': router_w, 'w1': w1, 'w2': w2}
    _L0_ffn_all = _L0_ffn_setup()
    _L0_ffn_in = {k: v for k, v in _L0_ffn_all.items() if k in ('router_w', 'w1', 'w2')}
    del _L0_ffn_all

    def _L1_attn_setup():
        import jax, jax.numpy as jnp
        import numpy as np
        import math
        DIM = 128
        N_HEADS = 16
        HEAD_DIM = DIM // N_HEADS
        B, S = (2, 256)
        key = jax.random.key(seed)
        k_x, k_wqkv, k_bqkv, k_wout, k_bout = jax.random.split(key, 5)
        scale_in = 1.0 / math.sqrt(DIM)
        x = jax.random.normal(k_x, (B, S, DIM), dtype=jnp.float32)
        Wqkv = jax.random.uniform(k_wqkv, (N_HEADS, DIM, 3 * HEAD_DIM), dtype=jnp.float32, minval=-scale_in, maxval=scale_in)
        bqkv = jax.random.uniform(k_bqkv, (N_HEADS, 3 * HEAD_DIM), dtype=jnp.float32, minval=-scale_in, maxval=scale_in)
        Wout = jax.random.uniform(k_wout, (DIM, DIM), dtype=jnp.float32, minval=-scale_in, maxval=scale_in)
        bout = jax.random.uniform(k_bout, (DIM,), dtype=jnp.float32, minval=-scale_in, maxval=scale_in)
        return {'x': x, 'Wqkv': Wqkv, 'bqkv': bqkv, 'Wout': Wout, 'bout': bout}
    _L1_attn_all = _L1_attn_setup()
    _L1_attn_in = {k: v for k, v in _L1_attn_all.items() if k in ('Wqkv', 'bqkv', 'Wout', 'bout')}
    del _L1_attn_all

    def _L1_xattn_setup():
        import jax, jax.numpy as jnp
        import numpy as np
        NUM_HEADS = 16
        HEAD_DIM = 64
        INNER = NUM_HEADS * HEAD_DIM
        QUERY_DIM = 128
        CONTEXT_DIM = 96
        SCALE = HEAD_DIM ** (-0.5)
        key = jax.random.key(seed)
        ks = jax.random.split(key, 6)
        B, NQ, NKV = (8, 128, 256)
        query = jax.random.normal(ks[0], (B, NQ, QUERY_DIM), dtype=jnp.float32)
        context = jax.random.normal(ks[1], (B, NKV, CONTEXT_DIM), dtype=jnp.float32)
        w_q = jax.random.normal(ks[2], (QUERY_DIM, INNER), dtype=jnp.float32) * QUERY_DIM ** (-0.5)
        w_kv = jax.random.normal(ks[3], (CONTEXT_DIM, 2 * INNER), dtype=jnp.float32) * CONTEXT_DIM ** (-0.5)
        w_out = jax.random.normal(ks[4], (INNER, QUERY_DIM), dtype=jnp.float32) * INNER ** (-0.5)
        b_out = jax.random.normal(ks[5], (QUERY_DIM,), dtype=jnp.float32) * 0.01
        return {'query': query, 'context': context, 'w_q': w_q, 'w_kv': w_kv, 'w_out': w_out, 'b_out': b_out}
    _L1_xattn_all = _L1_xattn_setup()
    _L1_xattn_in = {k: v for k, v in _L1_xattn_all.items() if k in ('w_q', 'w_kv', 'w_out', 'b_out')}
    del _L1_xattn_all

    def _L1_ffn_setup():
        import jax, jax.numpy as jnp
        import numpy as np
        E = 16
        K = 4
        B, S, H, I = (4, 128, 128, 256)
        key = jax.random.key(seed)
        k0, k1, k2, k3 = jax.random.split(key, 4)
        scale = 0.02
        return {'hidden_states': jax.random.normal(k0, (B, S, H), jnp.float32), 'router_w': jax.random.normal(k1, (H, E), jnp.float32) * scale, 'router_b': jnp.zeros((E,), jnp.float32), 'w1': jax.random.normal(k2, (E, H, I), jnp.float32) * scale, 'b1': jnp.zeros((E, I), jnp.float32), 'w2': jax.random.normal(k3, (E, I, H), jnp.float32) * scale, 'b2': jnp.zeros((E, H), jnp.float32)}
    _L1_ffn_all = _L1_ffn_setup()
    _L1_ffn_in = {k: v for k, v in _L1_ffn_all.items() if k in ('router_w', 'router_b', 'w1', 'b1', 'w2', 'b2')}
    del _L1_ffn_all
    return {'x': x, 'ctx_768': ctx_768, 'L0_attn_W_qkv': _L0_attn_in['W_qkv'], 'L0_attn_W_proj': _L0_attn_in['W_proj'], 'L0_attn_lambda_q1': _L0_attn_in['lambda_q1'], 'L0_attn_lambda_q2': _L0_attn_in['lambda_q2'], 'L0_attn_lambda_k1': _L0_attn_in['lambda_k1'], 'L0_attn_lambda_k2': _L0_attn_in['lambda_k2'], 'L0_xattn_Wq': _L0_xattn_in['Wq'], 'L0_xattn_bq': _L0_xattn_in['bq'], 'L0_xattn_Wk': _L0_xattn_in['Wk'], 'L0_xattn_bk': _L0_xattn_in['bk'], 'L0_xattn_Wv': _L0_xattn_in['Wv'], 'L0_xattn_bv': _L0_xattn_in['bv'], 'L0_ffn_router_w': _L0_ffn_in['router_w'], 'L0_ffn_w1': _L0_ffn_in['w1'], 'L0_ffn_w2': _L0_ffn_in['w2'], 'L1_attn_Wqkv': _L1_attn_in['Wqkv'], 'L1_attn_bqkv': _L1_attn_in['bqkv'], 'L1_attn_Wout': _L1_attn_in['Wout'], 'L1_attn_bout': _L1_attn_in['bout'], 'L1_xattn_w_q': _L1_xattn_in['w_q'], 'L1_xattn_w_kv': _L1_xattn_in['w_kv'], 'L1_xattn_w_out': _L1_xattn_in['w_out'], 'L1_xattn_b_out': _L1_xattn_in['b_out'], 'L1_ffn_router_w': _L1_ffn_in['router_w'], 'L1_ffn_router_b': _L1_ffn_in['router_b'], 'L1_ffn_w1': _L1_ffn_in['w1'], 'L1_ffn_b1': _L1_ffn_in['b1'], 'L1_ffn_w2': _L1_ffn_in['w2'], 'L1_ffn_b2': _L1_ffn_in['b2']}

def reference(x, ctx_768, L0_attn_W_qkv, L0_attn_W_proj, L0_attn_lambda_q1, L0_attn_lambda_q2, L0_attn_lambda_k1, L0_attn_lambda_k2, L0_xattn_Wq, L0_xattn_bq, L0_xattn_Wk, L0_xattn_bk, L0_xattn_Wv, L0_xattn_bv, L0_ffn_router_w, L0_ffn_w1, L0_ffn_w2, L1_attn_Wqkv, L1_attn_bqkv, L1_attn_Wout, L1_attn_bout, L1_xattn_w_q, L1_xattn_w_kv, L1_xattn_w_out, L1_xattn_b_out, L1_ffn_router_w, L1_ffn_router_b, L1_ffn_w1, L1_ffn_b1, L1_ffn_w2, L1_ffn_b2):
    import jax
    import jax.numpy as jnp

    def _L0_attn_ref(x, W_qkv, W_proj, lambda_q1, lambda_q2, lambda_k1, lambda_k2):
        import jax, jax.numpy as jnp
        import numpy as np
        NUM_HEADS = 16
        DEPTH = 0

        def rotate_half(x):
            x1, x2 = jnp.split(x, 2, axis=-1)
            return jnp.concatenate((-x2, x1), axis=-1)

        def rotary_tables(seq_len, rot_dim, dtype):
            inv_freq = 1.0 / 10000.0 ** (jnp.arange(0, rot_dim, 2, dtype=jnp.float32) / rot_dim)
            freqs = jnp.arange(seq_len, dtype=jnp.float32)[:, None] * inv_freq[None, :]
            emb = jnp.concatenate((freqs, freqs), axis=-1)
            return (emb.astype(dtype), jnp.cos(emb).astype(dtype), jnp.sin(emb).astype(dtype))
        B, N, C = x.shape
        H = NUM_HEADS
        hd = C // H
        scale = hd ** (-0.5)
        lambda_init = 0.8 - 0.6 * np.exp(-0.3 * DEPTH)
        qkv = jnp.einsum('bnc,dc->bnd', x, W_qkv)
        qkv = qkv.reshape(B, N, 6, H, hd).transpose(2, 0, 3, 1, 4)
        q = jnp.concatenate((qkv[0], qkv[1]), axis=-1)
        k = jnp.concatenate((qkv[2], qkv[3]), axis=-1)
        v = jnp.concatenate((qkv[4], qkv[5]), axis=-1)
        _, cos, sin = rotary_tables(N, 2 * hd, x.dtype)
        q = q * cos + rotate_half(q) * sin
        k = k * cos + rotate_half(k) * sin
        q1, q2 = jnp.split(q, 2, axis=-1)
        k1, k2 = jnp.split(k, 2, axis=-1)
        attn1 = jnp.einsum('bhid,bhjd->bhij', q1, k1) * scale
        attn2 = jnp.einsum('bhid,bhjd->bhij', q2, k2) * scale
        lam1 = jnp.exp(jnp.sum(lambda_q1 * lambda_k1))
        lam2 = jnp.exp(jnp.sum(lambda_q2 * lambda_k2))
        lam = (lam1 - lam2 + lambda_init).astype(x.dtype)
        probs = jax.nn.softmax(attn1, axis=-1) - lam * jax.nn.softmax(attn2, axis=-1)
        out = jnp.einsum('bhij,bhjd->bhid', probs, v)
        out = out.transpose(0, 2, 1, 3).reshape(B, N, 2 * C)
        out = jnp.einsum('bnd,cd->bnc', out, W_proj)
        return out

    def _L0_xattn_ref(image_features, text_features, Wq, bq, Wk, bk, Wv, bv):
        import jax, jax.numpy as jnp
        import numpy as np
        IMG_DIM, TXT_DIM, HID = (128, 96, 128)
        B, LQ, LK = (8, 256, 256)
        query = jnp.einsum('bqi,ih->bqh', image_features, Wq) + bq
        key = jnp.einsum('bkt,th->bkh', text_features, Wk) + bk
        value = jnp.einsum('bkt,th->bkh', text_features, Wv) + bv
        scale = 1.0 / jnp.sqrt(jnp.asarray(HID, query.dtype))
        scores = jnp.einsum('bqh,bkh->bqk', query, key) * scale
        weights = jax.nn.softmax(scores, axis=-1)
        attended = jnp.einsum('bqk,bkh->bqh', weights, value)
        return attended

    def _L0_ffn_ref(x, router_w, w1, w2):
        import jax, jax.numpy as jnp
        import numpy as np
        NUM_EXPERTS = 8
        CAPACITY_FACTOR = 1.0
        B, S, D = x.shape
        E = router_w.shape[1]
        T = B * S
        C = int(CAPACITY_FACTOR * T / E)
        x_flat = x.reshape(T, D)
        logits = x_flat @ router_w
        probs = jax.nn.softmax(logits, axis=-1)
        expert_idx = jnp.argmax(probs, axis=-1)
        gate = jnp.take_along_axis(probs, expert_idx[:, None], axis=1)[:, 0]
        onehot = jax.nn.one_hot(expert_idx, E, dtype=jnp.float32)
        pos_all = jnp.cumsum(onehot, axis=0) - 1.0
        pos = jnp.take_along_axis(pos_all, expert_idx[:, None], axis=1)[:, 0]
        pos = pos.astype(jnp.int32)
        keep = (pos < C).astype(x_flat.dtype)
        pos_c = jnp.clip(pos, 0, C - 1)
        expert_in = jnp.zeros((E, C, D), dtype=x_flat.dtype)
        expert_in = expert_in.at[expert_idx, pos_c].add(x_flat * keep[:, None])
        hidden = jax.nn.gelu(jnp.einsum('ecd,edf->ecf', expert_in, w1))
        expert_out = jnp.einsum('ecf,efd->ecd', hidden, w2)
        y = expert_out[expert_idx, pos_c] * (gate * keep)[:, None]
        return y.reshape(B, S, D)

    def _L1_attn_ref(x, Wqkv, bqkv, Wout, bout):
        import jax, jax.numpy as jnp
        import numpy as np
        import math
        DIM = 128
        N_HEADS = 16
        HEAD_DIM = DIM // N_HEADS
        B, S = (2, 256)
        b, s, d = x.shape
        qkv = jnp.einsum('bsd,hde->bhse', x, Wqkv) + bqkv[None, :, None, :]
        q, k, v = jnp.split(qkv, 3, axis=-1)
        score = jnp.einsum('bhsd,bhtd->bhst', q, k)
        causal = jnp.tril(jnp.ones((s, s), dtype=bool))
        score = jnp.where(causal[None, None], score, -jnp.inf)
        attn = jax.nn.softmax(score / jnp.sqrt(jnp.asarray(HEAD_DIM, x.dtype)), axis=-1)
        y = jnp.einsum('bhst,bhtd->bhsd', attn, v)
        y = jnp.transpose(y, (0, 2, 1, 3)).reshape(b, s, d)
        out = y @ Wout + bout
        return out

    def _L1_xattn_ref(query, context, w_q, w_kv, w_out, b_out):
        import jax, jax.numpy as jnp
        import numpy as np
        NUM_HEADS = 16
        HEAD_DIM = 64
        INNER = NUM_HEADS * HEAD_DIM
        QUERY_DIM = 128
        CONTEXT_DIM = 96
        SCALE = HEAD_DIM ** (-0.5)
        B, NQ, _ = query.shape
        NKV = context.shape[1]
        q = query @ w_q
        kv = context @ w_kv
        k, v = jnp.split(kv, 2, axis=-1)
        q = q.reshape(B, NQ, NUM_HEADS, HEAD_DIM).transpose(0, 2, 1, 3)
        k = k.reshape(B, NKV, NUM_HEADS, HEAD_DIM).transpose(0, 2, 1, 3)
        v = v.reshape(B, NKV, NUM_HEADS, HEAD_DIM).transpose(0, 2, 1, 3)
        scores = jnp.einsum('bhqd,bhkd->bhqk', q, k) * SCALE
        attn = jax.nn.softmax(scores, axis=-1)
        out = jnp.einsum('bhqk,bhkd->bhqd', attn, v)
        out = out.transpose(0, 2, 1, 3).reshape(B, NQ, INNER)
        return out @ w_out + b_out

    def _L1_ffn_ref(hidden_states, router_w, router_b, w1, b1, w2, b2):
        import jax, jax.numpy as jnp
        import numpy as np
        E = 16
        K = 4
        B, S, H, I = (4, 128, 128, 256)
        b, s, h = hidden_states.shape
        logits = hidden_states @ router_w + router_b
        probs = jax.nn.softmax(logits, axis=-1)
        topw, topi = jax.lax.top_k(probs, K)
        topw = topw / jnp.sum(topw, axis=-1, keepdims=True)
        combine = jnp.sum(jax.nn.one_hot(topi, E, dtype=hidden_states.dtype) * topw[..., None], axis=2)
        x = hidden_states.reshape(b * s, h)
        c = combine.reshape(b * s, E)

        def body(acc, expert):
            w1e, b1e, w2e, b2e, ce = expert
            hmid = jax.nn.gelu(x @ w1e + b1e, approximate=False)
            return (acc + (hmid @ w2e + b2e) * ce[:, None], None)
        out, _ = jax.lax.scan(body, jnp.zeros_like(x), (w1, b1, w2, b2, c.T))
        return out.reshape(b, s, h)
    x = _layernorm(x + _L0_attn_ref(x, L0_attn_W_qkv, L0_attn_W_proj, L0_attn_lambda_q1, L0_attn_lambda_q2, L0_attn_lambda_k1, L0_attn_lambda_k2), axis=-1)
    x = _layernorm(x + _L0_xattn_ref(x, ctx_768, L0_xattn_Wq, L0_xattn_bq, L0_xattn_Wk, L0_xattn_bk, L0_xattn_Wv, L0_xattn_bv), axis=-1)
    x = _layernorm(x + _L0_ffn_ref(x, L0_ffn_router_w, L0_ffn_w1, L0_ffn_w2), axis=-1)
    x = _layernorm(x + _L1_attn_ref(x, L1_attn_Wqkv, L1_attn_bqkv, L1_attn_Wout, L1_attn_bout), axis=-1)
    x = _layernorm(x + _L1_xattn_ref(x, ctx_768, L1_xattn_w_q, L1_xattn_w_kv, L1_xattn_w_out, L1_xattn_b_out), axis=-1)
    x = _layernorm(x + _L1_ffn_ref(x, L1_ffn_router_w, L1_ffn_router_b, L1_ffn_w1, L1_ffn_b1, L1_ffn_w2, L1_ffn_b2), axis=-1)
    return x

_drawn_inputs = setup_inputs


def setup_inputs(seed=0):
    import zlib

    import numpy as np

    out = dict(_drawn_inputs(seed))
    spreads = {'L1_ffn_router_b': (0.0, 0.1), 'L1_ffn_b1': (0.0, 0.8), 'L1_ffn_b2': (0.0, 0.1)}
    factors = {'L0_attn_lambda_q1': 3.281,
     'L0_attn_lambda_q2': 3.379,
     'L0_attn_lambda_k1': 3.397,
     'L0_xattn_bq': 7.143,
     'L0_xattn_bk': 8.0,
     'L1_xattn_b_out': 4.902,
     'L1_ffn_w1': 2.997,
     'L1_ffn_w2': 2.728}
    for name, (base, spread) in spreads.items():
        noise = np.random.default_rng([zlib.crc32(name.encode()), seed]).standard_normal(out[name].shape)
        drawn = base * np.exp(spread * noise) if base else spread * noise
        out[name] = jnp.asarray(drawn.astype(out[name].dtype))
    for name, factor in factors.items():
        out[name] = (out[name] * factor).astype(out[name].dtype)
    return out
```

```python
from contextlib import ExitStack

import numpy as np

import concourse.bass as bass
from concourse import mybir

F32 = mybir.dt.float32
BF16 = mybir.dt.bfloat16
ALU = mybir.AluOpType
ACT = mybir.ActivationFunctionType
AX = mybir.AxisListType

P = 128
B = 8
T = B * P
HALF = T // 2
L = 120
CD = 96
NH = 16
HD = 8
XD = 64
PAIRS = NH // 2
E0 = 8
F0 = 512 // P
E1 = 16
TOPK = 4
F1 = 256 // P
PARTS = 3
ROWS = PARTS * PARTS * HD
MROW = 96
EPS = 1e-5
BIG = -1e30
BANK_M0, BANK_M1, BANK_S, BANK_T, BANK_O = 0, 1, 2, 4, 6

C_ID, C_TRI, C_COSQ, C_SINQ, C_COSK, C_SINK, C_CS, C_CT = (P * n for n in range(8))
C_IOTA = 8 * P
C_R8 = C_IOTA + T
C_R16 = C_R8 + B * E0
C_EOFF = C_R16 + B * E1
C_SLOT = C_EOFF + B * E0
C_ALL = C_SLOT + E0


def constant_table():
    t = np.zeros((P, C_ALL), np.float32)
    n = np.arange(P)
    t[:, C_ID:C_ID + P] = np.eye(P)
    t[:, C_TRI:C_TRI + P] = n[:, None] <= n[None, :]
    inv = (1.0 / np.float32(10000.0) ** (np.arange(0, 2 * HD, 2, dtype=np.float32) / np.float32(2 * HD)))
    angle = (n.astype(np.float32)[None, :] * inv.astype(np.float32)[:, None]).astype(np.float32)
    cos, sin = np.tile(np.cos(angle), (NH, 1)), np.tile(np.sin(angle), (NH, 1))
    scale = HD ** -0.5
    t[:, C_COSQ:C_COSQ + P], t[:, C_SINQ:C_SINQ + P] = cos * scale, sin * scale
    t[:, C_COSK:C_COSK + P], t[:, C_SINK:C_SINK + P] = cos, sin
    t[:, C_CS:C_CS + P] = np.where(n[None, :] > n[:, None], BIG, 0.0)
    t[:, C_CT:C_CT + P] = np.where(n[:, None] > n[None, :], BIG, 0.0)
    t[:, C_IOTA:C_IOTA + T] = np.arange(T)[None, :]
    t[:, C_R8:C_R8 + B * E0] = (np.arange(B * E0) % 8 != 0)[None, :]
    t[:, C_R16:C_R16 + B * E1] = (np.arange(B * E1) % E1 != 0)[None, :]
    t[:, C_EOFF:C_EOFF + B * E0] = (np.arange(B * E0) // B * P)[None, :]
    t[:, C_SLOT:C_SLOT + E0] = np.arange(E0)[None, :] * P + n[:, None]
    return t


class Chain:

    def __init__(self, eng, sem):
        self.eng, self.sem, self.n = eng, sem, 0

    def __call__(self, ins):
        ins.then_inc(self.sem, 1)
        self.n = self.n + 1

    def wait(self):
        self.eng.wait_ge(self.sem, self.n)

    def enter(self, i, first, stride):
        self.entered, self.stride = self.n, stride
        self.n = (i - first) * stride + self.entered
        self.local = self.n

    def leave(self, times):
        self.n = self.entered + times * self.stride


def decoder_kernel(nc, d, out):
    with ExitStack() as ctx:
        def sb(name, shape, dt=F32):
            return ctx.enter_context(nc.sbuf_tensor(name, shape, dt))

        def sem(name):
            return ctx.enter_context(nc.semaphore(name))

        ps = ctx.enter_context(nc.psum_tensor("ps", [P, 8, 512], F32))
        con = sb("con", [P, C_ALL])
        identb, trib, onesb, causS, causT = (sb(n, [P, P], BF16) for n in ("identb", "trib", "onesb", "causS", "causT"))
        onesf = sb("onesf", [P, XD])
        xres = sb("xres", [P, B, P])
        racc = sb("racc", [P, B, P])
        xT = sb("xT", [P, T])
        ctxT = sb("ctxT", [CD, B * L])
        wqk0 = sb("wqk0", [P, 4, P])
        wv0 = sb("wv0", [P, 2 * P])
        wproj0 = sb("wproj0", [P, 2, P])
        lamin = sb("lamin", [P, 4, HD])
        lams = sb("lams", [P, 8])
        wqB, wkB, wvB = sb("wqB", [P, P]), sb("wkB", [CD, P]), sb("wvB", [CD, P])
        bqB, bkB, bvB = sb("bqB", [P, 1]), sb("bkB", [P, 1]), sb("bvB", [P, P])
        rw0 = sb("rw0", [P, E0])
        w1a = sb("w1a", [P, E0, F0 * P])
        w2a = sb("w2a", [P, E0, F0, P])
        before = w2a[:].rearrange("p e f n -> p (e f n)")
        kTB = before[:, 0:960].rearrange("p (a b) -> p a b", a=2)
        vB = before[:, 1024:1024 + B * 132].rearrange("p (b n) -> p b n", b=B)
        wqkD, wvD, woD = sb("wqkD", [P, 2, P]), sb("wvD", [P, P]), sb("woD", [P, P])
        bqkD, bvD, boD = sb("bqkD", [P, 2]), sb("bvD", [P, P]), sb("boD", [P, P])
        boE = sb("boE", [P, P])
        rw1, rb1, b2s = sb("rw1", [P, E1]), sb("rb1", [P, E1]), sb("b2s", [E1, P])
        stq = sb("stq", [P, 2, 2, T], BF16)
        stk = sb("stk", [P, 2, 2, T], BF16)
        probs = sb("probs", [P, 2, 16, P])
        outT = sb("outT", [P, 512])
        vall = sb("vall", [P, B, 2 * P])
        vs = sb("vs", [P, 2, 2, B, 32])
        oall = sb("oall", [P, B, 2 * P])
        oT = sb("oT", [P, B, 2, P])
        negm = sb("negm", [P, 2, 16])
        mhi, mmid, mlo = (sb(n, [16, P], BF16) for n in ("mhi", "mmid", "mlo"))
        mres = sb("mres", [16, P])
        mrow = sb("mrow", [PARTS, 2, 16 * P], BF16)
        rz = sb("rz", [P, 16])
        ot1, ot2 = sb("ot1", [P, B, 16]), sb("ot2", [P, B, 16])
        bst, mv = sb("bst", [P, B, 6]), sb("mv", [P, B, 2])
        rstd, mhalf = sb("rstd", [P, B]), sb("mhalf", [P, B])
        sm = sb("sm", [P, 12, 128])
        smb = sb("smb", [P, 2, B * E0], BF16)
        arena = sb("arena", [P, 14976])

        def area(at, *shape, dt=F32, rows=P):
            n = int(np.prod(shape)) * (2 if dt == BF16 else 4) // 4
            a = arena[0:rows, at:at + n]
            if dt == BF16:
                a = a.bitcast(BF16)
            names = "abcd"[:len(shape)]
            return a.rearrange(f"p ({' '.join(names)}) -> p {' '.join(names)}",
                               **dict(zip(names[1:], shape[1:]))) if len(shape) > 1 else a

        rope = area(0, 8, T)
        part = area(8192, 4, PARTS, T, dt=BF16)
        sel = area(0, B, T, dt=BF16)
        selT = area(4096, E0, T, dt=BF16)
        xpart = area(8192, PARTS, B, P, dt=BF16)
        epart = area(9728, PARTS, E0, P, dt=BF16)
        xin = area(11264, T)
        hid0 = area(12288, 2, 512)
        eout = area(13312, E0, P)
        slotrow = probs[:, 0, 0:8, :].rearrange("p a b -> p (a b)")
        qB = area(0, B, P)
        otall = area(0, PAIRS, T)
        qz = area(8192, 2, B, 2, P)
        kE = area(12288, 2, B * L)
        wE = area(14208, 2, 3, P)
        vE = vall[0:L, :, :].rearrange("p b (s n) -> p s b n", s=2)
        rzE = oall[:, 0:4, 0:P]
        hid1 = area(0, 2, F1, T)
        w1s = area(4096, 2, F1 * P)
        w2s = area(4608, 2, F1, P)
        b1s = area(5120, 2, F1)

        stackA = nc.dram_tensor("stackA", [2 * NH * PARTS * HD * 2 * T], BF16, kind="Internal")
        stackD = nc.dram_tensor("stackD", [2 * NH * PARTS * HD * T], BF16, kind="Internal")

        ident = con[:, C_ID:C_ID + P]

        def bank(n, k=1):
            return ps[:, n, :] if k == 1 else ps[:, n:n + k, :].rearrange("p a b -> p (a b)")

        def tiles(ap, n, w):
            return ap[:, 0:n * w].rearrange("p (a b) -> p a b", b=w)

        def over(ap, n):
            return ap.unsqueeze(1).to_broadcast([ap.shape[0], n, ap.shape[1]])

        def along(ap, n):
            return ap.unsqueeze(2).to_broadcast([ap.shape[0], ap.shape[1], n])

        ld_a, ld_b, ld_x, ld_f, ld_d, ld_g = (sem(f"ld_{n}") for n in "abxfdg")
        fixed = sem("fixed")
        tables = sem("tables")
        dchain, achain, pchain = sem("dchain"), sem("achain"), sem("pchain")

        class Heads:

            def __init__(self, n):
                self.qk = sem(n + "_qk")
                self.mul = sem(n + "_mul")
                self.full = sem(n + "_full")
                self.hi, self.mid, self.lo = sem(n + "_hi"), sem(n + "_mid"), sem(n + "_lo")
                self.rest = sem(n + "_rest")
                self.kept = sem(n + "_kept")
                self.vps, self.vall = sem(n + "_vps"), sem(n + "_vall")
                self.stack = [sem(n + "_stack0"), sem(n + "_stack1")]
                self.mrow = [sem(n + "_mrow0"), sem(n + "_mrow1")]
                self.s = sem(n + "_s")
                self.max = sem(n + "_max")
                self.mt = sem(n + "_mt")
                self.msplit = sem(n + "_msplit")
                self.st = sem(n + "_st")
                self.exp = sem(n + "_exp")
                self.vs = sem(n + "_vs")
                self.pv = sem(n + "_pv")
                self.ot = sem(n + "_ot")
                self.to = sem(n + "_to")
                self.norm = sem(n + "_norm")
                self.post = sem(n + "_post")
                self.postc = sem(n + "_postc")
                self.y = sem(n + "_y")

        A, D = Heads("a"), Heads("d")
        ln_var, ln_rstd, ln_out, ln_tp, ln_xT = (sem("ln_" + n) for n in ("var", "rstd", "out", "tp", "xT"))
        resb = sem("resb")
        bkv, bkvc = sem("b_kv"), sem("b_kvc")
        b_q, b_qc, b_s, b_max, b_mt, b_msplit, b_mrow, b_st, b_exp, b_pv, b_r = (
            sem("b_" + n) for n in ("q", "qc", "s", "max", "mt", "msplit", "mrow", "st", "exp", "pv", "r"))
        lam_sum, lam_exp, lam_done = sem("lam_sum"), sem("lam_exp"), sem("lam_done")
        f_log, f_sub, f_exp, f_one, f_cnt, f_slot, f_srow, f_srowc, f_sel, f_selT, f_hi, f_rest, f_mid, f_part = (
            sem("f_" + n) for n in ("log", "sub", "exp", "one", "cnt", "slot", "srow", "srowc", "sel", "selT", "hi",
                                    "rest", "mid", "part"))
        f_xin, f_xinc, f_up, f_gelu, f_dn, f_ehi, f_erest, f_emid, f_epart, f_y, f_r = (
            sem("f_" + n) for n in ("xin", "xinc", "up", "gelu", "dn", "ehi", "erest", "emid", "epart", "y", "r"))
        e_w = [sem("e_w0"), sem("e_w1")]
        e_mrow = [sem("e_mrow0"), sem("e_mrow1")]
        (e_q, e_k, e_v, e_qa, e_qd, e_kc, e_vc, e_s, e_max, e_mt, e_msplit, e_st, e_exp, e_pv, e_norm, e_zero,
         e_wo, e_y) = (
            sem("e_" + n) for n in ("q", "k", "v", "qa", "qd", "kc", "vc", "s", "max", "mt", "msplit", "st", "exp",
                                    "pv", "norm", "zero", "wo", "y"))
        woE = oT[:, 0:4, :, :].rearrange("p a b c -> p (a b) c")
        g_w = [sem("g_w0"), sem("g_w1")]
        g_log, g_sub, g_exp, g_c, g_ct, g_ctc, g_b2, g_up, g_gelu, g_dn, g_acc, g_out = (
            sem("g_" + n) for n in ("log", "sub", "exp", "c", "ct", "ctc", "b2", "up", "gelu", "dn", "acc", "out"))

        block = ctx.enter_context(nc.Block())

        @block.sync
        def _(sp):
            def load(dst, src, signal):
                sp.dma_start(dst, src).then_inc(signal, 16)

            load(con[:], d["con"], ld_a)
            load(xT[:], d["xT"], ld_a)
            load(wqk0[:], d["wqk0"], ld_a)
            load(wv0[:], d["wv0"], ld_b)
            load(ctxT[:], d["ctxT"], ld_x)
            for dst, n in ((wqB, "wqB"), (wkB, "wkB"), (wvB, "wvB"), (bqB, "bqB"), (bkB, "bkB")):
                load(dst[:], d[n], ld_x)
            load(bvB[:], d["bvB"].to_broadcast([P, P]), ld_x)
            load(xres[:], d["x"], ld_b)
            load(wproj0[:], d["wproj0"], ld_b)
            for n, name in enumerate(("lq1", "lq2", "lk1", "lk2")):
                load(lamin[:, n, :], d[name].to_broadcast([P, HD]), ld_b)
            load(rw0[:], d["rw0"], ld_f)
            load(w1a[:], d["w1a"], ld_f)
            for dst, n in ((wqkD, "wqkD"), (wvD, "wvD"), (woD, "woD"), (bqkD, "bqkD"), (rw1, "rw1"), (b2s, "b2s")):
                load(dst[:], d[n], ld_d)
            for dst, n, w in ((bvD, "bvD", P), (boD, "boD", P), (boE, "boE", P), (rb1, "rb1", E1)):
                load(dst[:], d[n].to_broadcast([P, w]), ld_d)

            def keep(a, n, dst):
                for p, made in enumerate((a.hi, a.mid, a.lo)):
                    sp.wait_ge(made, n + 1)
                    sp.dma_start(dst(p), part[:, n, p, :]).then_inc(a.kept, 16)

            def move_maxima(a, made, slot):
                sp.wait_ge(a.msplit, made)
                for p, m in enumerate((mhi, mmid, mlo)):
                    sp.dma_start(stq[MROW + p:MROW + p + 1, slot, :, :], m[:]).then_inc(a.mrow[slot], 16)

            def heads(a, count):
                move_maxima(a, 1, 0)
                move_maxima(a, 2, 1)
                with sp.Fori(1, count // 2) as i:
                    made = [sp.snap(i * 2 + (u + 1)) for u in range(2)]
                    for u in range(2):
                        move_maxima(a, made[u], u)

            for n, (t, c) in enumerate(((0, 0), (0, 1), (1, 0), (1, 1))):
                keep(A, n, lambda p: bass.AP(
                    stackA, t * NH * PARTS * HD * 2 * T + p * HD * 2 * T + c * T,
                    [[PARTS * HD * 2 * T, NH], [2 * T, HD], [1, T]]))
            heads(A, NH)
            sp.wait_ge(b_msplit, 1)
            for p, m in enumerate((mhi, mmid, mlo)):
                sp.dma_start(mrow[p:p + 1, 0, 0:T], m[0:B, :]).then_inc(b_mrow, 16)
            sp.wait_ge(b_pv, 3)
            load(w2a[:], d["w2a"], ld_f)
            for t in range(2):
                keep(D, t, lambda p: bass.AP(
                    stackD, (t * PAIRS * PARTS + p) * 2 * HD * T, [[PARTS * 2 * HD * T, PAIRS], [T, 2 * HD], [1, T]]))
            heads(D, PAIRS)

            def weights(pair, slot):
                for n, name in enumerate(("wqE", "wkE", "wvE")):
                    rows = P if n == 0 else CD
                    sp.dma_start(wE[0:rows, slot, n, :], d[name][0:rows, bass.ds(pair * P, P)]).then_inc(e_w[slot], 16)

            def maxima(made, slot):
                sp.wait_ge(e_msplit, made)
                for p, m in enumerate((mhi, mmid, mlo)):
                    sp.dma_start(mrow[p:p + 1, slot, :], m[:]).then_inc(e_mrow[slot], 16)

            sp.wait_ge(D.y, 2)
            sp.dma_start(woE, d["woE"]).then_inc(e_wo, 16)
            sp.wait_ge(e_zero, 2)
            weights(0, 0)
            weights(1, 1)
            maxima(1, 0)
            with sp.Fori(0, PAIRS // 2 - 1) as i:
                pair = [sp.snap(i * 2 + (u + 2)) for u in range(2)]
                projected = [sp.snap(i * 4 + 2 * (u + 1)) for u in range(2)]
                for u in range(2):
                    sp.wait_ge(e_v, projected[u])
                    weights(pair[u], u)
                    maxima(pair[u], 1 - u)
            maxima(PAIRS, 1)

            def expert(e, slot):
                sp.dma_start(w1s[:, slot, :], d["w1b"][bass.ds(e, 1), :, :]).then_inc(g_w[slot], 16)
                sp.dma_start(w2s[:, slot, :, :], d["w2b"][bass.ds(e, 1), :, :, :]).then_inc(g_w[slot], 16)
                sp.dma_start(b1s[:, slot, :], d["b1"][bass.ds(e, 1), :, :]).then_inc(g_w[slot], 16)

            sp.wait_ge(e_y, 2)
            expert(0, 0)
            expert(1, 1)
            with sp.Fori(0, E1 // 2 - 1) as i:
                nxt = [sp.snap(i * 2 + (u + 2)) for u in range(2)]
                used = [sp.snap(i * 4 + 2 * (u + 1)) for u in range(2)]
                for u in range(2):
                    sp.wait_ge(g_dn, used[u])
                    expert(nxt[u], u)
            for half in range(2):
                sp.wait_ge(ln_out, 2 * 5 + half + 1)
                sp.dma_start(out[:, 4 * half:4 * half + 4, :], xres[:, 4 * half:4 * half + 4, :]).then_inc(g_out, 16)
            sp.wait_ge(g_out, 32)

        @block.gpsimd
        def _(pool):
            for n, (tile, value) in enumerate((
                    (stq[64:MROW, :, :, :], 0.0), (stk[64:MROW, :, :, :], 0.0), (stk[MROW:MROW + PARTS, :, :, :], 1.0),
                    (onesb[:], 1.0), (onesf[:], 1.0), (mhalf[:], -0.5), (vB[:, :, P:P + 1], 1.0), (vs[:], 0.0),
                    (vs[:, :, :, :, 16:17], 1.0))):
                nc.gpsimd.memset(tile, value).then_inc(fixed, 1)
                pool.wait_ge(fixed, n + 1)
            pch = Chain(pool, pchain)

            for n in range(4):
                pool.wait_ge(A.mul, n + 1)
                op = ALU.subtract if n % 2 == 0 else ALU.add
                nc.gpsimd.tensor_tensor(rope[:, 2 * n, :], rope[:, 2 * n, :], rope[:, 2 * n + 1, :], op).then_inc(A.full, 1)

            def values(a, h, slot, width):
                if width == 16:
                    return nc.gpsimd.tensor_copy(vs[:, slot, 0, :, 0:16], vall[:, :, bass.ds(h * 16, 16)])
                return nc.gpsimd.tensor_copy(
                    vs[:, slot, :, :, 0:8].rearrange("p c b d -> p b c d"),
                    vall[:, :, bass.ds(h * 16, 16)].rearrange("p b (c d) -> p b c d", c=2))

            def heads(a, count, width):
                pool.wait_ge(a.vall, 4 if width == 16 else 2)
                values(a, 0, 0, width).then_inc(a.vs, 1)
                values(a, 1, 1, width).then_inc(a.vs, 1)
                with pool.Fori(1, count // 2) as i:
                    for u in range(2):
                        pool.wait_ge(a.pv, i * 2 + u - 1)
                        values(a, i * 2 + u, u, width).then_inc(a.vs, 1)

            def rsqrt(k, half):
                s = slice(4 * half, 4 * half + 4)
                pool.wait_ge(ln_var, 2 * k + half + 1)
                pch(nc.gpsimd.tensor_scalar(rstd[:, s], mv[:, s, 1], EPS, None, ALU.add))
                pch.wait()
                nc.gpsimd.tensor_tensor(rstd[:, s], rstd[:, s], mhalf[:, s], ALU.pow).then_inc(ln_rstd, 1)

            def add_bias(k, bias):
                pool.wait_ge(ln_xT, 2 * k)
                pool.wait_ge(ln_out, 2 * k)
                nc.gpsimd.tensor_tensor(xres[:], xres[:], over(bias[:], B), ALU.add).then_inc(resb, 1)

            heads(A, NH, 16)
            rsqrt(0, 0)
            rsqrt(0, 1)
            pool.wait_ge(ld_x, 16 * 7)
            add_bias(1, bvB)
            rsqrt(1, 0)
            rsqrt(1, 1)
            rsqrt(2, 0)
            rsqrt(2, 1)
            pool.wait_ge(ld_d, 16 * 10)
            add_bias(3, boD)
            nc.gpsimd.memset(vs[:, :, :, :, 8:9], 1.0).then_inc(fixed, 1)
            heads(D, PAIRS, 8)
            rsqrt(3, 0)
            rsqrt(3, 1)
            pool.wait_ge(D.lo, 2)
            pool.wait_ge(D.kept, 16 * 6)
            pool.wait_ge(ln_rstd, 8)
            nc.gpsimd.memset(qz[0:64, :, :, 1, :], 0.0).then_inc(e_zero, 1)
            pool.wait_ge(e_zero, 1)
            nc.gpsimd.memset(qz[64:128, :, :, 0, :], 0.0).then_inc(e_zero, 1)
            pool.wait_ge(e_zero, 2)
            add_bias(4, boE)
            rsqrt(4, 0)
            rsqrt(4, 1)
            rsqrt(5, 0)
            rsqrt(5, 1)

        @block.tensor
        def _(pe):
            mm = nc.tensor.matmul

            def head_scores(a, n, slot, causal, first=False):
                for g in range(4):
                    if not (first and g < 2):
                        pe.wait_ge(a.max, n * 4 + g - 1)
                    o = bank(BANK_S + g % 2)
                    if causal:
                        mm(tiles(o, 4, P), identb[:], over(causS[:], 4), start=True, stop=False)
                    for k in range(4):
                        tile = 4 * g + k
                        rows = slice(0, MROW)
                        last = mm(o[:, k * P:(k + 1) * P],
                                  stq[rows, slot, tile // B, tile % B * P:(tile % B + 1) * P],
                                  stk[rows, slot, tile // B, tile % B * P:(tile % B + 1) * P],
                                  start=not causal, stop=not causal or k == 3)
                    last.then_inc(a.s, 1)

            def head_scores_t(a, n, slot, count, causal, first=False):
                pe.wait_ge(a.mrow[slot], count * 48)
                for g in range(4):
                    if not (first and g < 2):
                        pe.wait_ge(a.exp, n * 4 + g - 1)
                    o = bank(BANK_T + g % 2)
                    if causal:
                        mm(tiles(o, 4, P), identb[:], over(causT[:], 4), start=True, stop=False)
                    for k in range(4):
                        tile = 4 * g + k
                        rows = slice(0, MROW + PARTS)
                        last = mm(o[:, k * P:(k + 1) * P],
                                  stk[rows, slot, tile // B, tile % B * P:(tile % B + 1) * P],
                                  stq[rows, slot, tile // B, tile % B * P:(tile % B + 1) * P],
                                  start=not causal, stop=not causal or k == 3)
                    last.then_inc(a.st, 1)

            def head_maxima(a, n, slot):
                pe.wait_ge(a.max, n * 4 + 4)
                pe.wait_ge(a.msplit, n)
                nc.tensor.transpose(bank(BANK_M0)[0:16, 0:P], negm[:, slot, :], ident).then_inc(a.mt, 1)

            def head_values(a, n, slot, pair):
                pe.wait_ge(a.vs, n + 1)
                pe.wait_ge(a.exp, n * 4 + 4)
                pe.wait_ge(a.ot, n)
                o = bank(BANK_O + slot)
                for tile in range(16):
                    c, b = tile // B, tile % B
                    col = (c * 2 + b // 4) * P
                    last = mm(o[32 * (b % 4):32 * (b % 4) + 32, col:col + P],
                              vs[:, slot, c if pair else 0, b, :], probs[:, slot, tile, :], start=True, stop=True)
                last.then_inc(a.pv, 1)

            def head_token(a, n):
                pe.wait_ge(a.ot, n + 1)
                pe.wait_ge(a.norm, n)
                o = bank(BANK_M1)
                for k in range(4):
                    last = nc.tensor.transpose(o[:, k * P:(k + 1) * P], outT[:, k * P:(k + 1) * P], ident)
                last.then_inc(a.to, 1)

            def heads(a, count, pair, causal):
                def step(n, slot, turn, first=False, last=False):
                    if not last:
                        other = turn + 1 if slot == 1 else turn
                        pe.wait_ge(a.stack[1 - slot], other * 64)
                        head_scores(a, n + 1, 1 - slot, causal)
                    if not first:
                        head_token(a, n - 1)
                    head_scores_t(a, n, slot, turn, causal, first)
                    if not last:
                        head_maxima(a, n + 1, 1 - slot)
                    head_values(a, n, slot, pair)

                pe.wait_ge(a.stack[0], 64)
                head_scores(a, 0, 0, causal, first=True)
                head_maxima(a, 0, 0)
                step(0, 0, 1, first=True)
                step(1, 1, 1)
                with pe.Fori(1, count // 2 - 1) as i:
                    for u in range(2):
                        step(i * 2 + u, u, i + 1)
                step(count - 2, 0, count // 2)
                step(count - 1, 1, count // 2, last=True)
                head_token(a, count - 1)

            def finish(a, chunks, w):
                pe.wait_ge(a.norm, NH if chunks == 2 else PAIRS)
                per = 4 // chunks
                banks = (BANK_S, BANK_S + 1, BANK_T, BANK_T + 1)
                for g in range(B // per):
                    for k in range(per):
                        for c in range(chunks):
                            o = bank(banks[g])[:, (k * chunks + c) * P:(k * chunks + c + 1) * P]
                            last = nc.tensor.transpose(o, oall[:, g * per + k, c * P:(c + 1) * P], ident)
                    last.then_inc(a.post, 1)
                for half in range(2):
                    pe.wait_ge(a.postc, (half + 1) * B // per // 2)
                    for k in range(4):
                        b = 4 * half + k
                        for c in range(chunks):
                            last = mm(bank(BANK_O + half)[:, k * P:(k + 1) * P], oT[:, b, c, :],
                                      w[:, c, :] if chunks == 2 else w[:],
                                      start=c == 0, stop=c == chunks - 1)
                    last.then_inc(a.y, 1)

            def to_feature(k):
                for half in range(2):
                    pe.wait_ge(ln_out, 2 * k + half + 1)
                    for j in range(4):
                        last = nc.tensor.transpose(bank(BANK_M0 + half)[:, j * P:(j + 1) * P],
                                                   xres[:, 4 * half + j, :], ident)
                    last.then_inc(ln_tp, 1)

            pe.wait_ge(ld_a, 48)
            for t in range(4):
                for half in range(2):
                    last = mm(bank(2 * t + half), wqk0[:, t, :], xT[:, half * HALF:(half + 1) * HALF],
                              start=True, stop=True)
                last.then_inc(A.qk, 1)
            pe.wait_ge(ld_b, 16 * 7)
            pe.wait_ge(A.mul, 2)
            for g in range(4):
                for k in range(2):
                    b = 2 * g + k
                    last = mm(bank(g)[:, k * 256:(k + 1) * 256], xT[:, b * P:(b + 1) * P], wv0[:], start=True, stop=True)
                last.then_inc(A.vps, 1)
            pe.wait_ge(ld_x, 16 * 7)
            pe.wait_ge(A.mul, 4)
            for half in range(2):
                mm(bank(4 + half)[:, 0:480], wkB[:], ctxT[:, half * 480:(half + 1) * 480],
                   start=True, stop=True).then_inc(bkv, 1)
            for half in range(2):
                for k in range(4):
                    b = 4 * half + k
                    last = mm(bank(6 + half)[0:L, k * P:(k + 1) * P], ctxT[:, b * L:(b + 1) * L], wvB[:],
                              start=True, stop=True)
                last.then_inc(bkv, 1)
            pe.wait_ge(A.vall, 4)
            pe.wait_ge(bkvc, 4)
            pe.wait_ge(fixed, 9)
            pe.wait_ge(tables, 4)
            heads(A, NH, pair=False, causal=False)
            finish(A, 2, wproj0)
            to_feature(0)

            for half in range(2):
                pe.wait_ge(ln_xT, half + 1)
                mm(bank(BANK_S + half), wqB[:], xT[:, half * HALF:(half + 1) * HALF], start=True, stop=True).then_inc(b_q, 1)
            kb = before[:, 0:960]
            for half in range(2):
                pe.wait_ge(b_qc, half + 1)
                for k in range(4):
                    b = 4 * half + k
                    last = mm(bank(BANK_T + half)[:, k * L:(k + 1) * L], qB[:, b, :], kb[:, b * L:(b + 1) * L],
                              start=True, stop=True)
                last.then_inc(b_s, 1)
            pe.wait_ge(b_max, 2)
            nc.tensor.transpose(bank(BANK_O)[0:B, 0:P], negm[:, 0, 0:B], ident).then_inc(b_mt, 1)
            pe.wait_ge(b_mrow, 48)
            for half in range(2):
                o = bank(BANK_S + half)
                mm(o[0:L, :], onesb[0:PARTS, 0:L], mrow[:, 0, half * 512:(half + 1) * 512], start=True, stop=False)
                for k in range(4):
                    b = 4 * half + k
                    last = mm(o[0:L, k * P:(k + 1) * P], kb[:, b * L:(b + 1) * L], qB[:, b, :], start=False, stop=k == 3)
                last.then_inc(b_st, 1)
            for g, (lo, hi) in enumerate(((0, 3), (3, 6), (6, 8))):
                o = bank((BANK_T, BANK_T + 1, BANK_O + 1)[g])
                pe.wait_ge(b_exp, 1 if hi <= 4 else 2)
                for b in range(lo, hi):
                    last = mm(o[:, (b - lo) * 129:(b - lo + 1) * 129], probs[0:L, 0, b, :], vB[0:L, b, 0:129],
                              start=True, stop=True)
                last.then_inc(b_pv, 1)
            to_feature(1)

            for b in range(B):
                pe.wait_ge(ln_xT, 2 + b // 4 + 1)
                last = mm(bank(BANK_S)[:, b * E0:(b + 1) * E0], xT[:, b * P:(b + 1) * P], rw0[:], start=True, stop=True)
            last.then_inc(f_log, 1)
            pe.wait_ge(f_one, 2)
            mm(bank(BANK_S + 1)[:, 0:B * E0], trib[:], smb[:, 0, :], start=True, stop=False)
            mm(bank(BANK_S + 1)[:, 0:B * E0], onesb[:], smb[:, 1, :], start=False, stop=True).then_inc(f_cnt, 1)
            pe.wait_ge(f_slot, 1)
            for b in range(B):
                last = mm(bank(BANK_T + b // 4)[:, b % 4 * P:(b % 4 + 1) * P],
                          sm[:, 9, b:b + 1].to_broadcast([P, P]), ident, start=True, stop=True)
                if b % 4 == 3:
                    last.then_inc(f_srow, 1)
            pe.wait_ge(f_part, 1)
            pe.wait_ge(f_mid, 1)
            pe.wait_ge(f_hi, 1)
            for b in range(B):
                pe.wait_ge(f_sel, b + 1)
                for half in range(2):
                    for p in range(PARTS):
                        last = mm(bank(BANK_O + half), xpart[:, p, b, :], sel[:, b, half * HALF:(half + 1) * HALF],
                                  start=b == 0 and p == 0, stop=b == B - 1 and p == PARTS - 1)
                if b == B - 1:
                    last.then_inc(f_xin, 1)
            pe.wait_ge(f_xinc, 2)
            pe.wait_ge(ld_f, 16 * 3)
            for e in range(E0 + 1):
                if e < E0:
                    if e >= 2:
                        pe.wait_ge(f_gelu, e - 1)
                    for f in range(F0):
                        last = mm(bank(BANK_S + e % 2)[:, f * P:(f + 1) * P], w1a[:, e, f * P:(f + 1) * P],
                                  xin[:, e * P:(e + 1) * P], start=True, stop=True)
                    last.then_inc(f_up, 1)
                if e > 0:
                    x = e - 1
                    pe.wait_ge(f_gelu, x + 1)
                    for f in range(F0):
                        last = mm(bank(BANK_M0 + x // 4)[:, x % 4 * P:(x % 4 + 1) * P], hid0[:, x % 2, f * P:(f + 1) * P],
                                  w2a[:, x, f, :], start=f == 0, stop=f == F0 - 1)
                    last.then_inc(f_dn, 1)
            pe.wait_ge(f_epart, 2)
            pe.wait_ge(f_selT, E0)
            for b in range(B):
                o = bank(BANK_O + b // 4)[:, b % 4 * P:(b % 4 + 1) * P]
                for e in range(E0):
                    for p in range(PARTS):
                        last = mm(o, selT[:, e, b * P:(b + 1) * P], epart[:, p, e, :],
                                  start=e == 0 and p == 0, stop=e == E0 - 1 and p == PARTS - 1)
                if b % 4 == 3:
                    last.then_inc(f_y, 1)
            pe.wait_ge(f_ehi, 2)
            to_feature(2)

            pe.wait_ge(f_r, 2)
            for t in range(2):
                for half in range(2):
                    pe.wait_ge(ln_xT, 4 + half + 1)
                    last = mm(bank(2 + 2 * t + half), wqkD[:, t, :], xT[:, half * HALF:(half + 1) * HALF],
                              start=True, stop=True)
                last.then_inc(D.qk, 1)
            for half in range(2):
                for k in range(4):
                    b = 4 * half + k
                    last = mm(bank(6 + half)[:, k * P:(k + 1) * P], xT[:, b * P:(b + 1) * P], wvD[:], start=True, stop=True)
                last.then_inc(D.vps, 1)
            pe.wait_ge(D.vall, 2)
            pe.wait_ge(D.mul, 2)
            heads(D, PAIRS, pair=True, causal=True)
            finish(D, 1, woD)
            to_feature(3)

            def project(n, slot, turn):
                pe.wait_ge(e_w[slot], turn * 48)
                pe.wait_ge(e_msplit, n)
                for half in range(2):
                    pe.wait_ge(e_vc, n * 2)
                    mm(bank(BANK_M0 + half), wE[:, slot, 0, :], xT[:, half * HALF:(half + 1) * HALF],
                       start=True, stop=True).then_inc(e_q, 1)
                for half in range(2):
                    pe.wait_ge(e_qa, n * 2 + half + 1)
                    pe.wait_ge(e_qd, n * 2 + half + 1)
                    mm(bank(BANK_M0 + half)[:, 0:480], wE[0:CD, slot, 1, :], ctxT[:, half * 480:(half + 1) * 480],
                       start=True, stop=True).then_inc(e_k, 1)
                for half in range(2):
                    pe.wait_ge(e_kc, n * 2 + half + 1)
                    for k in range(4):
                        b = 4 * half + k
                        last = mm(bank(BANK_M0 + half)[0:L, k * P:(k + 1) * P], ctxT[:, b * L:(b + 1) * L],
                                  wE[0:CD, slot, 2, :], start=True, stop=True)
                    last.then_inc(e_v, 1)

            def pair_scores(n, slot, first=False):
                for g in range(4):
                    if not (first and g < 2):
                        pe.wait_ge(e_max, n * 4 + g - 1)
                    if not first and g < 2:
                        pe.wait_ge(e_norm, n * 2 - 2)
                    for k in range(4):
                        b, j = 2 * g + k // 2, k % 2
                        last = mm(bank(BANK_S + g % 2)[:, k * L:(k + 1) * L], qz[:, slot, b, j, :],
                                  kE[:, slot, b * L:(b + 1) * L], start=True, stop=True)
                    last.then_inc(e_s, 1)

            def pair_scores_t(n, slot, turn, first=False):
                pe.wait_ge(e_mrow[slot], turn * 48)
                for g in range(4):
                    if not (first and g < 2):
                        pe.wait_ge(e_exp, n * 4 + g - 1)
                    o = bank(BANK_T + g % 2)
                    mm(o[0:L, :], onesb[0:PARTS, 0:L], mrow[:, slot, g * 512:(g + 1) * 512], start=True, stop=False)
                    for k in range(2):
                        b = 2 * g + k
                        last = mm(o[0:L, k * 256:(k + 1) * 256], kE[:, slot, b * L:(b + 1) * L],
                                  qz[:, slot, b, :, :].rearrange("p a b -> p (a b)"), start=False, stop=k == 1)
                    last.then_inc(e_st, 1)

            def pair_maxima(n, slot):
                pe.wait_ge(e_max, n * 4 + 4)
                pe.wait_ge(e_vc, n * 2 + 2)
                nc.tensor.transpose(bank(BANK_M0)[0:16, 0:P], negm[:, slot, :], ident).then_inc(e_mt, 1)

            def pair_values(n, slot):
                for half in range(2):
                    o, z = (bank(BANK_O), bank(BANK_O + 1)) if half == 0 else (bank(BANK_S), bank(BANK_S + 1))
                    pe.wait_ge(e_exp, n * 4 + 2 * half + 2)
                    if half == 0:
                        pe.wait_ge(e_norm, n * 2)
                    for b in range(4 * half, 4 * half + 4):
                        for j in range(2):
                            rows, cols = slice(64 * j, 64 * j + 64), slice(b % 4 * P, (b % 4 + 1) * P)
                            mm(o[rows, cols], vE[:, slot, b, 64 * j:64 * j + 64], probs[0:L, slot, 2 * b + j, :],
                               start=True, stop=True)
                            last = mm(z[rows, cols], onesf[0:L, :], probs[0:L, slot, 2 * b + j, :], start=True, stop=True)
                    last.then_inc(e_pv, 1)

            def pair_step(n, slot, turn, first=False, last=False):
                if not last:
                    other = turn + 1 if slot == 1 else turn
                    project(n + 1, 1 - slot, other)
                    pe.wait_ge(e_vc, (n + 2) * 2)
                    pair_scores(n + 1, 1 - slot)
                pair_scores_t(n, slot, turn, first)
                if not last:
                    pair_maxima(n + 1, 1 - slot)
                pair_values(n, slot)

            pe.wait_ge(ln_xT, 8)
            project(0, 0, 1)
            pe.wait_ge(e_vc, 2)
            pair_scores(0, 0, first=True)
            pair_maxima(0, 0)
            pair_step(0, 0, 1, first=True)
            pair_step(1, 1, 1)
            with pe.Fori(1, PAIRS // 2 - 1) as i:
                for u in range(2):
                    pair_step(i * 2 + u, u, i + 1)
            pair_step(PAIRS - 2, 0, PAIRS // 2)
            pair_step(PAIRS - 1, 1, PAIRS // 2, last=True)
            pe.wait_ge(e_norm, 2 * PAIRS)
            pe.wait_ge(e_wo, 16)
            for half in range(2):
                for k in range(4):
                    b = 4 * half + k
                    for p in range(PAIRS):
                        last = mm(bank(BANK_O + half)[:, k * P:(k + 1) * P], otall[:, p, b * P:(b + 1) * P], woE[:, p, :],
                                  start=p == 0, stop=p == PAIRS - 1)
                last.then_inc(e_y, 1)
            to_feature(4)

            for b in range(B):
                pe.wait_ge(ln_xT, 8 + b // 4 + 1)
                last = mm(bank(BANK_S)[:, b * E1:(b + 1) * E1], xT[:, b * P:(b + 1) * P], rw1[:], start=True, stop=True)
            last.then_inc(g_log, 1)

            def up(e, slot, turn, first=False):
                pe.wait_ge(g_w[slot], turn * 48)
                for f in range(F1):
                    for half in range(2):
                        u = 2 * f + half
                        if not first:
                            pe.wait_ge(g_gelu, e * 4 + u - 3)
                        mm(bank(BANK_S + u), w1s[:, slot, f * P:(f + 1) * P], xT[:, half * HALF:(half + 1) * HALF],
                           start=True, stop=True).then_inc(g_up, 1)

            def down(e, slot, first=False):
                banks = (BANK_M0, BANK_O)[slot]
                pe.wait_ge(g_gelu, e * 4 + 4)
                for half in range(2):
                    if not first:
                        pe.wait_ge(g_acc, e * 2 + half - 1)
                    for k in range(4):
                        b = 4 * half + k
                        for f in range(F1):
                            last = mm(bank(banks + half)[:, k * P:(k + 1) * P], hid1[:, slot, f, b * P:(b + 1) * P],
                                      w2s[:, slot, f, :], start=f == 0, stop=f == F1 - 1)
                    last.then_inc(g_dn, 1)

            pe.wait_ge(g_c, 1)
            for half in range(2):
                for k in range(4):
                    b = 4 * half + k
                    last = nc.tensor.transpose(bank(BANK_O + half)[0:E1, k * P:(k + 1) * P], sm[:, 11, b * E1:(b + 1) * E1],
                                               ident)
                last.then_inc(g_ct, 1)
            up(0, 0, 1, first=True)
            pe.wait_ge(g_ctc, 2)
            for half in range(2):
                for k in range(4):
                    b = 4 * half + k
                    last = mm(bank(BANK_O + half)[:, k * P:(k + 1) * P], oT[0:E1, b, 0, :], b2s[:], start=True, stop=True)
                last.then_inc(g_b2, 1)
            up(1, 1, 1)
            down(0, 0, first=True)
            up(2, 0, 2)
            pe.wait_ge(g_acc, 2)
            down(1, 1, first=True)
            with pe.Fori(1, E1 // 2 - 1) as i:
                for u in range(2):
                    up(i * 2 + u + 1, 1 - u, i + 1 + u)
                    down(i * 2 + u, u)
            up(E1 - 1, 1, E1 // 2)
            down(E1 - 2, 0)
            down(E1 - 1, 1)

        @block.scalar
        def _(act):
            ach = Chain(act, achain)

            def fn(o, i, f, **kw):
                return nc.scalar.activation(o, i, f, **kw)

            def parts_hi_mid(a, n, src):
                act.wait_ge(a.full, n + 1)
                fn(part[:, n, 0, :], src, ACT.Copy).then_inc(a.hi, 1)

            def part_mid(a, n, src):
                act.wait_ge(a.rest, n + 1)
                fn(part[:, n, 1, :], src, ACT.Copy).then_inc(a.mid, 1)

            def load_stacks(a, h, slot, base, rows):
                head = PARTS * HD * 2 * T
                keys = rows * head
                act.dma_start(stk[0:ROWS, slot, :, :], bass.AP(
                    base, h * head + keys, [[0, PARTS], [2 * T, PARTS * HD], [1, 2 * T]])).then_inc(a.stack[slot], 16)
                for p in range(PARTS):
                    act.dma_start(stq[p * PARTS * HD:(p + 1) * PARTS * HD, slot, :, :], bass.AP(
                        base, h * head + p * HD * 2 * T, [[0, PARTS], [2 * T, HD], [1, 2 * T]])
                    ).then_inc(a.stack[slot], 16)

            def heads(a, count, base):
                def step(n, slot, first=False, load=True):
                    for g in range(4):
                        act.wait_ge(a.st, n * 4 + g + 1)
                        if not first and g == 0:
                            act.wait_ge(a.pv, n - 1)
                        fn(probs[:, slot, 4 * g:4 * g + 4, :], tiles(bank(BANK_T + g % 2), 4, P), ACT.Exp).then_inc(a.exp, 1)
                    if load:
                        load_stacks(a, n + 2, slot, base, count)
                    act.wait_ge(a.pv, n + 1)
                    if not first or slot == 1:
                        act.wait_ge(a.to, n)
                    fn(outT[:], bank(BANK_O + slot), ACT.Copy).then_inc(a.ot, 1)

                load_stacks(a, 0, 0, base, count)
                load_stacks(a, 1, 1, base, count)
                step(0, 0, first=True)
                step(1, 1, first=True)
                with act.Fori(1, count // 2 - 1) as i:
                    for u in range(2):
                        step(i * 2 + u, u)
                step(count - 2, 0, load=False)
                step(count - 1, 1, load=False)

            def finish(a, chunks):
                per = 4 // chunks
                banks = (BANK_S, BANK_S + 1, BANK_T, BANK_T + 1)
                for g in range(B // per):
                    act.wait_ge(a.post, g + 1)
                    o = oT[:, g * per:(g + 1) * per, 0:chunks, :]
                    fn(o, bank(banks[g]).rearrange("p (a b c) -> p a b c", b=chunks, c=P), ACT.Copy).then_inc(a.postc, 1)

            def feature_copies(k):
                for half in range(2):
                    act.wait_ge(ln_tp, 2 * k + half + 1)
                    fn(xT[:, half * HALF:(half + 1) * HALF], bank(BANK_M0 + half), ACT.Copy).then_inc(ln_xT, 1)

            act.wait_ge(ld_a, 48)
            for dst, c in ((identb, C_ID), (trib, C_TRI), (causS, C_CS), (causT, C_CT)):
                fn(dst[:], con[:, c:c + P], ACT.Copy).then_inc(tables, 1)
            act.wait_ge(lam_sum, 1)
            fn(lams[:, 2:4], lams[:, 0:2], ACT.Exp).then_inc(lam_exp, 1)
            for g in range(2):
                act.wait_ge(A.vps, g + 1)
                fn(vall[:, 2 * g:2 * g + 2, :], bank(g).rearrange("p (a b) -> p a b", a=2), ACT.Copy).then_inc(A.vall, 1)
            for n in range(2):
                parts_hi_mid(A, n, rope[:, 2 * n, :])
            for g in range(2, 4):
                act.wait_ge(A.vps, g + 1)
                fn(vall[:, 2 * g:2 * g + 2, :], bank(g).rearrange("p (a b) -> p a b", a=2), ACT.Copy).then_inc(A.vall, 1)
            for n in range(2):
                part_mid(A, n, rope[:, 2 * n + 1, :])
            for half in range(2):
                act.wait_ge(bkv, half + 1)
                fn(kTB[:, half, :], bank(4 + half)[:, 0:480], ACT.Identity, bias=bkB[:, 0:1]).then_inc(bkvc, 1)
            act.wait_ge(fixed, 7)
            for half in range(2):
                act.wait_ge(bkv, 2 + half + 1)
                fn(vB[0:L, 4 * half:4 * half + 4, 0:P], tiles(bank(6 + half)[0:L, :], 4, P), ACT.Copy).then_inc(bkvc, 1)
            for n in range(2, 4):
                parts_hi_mid(A, n, rope[:, 2 * n, :])
            for n in range(2, 4):
                part_mid(A, n, rope[:, 2 * n + 1, :])
            act.wait_ge(A.kept, 16 * 12)
            act.wait_ge(fixed, 9)
            heads(A, NH, stackA)
            finish(A, 2)
            feature_copies(0)

            for half in range(2):
                act.wait_ge(b_st, half + 1)
                fn(probs[0:L, 0, 4 * half:4 * half + 4, :], tiles(bank(BANK_S + half)[0:L, :], 4, P), ACT.Exp).then_inc(b_exp, 1)
            feature_copies(1)

            act.wait_ge(f_sub, 1)
            fn(sm[:, 1, 0:64], sm[:, 0, 0:64], ACT.Exp).then_inc(f_exp, 1)
            fn(xpart[:, 0, :, :], xres[:], ACT.Copy).then_inc(f_hi, 1)
            for half in range(2):
                act.wait_ge(f_srow, half + 1)
                fn(slotrow[:, half * HALF:(half + 1) * HALF], bank(BANK_T + half), ACT.Copy).then_inc(f_srowc, 1)
            act.wait_ge(f_rest, 1)
            fn(xpart[:, 1, :, :], racc[:], ACT.Copy).then_inc(f_mid, 1)
            act.wait_ge(f_xin, 1)
            for half in range(2):
                fn(xin[:, half * HALF:(half + 1) * HALF], bank(BANK_O + half), ACT.Copy).then_inc(f_xinc, 1)
            for e in range(E0):
                act.wait_ge(f_up, e + 1)
                if e >= 2:
                    act.wait_ge(f_dn, e - 1)
                fn(hid0[:, e % 2, :], bank(BANK_S + e % 2), ACT.Gelu_apprx_tanh).then_inc(f_gelu, 1)
            for half in range(2):
                act.wait_ge(f_dn, 4 * half + 4)
                fn(epart[:, 0, 4 * half:4 * half + 4, :], tiles(bank(BANK_M0 + half), 4, P), ACT.Copy).then_inc(f_ehi, 1)
            for half in range(2):
                act.wait_ge(f_erest, half + 1)
                fn(epart[:, 1, 4 * half:4 * half + 4, :], eout[:, 4 * half:4 * half + 4, :], ACT.Copy).then_inc(f_emid, 1)
            feature_copies(2)

            for n in range(2):
                parts_hi_mid(D, n, rope[:, 2 * n, :])
            for n in range(2):
                part_mid(D, n, rope[:, 2 * n + 1, :])
            act.wait_ge(D.kept, 16 * 6)
            heads(D, PAIRS, stackD)
            finish(D, 1)
            feature_copies(3)

            def copies(n, slot):
                for half in range(2):
                    act.wait_ge(e_q, n * 2 + half + 1)
                    fn(qz[0:64, slot, 4 * half:4 * half + 4, 0, :], tiles(bank(BANK_M0 + half)[0:64, :], 4, P),
                       ACT.Copy, scale=XD ** -0.5).then_inc(e_qa, 1)
                for half in range(2):
                    act.wait_ge(e_k, n * 2 + half + 1)
                    fn(kE[:, slot, half * 480:(half + 1) * 480], bank(BANK_M0 + half)[:, 0:480], ACT.Copy).then_inc(e_kc, 1)
                for half in range(2):
                    act.wait_ge(e_v, n * 2 + half + 1)
                    fn(vE[:, slot, 4 * half:4 * half + 4, :], tiles(bank(BANK_M0 + half)[0:L, :], 4, P),
                       ACT.Copy).then_inc(e_vc, 1)

            def pair_exps(n, slot, first=False):
                for g in range(4):
                    act.wait_ge(e_st, n * 4 + g + 1)
                    if not first and g == 0:
                        act.wait_ge(e_pv, n * 2 - 2)
                    fn(probs[0:L, slot, 4 * g:4 * g + 4, :], tiles(bank(BANK_T + g % 2)[0:L, :], 4, P),
                       ACT.Exp).then_inc(e_exp, 1)

            act.wait_ge(e_zero, 2)
            copies(0, 0)
            copies(1, 1)
            pair_exps(0, 0, first=True)
            act.wait_ge(e_pv, 2)
            copies(2, 0)
            pair_exps(1, 1, first=True)
            with act.Fori(1, PAIRS // 2 - 1) as i:
                for u in range(2):
                    act.wait_ge(e_pv, (i * 2 + u) * 2)
                    copies(i * 2 + u + 1, 1 - u)
                    pair_exps(i * 2 + u, u)
            act.wait_ge(e_pv, (PAIRS - 2) * 2)
            copies(PAIRS - 1, 1)
            pair_exps(PAIRS - 2, 0)
            pair_exps(PAIRS - 1, 1)
            feature_copies(4)

            act.wait_ge(g_sub, 1)
            fn(sm[:, 1, :], sm[:, 0, :], ACT.Exp).then_inc(g_exp, 1)
            for half in range(2):
                act.wait_ge(g_ct, half + 1)
                fn(oT[0:E1, 4 * half:4 * half + 4, 0, :], tiles(bank(BANK_O + half)[0:E1, :], 4, P), ACT.Copy).then_inc(g_ctc, 1)

            def gelus(e, slot, first=False):
                for f in range(F1):
                    for half in range(2):
                        u = 2 * f + half
                        act.wait_ge(g_up, e * 4 + u + 1)
                        if u == 0 and not first:
                            act.wait_ge(g_dn, e * 2 - 2)
                        fn(hid1[:, slot, f, half * HALF:(half + 1) * HALF], bank(BANK_S + u), ACT.Gelu,
                           bias=b1s[:, slot, f:f + 1]).then_inc(g_gelu, 1)

            for e in range(2):
                act.wait_ge(g_w[e], 48)
                gelus(e, e, first=True)
            with act.Fori(1, E1 // 2) as i:
                for u in range(2):
                    act.wait_ge(g_w[u], (i + 1) * 48)
                    gelus(i * 2 + u, u)

        @block.vector
        def _(dve):
            dch = Chain(dve, dchain)
            tt, ts, stt = nc.vector.tensor_tensor, nc.vector.tensor_scalar, nc.vector.scalar_tensor_tensor

            def link(ins):
                dch(ins)
                dch.wait()

            def split_maxima(rows, src):
                link(nc.vector.tensor_copy(mhi[0:rows, :], src))
                link(tt(mres[0:rows, :], src, mhi[0:rows, :], ALU.subtract))
                link(nc.vector.tensor_copy(mmid[0:rows, :], mres[0:rows, :]))
                return tt(mlo[0:rows, :], mres[0:rows, :], mmid[0:rows, :], ALU.subtract)

            SPLIT = 3

            def heads(a, count, finish_head, links):
                def maxima(n, slot):
                    for g in range(4):
                        dve.wait_ge(a.s, n * 4 + g + 1)
                        nc.vector.tensor_reduce(negm[:, slot, 4 * g:4 * g + 4], tiles(bank(BANK_S + g % 2), 4, P),
                                                AX.X, ALU.max, negate=True).then_inc(a.max, 1)

                def split(n, slot, moved):
                    dve.wait_ge(a.mt, n + 1)
                    if moved is not None:
                        dve.wait_ge(a.mrow[1 - slot], moved * 48)
                    split_maxima(16, bank(BANK_M0)[0:16, 0:P]).then_inc(a.msplit, 1)

                def step(n, slot, turn, first=False, last=False):
                    if not last:
                        maxima(n + 1, 1 - slot)
                    if not first:
                        finish_head(n - 1)
                    if not last:
                        split(n + 1, 1 - slot, turn)

                maxima(0, 0)
                split(0, 0, None)
                step(0, 0, 1, first=True)
                step(1, 1, 1)
                with dve.Fori(1, count // 2 - 1) as i:
                    dch.enter(i, 1, 2 * (SPLIT + links))
                    for u in range(2):
                        step(i * 2 + u, u, i + 1)
                    dch.leave(count // 2 - 2)
                step(count - 2, 0, count // 2)
                step(count - 1, 1, count // 2, last=True)
                finish_head(count - 1)

            def finish_a(n):
                o = bank(BANK_M1).rearrange("p (c b w) -> p c b w", c=2, w=32)
                dve.wait_ge(A.to, n + 1)
                link(nc.vector.reciprocal(rz[:].rearrange("p (c b) -> p c b", c=2), o[:, :, :, 16]))
                link(ts(rz[:, B:2 * B], rz[:, B:2 * B], lams[:, 5:6], None, ALU.mult))
                dch(tt(ot1[:], o[:, 0, :, 0:16], along(rz[:, 0:B], 16), ALU.mult))
                link(tt(ot2[:], o[:, 1, :, 0:16], along(rz[:, B:2 * B], 16), ALU.mult))
                tt(oall[:, :, bass.ds(n * 16, 16)], ot1[:], ot2[:], ALU.add).then_inc(A.norm, 1)

            def finish_d(n):
                o = bank(BANK_M1).rearrange("p (c b w) -> p c b w", c=2, w=32)
                dve.wait_ge(D.to, n + 1)
                link(nc.vector.reciprocal(rz[:].rearrange("p (c b) -> p c b", c=2), o[:, :, :, 8]))
                dch(tt(oall[:, :, bass.ds(n * 16, 8)], o[:, 0, :, 0:8], along(rz[:, 0:B], 8), ALU.mult))
                tt(oall[:, :, bass.ds(n * 16 + 8, 8)], o[:, 1, :, 0:8], along(rz[:, B:2 * B], 8), ALU.mult).then_inc(D.norm, 1)

            def layernorm(k, half):
                s = range(4 * half, 4 * half + 4)
                for b in s:
                    dch(nc.vector.bn_stats(bst[:, b, :], racc[:, b, :]))
                dch.wait()
                for b in s:
                    last = nc.vector.bn_aggr(mv[:, b, :], bst[:, b, :])
                    if b < s[-1]:
                        dch(last)
                last.then_inc(ln_var, 1)
                dve.wait_ge(ln_rstd, 2 * k + half + 1)
                for b in s:
                    last = ts(xres[:, b, :], racc[:, b, :], mv[:, b, 0:1], rstd[:, b:b + 1], ALU.subtract, ALU.mult)
                    if b < s[-1]:
                        dch(last)
                last.then_inc(ln_out, 1)

            def half_of(ap, half):
                return ap[:, 4 * half:4 * half + 4, :]

            dve.wait_ge(ld_b, 16 * 7)
            link(tt(lamin[:, 0:2, :], lamin[:, 0:2, :], lamin[:, 2:4, :], ALU.mult))
            nc.vector.tensor_reduce(lams[:, 0:2], lamin[:, 0:2, :], AX.X, ALU.add).then_inc(lam_sum, 1)
            dve.wait_ge(ld_a, 48)

            def rotary(n, t0, cos, sin):
                mine, other = (t0, t0 + 2) if n % 2 == 0 else (t0 + 2, t0)
                for k, (at, table) in enumerate(((mine, cos), (other, sin))):
                    last = tt(rope[:, 2 * n + k, :].rearrange("p (a b) -> p a b", b=P),
                              bank(at, 2).rearrange("p (a b) -> p a b", b=P), over(con[:, table:table + P], B), ALU.mult)
                    if k == 0:
                        dch(last)
                last.then_inc(A.mul, 1)

            def rest_part(a, n):
                dve.wait_ge(a.hi, n + 1)
                tt(rope[:, 2 * n + 1, :], rope[:, 2 * n, :], part[:, n, 0, :], ALU.subtract).then_inc(a.rest, 1)

            def low_part(a, n):
                dve.wait_ge(a.mid, n + 1)
                tt(part[:, n, 2, :], rope[:, 2 * n + 1, :], part[:, n, 1, :], ALU.subtract).then_inc(a.lo, 1)

            for n in range(4):
                dve.wait_ge(A.qk, 2 if n < 2 else 4)
                rotary(n, 0 if n < 2 else 4, *((C_COSQ, C_SINQ) if n < 2 else (C_COSK, C_SINK)))
            dve.wait_ge(lam_exp, 1)
            link(tt(lams[:, 4:5], lams[:, 3:4], lams[:, 2:3], ALU.subtract))
            link(ts(lams[:, 5:6], lams[:, 4:5], -(0.8 - 0.6), None, ALU.add))
            for pair in ((0, 1), (2, 3)):
                for n in pair:
                    rest_part(A, n)
                for n in pair:
                    low_part(A, n)
            heads(A, NH, finish_a, 4)
            for half in range(2):
                dve.wait_ge(A.y, half + 1)
                link(tt(half_of(racc, half), tiles(bank(BANK_O + half), 4, P), half_of(xres, half), ALU.add))
                layernorm(0, half)

            for half in range(2):
                dve.wait_ge(b_q, half + 1)
                ts(qB[:, 4 * half:4 * half + 4, :], tiles(bank(BANK_S + half), 4, P), bqB[:, 0:1], float(P) ** -0.5,
                   ALU.add, ALU.mult).then_inc(b_qc, 1)
            for half in range(2):
                dve.wait_ge(b_s, half + 1)
                nc.vector.tensor_reduce(negm[:, 0, 4 * half:4 * half + 4], tiles(bank(BANK_T + half), 4, L), AX.X, ALU.max,
                                        negate=True).then_inc(b_max, 1)
            dve.wait_ge(b_mt, 1)
            split_maxima(B, bank(BANK_O)[0:B, 0:P]).then_inc(b_msplit, 1)
            dve.wait_ge(resb, 1)
            for g, (lo, hi) in enumerate(((0, 3), (3, 6), (6, 8))):
                o = tiles(bank((BANK_T, BANK_T + 1, BANK_O + 1)[g]), hi - lo, 129)
                dve.wait_ge(b_pv, g + 1)
                link(nc.vector.reciprocal(rz[:, lo:hi], o[:, :, P]))
                for b in range(lo, hi):
                    dch(stt(racc[:, b, :], o[:, b - lo, 0:P], rz[:, b:b + 1], xres[:, b, :], ALU.mult, ALU.add))
                if g == 1:
                    dch.wait()
                    layernorm(1, 0)
            dch.wait()
            layernorm(1, 1)

            def by_token(n):
                return sm[:, n, 0:B * E0].rearrange("p (b e) -> p b e", e=E0)

            def by_expert(ap):
                return ap.rearrange("p (e b) -> p b e", b=B)

            logits = tiles(bank(BANK_S), B, E0)
            dve.wait_ge(f_log, 1)
            link(nc.vector.tensor_reduce(sm[:, 5, 0:B], logits, AX.X, ALU.max))
            tt(by_token(0), logits, along(sm[:, 5, 0:B], E0), ALU.subtract).then_inc(f_sub, 1)
            link(tt(by_token(2), logits, along(sm[:, 5, 0:B], E0), ALU.is_equal))
            link(nc.vector.tensor_tensor_scan(sm[:, 3, 0:64], con[:, C_R8:C_R8 + 64], sm[:, 2, 0:64], 0.0, ALU.mult, ALU.add))
            link(stt(by_expert(sm[:, 4, 0:64]), by_token(3), 1.0, by_token(2), ALU.is_equal, ALU.mult))
            link(nc.vector.tensor_tensor_scan(sm[:, 7, 0:64], con[:, C_R8:C_R8 + 64], sm[:, 4, 0:64], 0.0, ALU.mult, ALU.add))
            nc.vector.tensor_copy(smb[:, 0, :], sm[:, 4, 0:64]).then_inc(f_one, 1)
            tt(smb[:, 1, :], sm[:, 7, 0:64], sm[:, 4, 0:64], ALU.subtract).then_inc(f_one, 1)
            dve.wait_ge(f_exp, 1)
            link(nc.vector.tensor_reduce(sm[:, 6, 0:B], by_token(1), AX.X, ALU.add))
            link(nc.vector.reciprocal(sm[:, 6, 0:B], sm[:, 6, 0:B]))
            dve.wait_ge(f_cnt, 1)
            count = bank(BANK_S + 1)[:, 0:64]
            link(tt(sm[:, 7, 0:64], count, sm[:, 4, 0:64], ALU.mult))
            link(nc.vector.tensor_reduce(sm[:, 8, 0:B], by_expert(sm[:, 7, 0:64]), AX.X, ALU.add))
            link(ts(sm[:, 10, 0:B], sm[:, 8, 0:B], float(P), None, ALU.is_le))
            link(tt(sm[:, 7, 0:64], sm[:, 4, 0:64], con[:, C_EOFF:C_EOFF + 64], ALU.mult))
            link(nc.vector.tensor_reduce(sm[:, 9, 0:B], by_expert(sm[:, 7, 0:64]), AX.X, ALU.add))
            link(tt(sm[:, 9, 0:B], sm[:, 9, 0:B], sm[:, 8, 0:B], ALU.add))
            link(tt(sm[:, 9, 0:B], sm[:, 9, 0:B], sm[:, 10, 0:B], ALU.mult))
            ts(sm[:, 9, 0:B], sm[:, 9, 0:B], -1.0, None, ALU.add).then_inc(f_slot, 1)
            dve.wait_ge(f_hi, 1)
            tt(racc[:], xres[:], xpart[:, 0, :, :], ALU.subtract).then_inc(f_rest, 1)
            dve.wait_ge(f_mid, 1)
            tt(xpart[:, 2, :, :], racc[:], xpart[:, 1, :, :], ALU.subtract).then_inc(f_part, 1)
            dve.wait_ge(f_slot, 1)
            for b in range(B):
                ts(sel[:, b, :], con[:, C_IOTA:C_IOTA + T], sm[:, 9, b:b + 1], None, ALU.is_equal).then_inc(f_sel, 1)
            dve.wait_ge(f_srowc, 2)
            for e in range(E0):
                ts(selT[:, e, :], slotrow[:], con[:, C_SLOT + e:C_SLOT + e + 1], None, ALU.is_equal).then_inc(f_selT, 1)
            for half in range(2):
                dve.wait_ge(f_ehi, half + 1)
                tt(half_of(eout, half), tiles(bank(BANK_M0 + half), 4, P), epart[:, 0, 4 * half:4 * half + 4, :],
                   ALU.subtract).then_inc(f_erest, 1)
            for half in range(2):
                dve.wait_ge(f_emid, half + 1)
                tt(epart[:, 2, 4 * half:4 * half + 4, :], half_of(eout, half), epart[:, 1, 4 * half:4 * half + 4, :],
                   ALU.subtract).then_inc(f_epart, 1)
            for half in range(2):
                dve.wait_ge(f_y, half + 1)
                for k in range(4):
                    b = 4 * half + k
                    last = stt(racc[:, b, :], bank(BANK_O + half)[:, k * P:(k + 1) * P], sm[:, 6, b:b + 1], xres[:, b, :],
                               ALU.mult, ALU.add)
                    if k < 3:
                        dch(last)
                last.then_inc(f_r, 1)
                dve.wait_ge(f_r, half + 1)
                layernorm(2, half)

            dve.wait_ge(ld_d, 16 * 10)
            for n in range(2):
                dve.wait_ge(D.qk, n + 1)
                ts(rope[:, 2 * n, :], bank(2 + 2 * n, 2), bqkD[:, n:n + 1], HD ** -0.5 if n == 0 else 1.0,
                   ALU.add, ALU.mult).then_inc(D.mul, 1)
                dve.wait_ge(D.mul, n + 1)
                nc.vector.tensor_copy(lams[:, 6:7], lams[:, 5:6]).then_inc(D.full, 1)
            for half in range(2):
                dve.wait_ge(D.vps, half + 1)
                tt(vall[:, 4 * half:4 * half + 4, 0:P], tiles(bank(6 + half), 4, P), over(bvD[:], 4), ALU.add).then_inc(D.vall, 1)
            rest_part(D, 0)
            rest_part(D, 1)
            low_part(D, 0)
            low_part(D, 1)
            heads(D, PAIRS, finish_d, 2)
            dve.wait_ge(resb, 2)
            for half in range(2):
                dve.wait_ge(D.y, half + 1)
                link(tt(half_of(racc, half), tiles(bank(BANK_O + half), 4, P), half_of(xres, half), ALU.add))
                layernorm(3, half)

            def queries(n, slot):
                for half in range(2):
                    dve.wait_ge(e_q, n * 2 + half + 1)
                    ts(qz[64:P, slot, 4 * half:4 * half + 4, 1, :], tiles(bank(BANK_M0 + half)[64:P, :], 4, P), XD ** -0.5,
                       None, ALU.mult).then_inc(e_qd, 1)

            def pair_maxima(n, slot):
                for g in range(4):
                    dve.wait_ge(e_s, n * 4 + g + 1)
                    nc.vector.tensor_reduce(negm[:, slot, 4 * g:4 * g + 4], tiles(bank(BANK_S + g % 2), 4, L), AX.X, ALU.max,
                                            negate=True).then_inc(e_max, 1)

            def pair_split(n, slot, moved):
                dve.wait_ge(e_mt, n + 1)
                if moved is not None:
                    dve.wait_ge(e_mrow[1 - slot], moved * 48)
                split_maxima(16, bank(BANK_M0)[0:16, 0:P]).then_inc(e_msplit, 1)

            def pair_norm(n):
                for half in range(2):
                    o, z = (bank(BANK_O), bank(BANK_O + 1)) if half == 0 else (bank(BANK_S), bank(BANK_S + 1))
                    dve.wait_ge(e_pv, n * 2 + half + 1)
                    link(nc.vector.reciprocal(rzE, tiles(z, 4, P)))
                    tt(otall[:, bass.ds(n, 1), half * HALF:(half + 1) * HALF].rearrange("p a (b c) -> p (a b) c", c=P),
                       tiles(o, 4, P), rzE, ALU.mult).then_inc(e_norm, 1)
                    dve.wait_ge(e_norm, n * 2 + half + 1)

            def pair_step(n, slot, turn, last=False):
                if not last:
                    queries(n + 1, 1 - slot)
                    pair_maxima(n + 1, 1 - slot)
                    pair_split(n + 1, 1 - slot, turn)
                pair_norm(n)

            dve.wait_ge(e_zero, 2)
            queries(0, 0)
            pair_maxima(0, 0)
            pair_split(0, 0, None)
            pair_step(0, 0, 1)
            pair_step(1, 1, 1)
            with dve.Fori(1, PAIRS // 2 - 1) as i:
                dch.enter(i, 1, 2 * (SPLIT + 2))
                for u in range(2):
                    pair_step(i * 2 + u, u, i + 1)
                dch.leave(PAIRS // 2 - 2)
            pair_step(PAIRS - 2, 0, PAIRS // 2)
            pair_step(PAIRS - 1, 1, PAIRS // 2, last=True)
            dve.wait_ge(resb, 3)
            for half in range(2):
                dve.wait_ge(e_y, half + 1)
                link(tt(half_of(racc, half), tiles(bank(BANK_O + half), 4, P), half_of(xres, half), ALU.add))
                layernorm(4, half)

            def b16(n):
                return sm[:, n, :].rearrange("p (b e) -> p b e", e=E1)

            dve.wait_ge(g_log, 1)
            link(tt(b16(5), tiles(bank(BANK_S), B, E1), over(rb1[:], B), ALU.add))
            top = sm[:, 9, 0:B * 8].rearrange("p (b k) -> p b k", k=8)
            for b in range(B):
                dch(nc.vector.max(top[:, b, :], b16(5)[:, b, :]))
            dch.wait()
            tt(b16(0), b16(5), top[:, :, 0:1].to_broadcast([P, B, E1]), ALU.subtract).then_inc(g_sub, 1)
            fourth = top[:, :, TOPK - 1:TOPK].to_broadcast([P, B, E1])
            dch(tt(b16(2), b16(5), fourth, ALU.is_gt))
            link(tt(b16(3), b16(5), fourth, ALU.is_equal))
            dch(nc.vector.tensor_reduce(sm[:, 6, 0:B], b16(2), AX.X, ALU.add))
            link(nc.vector.tensor_tensor_scan(sm[:, 4, :], con[:, C_R16:C_R16 + B * E1], sm[:, 3, :], 0.0, ALU.mult, ALU.add))
            link(ts(sm[:, 6, 0:B], sm[:, 6, 0:B], -1.0, float(TOPK), ALU.mult, ALU.add))
            link(tt(b16(4), b16(4), along(sm[:, 6, 0:B], E1), ALU.is_le))
            link(tt(b16(3), b16(3), b16(4), ALU.mult))
            link(tt(b16(7), b16(2), b16(3), ALU.add))
            dve.wait_ge(g_exp, 1)
            link(tt(b16(7), b16(7), b16(1), ALU.mult))
            link(nc.vector.tensor_reduce(sm[:, 8, 0:B], b16(7), AX.X, ALU.add))
            link(nc.vector.reciprocal(sm[:, 8, 0:B], sm[:, 8, 0:B]))
            tt(b16(11), b16(7), along(sm[:, 8, 0:B], E1), ALU.mult).then_inc(g_c, 1)
            for half in range(2):
                dve.wait_ge(g_b2, half + 1)
                tt(half_of(racc, half), tiles(bank(BANK_O + half), 4, P), half_of(xres, half), ALU.add).then_inc(g_acc, 1)

            def accumulate(e, slot):
                banks = (BANK_M0, BANK_O)[slot]
                for half in range(2):
                    dve.wait_ge(g_dn, e * 2 + half + 1)
                    dve.wait_ge(g_acc, e * 2 + half + 1)
                    for k in range(4):
                        b = 4 * half + k
                        last = stt(racc[:, b, :], bank(banks + half)[:, k * P:(k + 1) * P],
                                   sm[:, 11, bass.ds(b * E1 + e, 1)], racc[:, b, :], ALU.mult, ALU.add)
                        if k < 3:
                            dch(last)
                    last.then_inc(g_acc, 1)

            accumulate(0, 0)
            accumulate(1, 1)
            with dve.Fori(1, E1 // 2) as i:
                dch.enter(i, 1, 12)
                for u in range(2):
                    accumulate(i * 2 + u, u)
                dch.leave(E1 // 2 - 1)
            for half in range(2):
                dve.wait_ge(g_acc, 2 * E1 + half + 1)
                dch.wait()
                layernorm(5, half)


def kernel(**inputs):
    import concourse.bacc as bacc
    from concourse.bass_utils import run_bass_kernel_spmd

    a = {k: np.asarray(v) for k, v in inputs.items()}
    wqkv0 = a["L0_attn_W_qkv"]
    w1 = a["L1_attn_Wqkv"]
    bq1 = a["L1_attn_bqkv"]

    def pair_order(w):
        n = w.shape[1]
        return w.reshape(PAIRS, 2, n, HD).transpose(2, 0, 3, 1).reshape(n, P)

    wkv = a["L1_xattn_w_kv"]
    arrays = {
        "con": constant_table(),
        "xT": a["x"].reshape(T, P).T,
        "x": a["x"].transpose(1, 0, 2),
        "ctxT": a["ctx_768"].reshape(B * L, CD).T,
        "wqk0": wqkv0[:4 * P].reshape(4, P, P).transpose(2, 0, 1),
        "wv0": wqkv0[4 * P:].reshape(2, NH, HD, P).transpose(3, 1, 0, 2).reshape(P, 2 * P),
        "wproj0": a["L0_attn_W_proj"].reshape(P, 2, P).transpose(2, 1, 0),
        "lq1": a["L0_attn_lambda_q1"].reshape(1, HD), "lq2": a["L0_attn_lambda_q2"].reshape(1, HD),
        "lk1": a["L0_attn_lambda_k1"].reshape(1, HD), "lk2": a["L0_attn_lambda_k2"].reshape(1, HD),
        "wqB": a["L0_xattn_Wq"], "wkB": a["L0_xattn_Wk"], "wvB": a["L0_xattn_Wv"],
        "bqB": a["L0_xattn_bq"].reshape(P, 1), "bkB": a["L0_xattn_bk"].reshape(P, 1), "bvB": a["L0_xattn_bv"].reshape(1, P),
        "rw0": a["L0_ffn_router_w"],
        "w1a": a["L0_ffn_w1"].transpose(1, 0, 2),
        "w2a": a["L0_ffn_w2"].reshape(E0, F0, P, P).transpose(2, 0, 1, 3),
        "wqkD": np.stack([pair_order(w1[:, :, 0:HD]), pair_order(w1[:, :, HD:2 * HD])], 1),
        "wvD": w1[:, :, 2 * HD:].transpose(1, 0, 2).reshape(P, P),
        "bqkD": np.stack([pair_order(bq1[:, None, 0:HD])[0], pair_order(bq1[:, None, HD:2 * HD])[0]], 1),
        "bvD": bq1[:, 2 * HD:].reshape(1, P),
        "woD": a["L1_attn_Wout"], "boD": a["L1_attn_bout"].reshape(1, P),
        "wqE": a["L1_xattn_w_q"], "wkE": wkv[:, :NH * XD], "wvE": wkv[:, NH * XD:],
        "woE": a["L1_xattn_w_out"].reshape(PAIRS, P, P).transpose(1, 0, 2), "boE": a["L1_xattn_b_out"].reshape(1, P),
        "rw1": a["L1_ffn_router_w"], "rb1": a["L1_ffn_router_b"].reshape(1, E1), "b2s": a["L1_ffn_b2"],
        "w1b": a["L1_ffn_w1"], "b1": a["L1_ffn_b1"].reshape(E1, F1, P).transpose(0, 2, 1),
        "w2b": a["L1_ffn_w2"].reshape(E1, F1, P, P).transpose(0, 2, 1, 3),
    }
    nc = bacc.Bacc("TRN2", target_bir_lowering=False, num_devices=1)
    feed, d = {}, {}
    for name, v in arrays.items():
        v = np.ascontiguousarray(v)
        feed[f"in_{name}"] = v
        d[name] = nc.dram_tensor(f"in_{name}", v.shape, mybir.dt.from_np(v.dtype), kind="ExternalInput").ap()
    out = nc.dram_tensor("out", (P, B, P), F32, kind="ExternalOutput").ap()
    decoder_kernel(nc, d, out)
    r = run_bass_kernel_spmd(nc, [feed], core_ids=[0])
    return r.results[0]["out"].transpose(1, 0, 2)
```

```python
from contextlib import ExitStack

import numpy as np

import concourse.bass as bass
from concourse import mybir

F32 = mybir.dt.float32
BF16 = mybir.dt.bfloat16
ALU = mybir.AluOpType
ACT = mybir.ActivationFunctionType
AX = mybir.AxisListType

P = 128
B = 8
T = B * P
HALF = T // 2
L = 120
CD = 96
NH = 16
HD = 8
XD = 64
PAIRS = NH // 2
E0 = 8
F0 = 512 // P
E1 = 16
TOPK = 4
F1 = 256 // P
PARTS = 3
ROWS = PARTS * PARTS * HD
MROW = 96
EPS = 1e-5
RING = 4
BIG = -1e30
BANK_M0, BANK_M1, BANK_S, BANK_T, BANK_O = 0, 1, 2, 4, 6

C_ID, C_TRI, C_COSQ, C_SINQ, C_COSK, C_SINK, C_CS, C_CT = (P * n for n in range(8))
C_IOTA = 8 * P
C_R8 = C_IOTA + T
C_R16 = C_R8 + B * E0
C_EOFF = C_R16 + B * E1
C_SLOT = C_EOFF + B * E0
C_ALL = C_SLOT + E0


def constant_table():
    t = np.zeros((P, C_ALL), np.float32)
    n = np.arange(P)
    t[:, C_ID:C_ID + P] = np.eye(P)
    t[:, C_TRI:C_TRI + P] = n[:, None] <= n[None, :]
    inv = (1.0 / np.float32(10000.0) ** (np.arange(0, 2 * HD, 2, dtype=np.float32) / np.float32(2 * HD)))
    angle = (n.astype(np.float32)[None, :] * inv.astype(np.float32)[:, None]).astype(np.float32)
    cos, sin = np.tile(np.cos(angle), (NH, 1)), np.tile(np.sin(angle), (NH, 1))
    scale = HD ** -0.5
    t[:, C_COSQ:C_COSQ + P], t[:, C_SINQ:C_SINQ + P] = cos * scale, sin * scale
    t[:, C_COSK:C_COSK + P], t[:, C_SINK:C_SINK + P] = cos, sin
    t[:, C_CS:C_CS + P] = np.where(n[None, :] > n[:, None], BIG, 0.0)
    t[:, C_CT:C_CT + P] = np.where(n[:, None] > n[None, :], BIG, 0.0)
    t[:, C_IOTA:C_IOTA + T] = np.arange(T)[None, :]
    t[:, C_R8:C_R8 + B * E0] = (np.arange(B * E0) % 8 != 0)[None, :]
    t[:, C_R16:C_R16 + B * E1] = (np.arange(B * E1) % E1 != 0)[None, :]
    t[:, C_EOFF:C_EOFF + B * E0] = (np.arange(B * E0) // B * P)[None, :]
    t[:, C_SLOT:C_SLOT + E0] = np.arange(E0)[None, :] * P + n[:, None]
    return t


class Chain:

    def __init__(self, eng, sem):
        self.eng, self.sem, self.n = eng, sem, 0

    def __call__(self, ins):
        ins.then_inc(self.sem, 1)
        self.n = self.n + 1

    def wait(self):
        self.eng.wait_ge(self.sem, self.n)

    def enter(self, i, first, stride):
        self.entered, self.stride = self.n, stride
        self.n = (i - first) * stride + self.entered
        self.local = self.n

    def leave(self, times):
        self.n = self.entered + times * self.stride


def decoder_kernel(nc, d, out):
    with ExitStack() as ctx:
        def sb(name, shape, dt=F32):
            return ctx.enter_context(nc.sbuf_tensor(name, shape, dt))

        def sem(name):
            return ctx.enter_context(nc.semaphore(name))

        ps = ctx.enter_context(nc.psum_tensor("ps", [P, 8, 512], F32))
        con = sb("con", [P, C_ALL])
        identb, trib, onesb, causS, causT = (sb(n, [P, P], BF16) for n in ("identb", "trib", "onesb", "causS", "causT"))
        onesf = sb("onesf", [P, XD])
        xres = sb("xres", [P, B, P])
        racc = sb("racc", [P, B, P])
        xT = sb("xT", [P, T])
        ctxT = sb("ctxT", [CD, B * L])
        wqk0 = sb("wqk0", [P, 4, P])
        wv0 = sb("wv0", [P, 2 * P])
        wproj0 = sb("wproj0", [P, 2, P])
        lamin = sb("lamin", [P, 4, HD])
        lams = sb("lams", [P, 8])
        wqB, wkB, wvB = sb("wqB", [P, P]), sb("wkB", [CD, P]), sb("wvB", [CD, P])
        bqB, bkB, bvB = sb("bqB", [P, 1]), sb("bkB", [P, 1]), sb("bvB", [P, P])
        rw0 = sb("rw0", [P, E0])
        w1a = sb("w1a", [P, E0, F0 * P])
        w2a = sb("w2a", [P, E0, F0, P])
        before = w2a[:].rearrange("p e f n -> p (e f n)")
        kTB = before[:, 0:960].rearrange("p (a b) -> p a b", a=2)
        vB = before[:, 1024:1024 + B * 132].rearrange("p (b n) -> p b n", b=B)
        wqkD, wvD, woD = sb("wqkD", [P, 2, P]), sb("wvD", [P, P]), sb("woD", [P, P])
        bqkD, bvD, boD = sb("bqkD", [P, 2]), sb("bvD", [P, P]), sb("boD", [P, P])
        boE = sb("boE", [P, P])
        rw1, rb1, b2s = sb("rw1", [P, E1]), sb("rb1", [P, E1]), sb("b2s", [E1, P])
        stq, stk = sb("stq", [P, 2, 2, T], BF16), sb("stk", [P, 2, 2, T], BF16)
        late = w1a[:].rearrange("p e f -> p (e f)").bitcast(BF16).rearrange("p (k s c t) -> p k s c t", k=2, s=2, c=2)
        queries_of = [stq[:, 0], stq[:, 1], late[:, 0, 0], late[:, 0, 1]]
        keys_of = [stk[:, 0], stk[:, 1], late[:, 1, 0], late[:, 1, 1]]
        probs = sb("probs", [P, 2, 16, P])
        outT = sb("outT", [P, 512])
        vall = sb("vall", [P, B, 2 * P])
        vs = sb("vs", [P, 2, 2, B, 32])
        oall = sb("oall", [P, B, 2 * P])
        oT = sb("oT", [P, B, 2, P])
        negm = sb("negm", [P, 2, 16])
        mparts = sb("mparts", [P, 2, PARTS, 16], BF16)
        mres = sb("mres", [P, 16])
        mT = sb("mT", [PARTS * 16, 2, P], BF16)
        mrow = sb("mrow", [PARTS, 2, 16 * P], BF16)
        rz = sb("rz", [P, 16])
        ot1, ot2 = sb("ot1", [P, B, 16]), sb("ot2", [P, B, 16])
        bst, mv = sb("bst", [P, B, 6]), sb("mv", [P, B, 2])
        rstd, mhalf = sb("rstd", [P, B]), sb("mhalf", [P, B])
        sm = sb("sm", [P, 12, 128])
        smb = sb("smb", [P, 2, B * E0], BF16)
        arena = sb("arena", [P, 14976])

        def area(at, *shape, dt=F32, rows=P):
            n = int(np.prod(shape)) * (2 if dt == BF16 else 4) // 4
            a = arena[0:rows, at:at + n]
            if dt == BF16:
                a = a.bitcast(BF16)
            names = "abcd"[:len(shape)]
            return a.rearrange(f"p ({' '.join(names)}) -> p {' '.join(names)}",
                               **dict(zip(names[1:], shape[1:]))) if len(shape) > 1 else a

        rope = area(0, 8, T)
        part = area(8192, 4, PARTS, T, dt=BF16)
        sel = area(0, B, T, dt=BF16)
        selT = area(4096, E0, T, dt=BF16)
        xpart = area(8192, PARTS, B, P, dt=BF16)
        epart = area(9728, PARTS, E0, P, dt=BF16)
        xin = area(11264, T)
        hid0 = area(12288, 2, 512)
        eout = area(13312, E0, P)
        bparts = mparts[:, 0].rearrange("p a b -> p (a b)")[:, 0:PARTS * B]
        slotrow = probs[:, 0, 0:8, :].rearrange("p a b -> p (a b)")
        qB = area(0, B, P)
        otall = area(0, PAIRS, T)
        qz = area(8192, 2, B, 2, P)
        kE = area(12288, 2, B * L)
        wE = area(14208, 2, 3, P)
        vE = w1a[0:L].rearrange("p e f -> p (e f)")[:, 0:2 * 2 * B * (XD + 1)].rearrange(
            "p (s b j n) -> p s b j n", s=2, b=B, j=2)
        outE = w2a[:].rearrange("p e f n -> p (e f n)")[:, 0:T].rearrange("p (t n) -> p t n", n=XD)
        OUT_TILES = ((0, 7, BANK_O), (7, 14, BANK_O + 1), (14, 16, BANK_S))
        hid1 = area(0, 2, F1, T)
        w1s = area(4096, 2, F1 * P)
        w2s = area(4608, 2, F1, P)
        b1s = area(5120, 2, F1)

        stackA = nc.dram_tensor("stackA", [2 * NH * PARTS * HD * 2 * T], BF16, kind="Internal")
        stackD = nc.dram_tensor("stackD", [2 * NH * PARTS * HD * T], BF16, kind="Internal")

        ident = con[:, C_ID:C_ID + P]

        def bank(n, k=1):
            return ps[:, n, :] if k == 1 else ps[:, n:n + k, :].rearrange("p a b -> p (a b)")

        def tiles(ap, n, w):
            return ap[:, 0:n * w].rearrange("p (a b) -> p a b", b=w)

        maxima_bank = bank(BANK_M0)[:, 0:P]

        def over(ap, n):
            return ap.unsqueeze(1).to_broadcast([ap.shape[0], n, ap.shape[1]])

        def early(n, k):
            return isinstance(n, int) and n < k

        def late_head(n, count):
            return isinstance(n, int) and n >= count

        def along(ap, n):
            return ap.unsqueeze(2).to_broadcast([ap.shape[0], ap.shape[1], n])

        ld_a, ld_b, ld_x, ld_f, ld_d, ld_g = (sem(f"ld_{n}") for n in "abxfdg")
        fixed = sem("fixed")
        tables = sem("tables")
        dchain, achain, pchain = sem("dchain"), sem("achain"), sem("pchain")

        stack, mrow_in = ([sem(f"{n}{k}") for k in range(RING)] for n in ("stack", "mrow_in"))

        class Heads:

            def __init__(self, n, turns):
                self.qk = sem(n + "_qk")
                self.mul = sem(n + "_mul")
                self.full = sem(n + "_full")
                self.hi, self.mid, self.lo = sem(n + "_hi"), sem(n + "_mid"), sem(n + "_lo")
                self.rest = sem(n + "_rest")
                self.kept = sem(n + "_kept")
                self.vps, self.vall = sem(n + "_vps"), sem(n + "_vall")
                self.stack, self.mrow, self.turns = stack, mrow_in, turns
                self.s = sem(n + "_s")
                self.max = sem(n + "_max")
                self.msplit = sem(n + "_msplit")
                self.mt = sem(n + "_mt")
                self.mc = sem(n + "_mc")
                self.st = sem(n + "_st")
                self.exp = sem(n + "_exp")
                self.vs = sem(n + "_vs")
                self.pv = sem(n + "_pv")
                self.ot = sem(n + "_ot")
                self.to = sem(n + "_to")
                self.norm = sem(n + "_norm")
                self.post = sem(n + "_post")
                self.postc = sem(n + "_postc")
                self.y = sem(n + "_y")

        A, D = Heads("a", 0), Heads("d", NH // RING)
        ln_var, ln_rstd, ln_out, ln_tp, ln_xT = (sem("ln_" + n) for n in ("var", "rstd", "out", "tp", "xT"))
        resb = sem("resb")
        bkv, bkvc = sem("b_kv"), sem("b_kvc")
        b_q, b_qc, b_s, b_max, b_mt, b_mc, b_msplit, b_mrow, b_st, b_exp, b_pv, b_r = (
            sem("b_" + n) for n in ("q", "qc", "s", "max", "mt", "mc", "msplit", "mrow", "st", "exp", "pv", "r"))
        lam_sum, lam_exp, lam_done = sem("lam_sum"), sem("lam_exp"), sem("lam_done")
        f_log, f_sub, f_exp, f_one, f_cnt, f_slot, f_srow, f_srowc, f_sel, f_selT, f_hi, f_rest, f_mid, f_part = (
            sem("f_" + n) for n in ("log", "sub", "exp", "one", "cnt", "slot", "srow", "srowc", "sel", "selT", "hi",
                                    "rest", "mid", "part"))
        f_xin, f_xinc, f_up, f_gelu, f_dn, f_ehi, f_erest, f_emid, f_epart, f_y, f_r = (
            sem("f_" + n) for n in ("xin", "xinc", "up", "gelu", "dn", "ehi", "erest", "emid", "epart", "y", "r"))
        e_w = [sem("e_w0"), sem("e_w1")]
        e_mrow = [sem("e_mrow0"), sem("e_mrow1")]
        (e_q, e_k, e_v, e_qc, e_kc, e_vc, e_s, e_max, e_mt, e_mc, e_msplit, e_st, e_exp, e_pv, e_norm, e_tp, e_oc,
         e_zero, e_wo, e_y) = (
            sem("e_" + n) for n in ("q", "k", "v", "qc", "kc", "vc", "s", "max", "mt", "mc", "msplit", "st", "exp",
                                    "pv", "norm", "tp", "oc", "zero", "wo", "y"))
        woE = oT[:, 0:4, :, :].rearrange("p a b c -> p (a b) c")
        g_w1, g_w2 = ([sem(f"g_{n}_{k}") for k in range(2)] for n in ("w1", "w2"))
        g_log, g_sub, g_exp, g_c, g_ct, g_ctc, g_b2, g_up, g_gelu, g_dn, g_acc, g_out = (
            sem("g_" + n) for n in ("log", "sub", "exp", "c", "ct", "ctc", "b2", "up", "gelu", "dn", "acc", "out"))

        block = ctx.enter_context(nc.Block())

        @block.sync
        def _(sp):
            def load(dst, src, signal):
                sp.dma_start(dst, src).then_inc(signal, 16)

            load(con[:], d["con"], ld_a)
            load(xT[:], d["xT"], ld_a)
            load(wqk0[:], d["wqk0"], ld_a)
            load(wv0[:], d["wv0"], ld_b)
            load(ctxT[:], d["ctxT"], ld_x)
            for dst, n in ((wqB, "wqB"), (wkB, "wkB"), (wvB, "wvB"), (bqB, "bqB"), (bkB, "bkB")):
                load(dst[:], d[n], ld_x)
            load(bvB[:], d["bvB"].to_broadcast([P, P]), ld_x)
            load(xres[:], d["x"], ld_b)
            load(wproj0[:], d["wproj0"], ld_b)
            for n, name in enumerate(("lq1", "lq2", "lk1", "lk2")):
                load(lamin[:, n, :], d[name].to_broadcast([P, HD]), ld_b)
            load(rw0[:], d["rw0"], ld_f)
            for dst, n in ((wqkD, "wqkD"), (wvD, "wvD"), (woD, "woD"), (bqkD, "bqkD"), (rw1, "rw1"), (b2s, "b2s")):
                load(dst[:], d[n], ld_d)
            for dst, n, w in ((bvD, "bvD", P), (boD, "boD", P), (boE, "boE", P), (rb1, "rb1", E1)):
                load(dst[:], d[n].to_broadcast([P, w]), ld_d)

            def keep(a, n, dst):
                for p, made in enumerate((a.hi, a.mid, a.lo)):
                    sp.wait_ge(made, n + 1)
                    sp.dma_start(dst(p), part[:, n, p, :]).then_inc(a.kept, 16)

            def load_stacks(a, h, slot, base, count):
                head = PARTS * HD * 2 * T
                sp.dma_start(keys_of[slot][0:ROWS], bass.AP(
                    base, h * head + count * head, [[0, PARTS], [2 * T, PARTS * HD], [1, 2 * T]])).then_inc(a.stack[slot], 16)
                for p in range(PARTS):
                    sp.dma_start(queries_of[slot][p * PARTS * HD:(p + 1) * PARTS * HD], bass.AP(
                        base, h * head + p * HD * 2 * T, [[0, PARTS], [2 * T, HD], [1, 2 * T]])
                    ).then_inc(a.stack[slot], 16)

            def move_maxima(a, made, slot):
                sp.wait_ge(a.mc, made)
                sp.dma_start(queries_of[slot][MROW:MROW + PARTS], mT[:, slot % 2, :]).then_inc(a.mrow[slot], 16)

            def heads(a, count, base):
                sp.wait_ge(a.kept, 16 * (12 if count == NH else 6))
                sp.wait_ge(fixed, 5 if count == NH else 14)
                for h in range(RING):
                    load_stacks(a, h, h, base, count)
                move_maxima(a, 1, 0)
                with sp.Fori(0, count // RING - 1) as i:
                    later = [sp.snap(i * RING + (u + RING)) for u in range(RING)]
                    made = [sp.snap(i * RING + (u + 2)) for u in range(RING)]
                    used = [sp.snap(i * (4 * RING) + 4 * (u + 1)) for u in range(RING)]
                    for u in range(RING):
                        move_maxima(a, made[u], (u + 1) % RING)
                        sp.wait_ge(a.st, used[u])
                        load_stacks(a, later[u], u, base, count)
                for u in range(RING - 1):
                    move_maxima(a, count - RING + u + 2, u + 1)

            for n, (t, c) in enumerate(((0, 0), (0, 1), (1, 0), (1, 1))):
                keep(A, n, lambda p: bass.AP(
                    stackA, t * NH * PARTS * HD * 2 * T + p * HD * 2 * T + c * T,
                    [[PARTS * HD * 2 * T, NH], [2 * T, HD], [1, T]]))
            heads(A, NH, stackA)
            sp.wait_ge(A.st, 4 * NH)
            load(w1a[:], d["w1a"], ld_f)
            sp.wait_ge(b_mc, 1)
            sp.dma_start(mrow[0:PARTS, 0, 0:T], mT[0:PARTS * B, 0, :]).then_inc(b_mrow, 16)
            sp.wait_ge(b_pv, 3)
            load(w2a[:], d["w2a"], ld_f)
            for t in range(2):
                keep(D, t, lambda p: bass.AP(
                    stackD, (t * PAIRS * PARTS + p) * 2 * HD * T, [[PARTS * 2 * HD * T, PAIRS], [T, 2 * HD], [1, T]]))
            heads(D, PAIRS, stackD)

            def weights(pair, slot):
                for n, name in enumerate(("wqE", "wkE", "wvE")):
                    rows = P if n == 0 else CD
                    sp.dma_start(wE[0:rows, slot, n, :], d[name][0:rows, bass.ds(pair * P, P)]).then_inc(e_w[slot], 16)

            def maxima(made, slot):
                sp.wait_ge(e_mc, made)
                sp.dma_start(mrow[0:PARTS, slot, :], mT[:, slot, :]).then_inc(e_mrow[slot], 16)

            sp.wait_ge(D.y, 2)
            sp.dma_start(woE, d["woE"]).then_inc(e_wo, 16)
            sp.wait_ge(e_zero, 3)
            weights(0, 0)
            weights(1, 1)
            maxima(1, 0)
            with sp.Fori(0, PAIRS // 2 - 1) as i:
                pair = [sp.snap(i * 2 + (u + 2)) for u in range(2)]
                projected = [sp.snap(i * 4 + 2 * (u + 1)) for u in range(2)]
                for u in range(2):
                    sp.wait_ge(e_v, projected[u])
                    weights(pair[u], u)
                    maxima(pair[u], 1 - u)
            maxima(PAIRS, 1)

            def up_weights(e, slot):
                sp.dma_start(w1s[:, slot, :], d["w1b"][bass.ds(e, 1), :, :]).then_inc(g_w1[slot], 16)
                sp.dma_start(b1s[:, slot, :], d["b1"][bass.ds(e, 1), :, :]).then_inc(g_w1[slot], 16)

            def down_weights(e, slot):
                sp.dma_start(w2s[:, slot, :, :], d["w2b"][bass.ds(e, 1), :, :, :]).then_inc(g_w2[slot], 16)

            sp.wait_ge(e_y, 2)
            for e in range(2):
                up_weights(e, e)
                down_weights(e, e)
            with sp.Fori(0, E1 // 2 - 1) as i:
                nxt = [sp.snap(i * 2 + (u + 2)) for u in range(2)]
                done = [sp.snap(i * 8 + 4 * (u + 1)) for u in range(2)]
                used = [sp.snap(i * 4 + 2 * (u + 1)) for u in range(2)]
                for u in range(2):
                    sp.wait_ge(g_gelu, done[u])
                    up_weights(nxt[u], u)
                    sp.wait_ge(g_dn, used[u])
                    down_weights(nxt[u], u)
            for half in range(2):
                sp.wait_ge(ln_out, 2 * 5 + half + 1)
                sp.dma_start(out[:, 4 * half:4 * half + 4, :], xres[:, 4 * half:4 * half + 4, :]).then_inc(g_out, 16)
            sp.wait_ge(g_out, 32)

        @block.gpsimd
        def _(pool):
            for n, (tile, value) in enumerate((
                    (stq[64:MROW, :, :, :], 0.0), (stk[64:MROW, :, :, :], 0.0), (stk[MROW:MROW + PARTS, :, :, :], 1.0),
                    (late[64:MROW], 0.0), (late[MROW:MROW + PARTS, 1], 1.0),
                    (onesb[:], 1.0), (onesf[:], 1.0), (mhalf[:], -0.5), (vB[:, :, P:P + 1], 1.0), (vs[:], 0.0),
                    (vs[:, :, :, :, 16:17], 1.0))):
                nc.gpsimd.memset(tile, value).then_inc(fixed, 1)
                pool.wait_ge(fixed, n + 1)
            pch = Chain(pool, pchain)

            for n in range(4):
                pool.wait_ge(A.mul, n + 1)
                op = ALU.subtract if n % 2 == 0 else ALU.add
                nc.gpsimd.tensor_tensor(rope[:, 2 * n, :], rope[:, 2 * n, :], rope[:, 2 * n + 1, :], op).then_inc(A.full, 1)

            def values(a, h, slot, width):
                if width == 16:
                    return nc.gpsimd.tensor_copy(vs[:, slot, 0, :, 0:16], vall[:, :, bass.ds(h * 16, 16)])
                return nc.gpsimd.tensor_copy(
                    vs[:, slot, :, :, 0:8].rearrange("p c b d -> p b c d"),
                    vall[:, :, bass.ds(h * 16, 16)].rearrange("p b (c d) -> p b c d", c=2))

            def heads(a, count, width):
                pool.wait_ge(a.vall, 4 if width == 16 else 2)
                values(a, 0, 0, width).then_inc(a.vs, 1)
                values(a, 1, 1, width).then_inc(a.vs, 1)
                with pool.Fori(1, count // 2) as i:
                    for u in range(2):
                        pool.wait_ge(a.pv, i * 2 + u - 1)
                        values(a, i * 2 + u, u, width).then_inc(a.vs, 1)

            def rsqrt(k, half):
                s = slice(4 * half, 4 * half + 4)
                pool.wait_ge(ln_var, 2 * k + half + 1)
                pch(nc.gpsimd.tensor_scalar(rstd[:, s], mv[:, s, 1], EPS, None, ALU.add))
                pch.wait()
                nc.gpsimd.tensor_tensor(rstd[:, s], rstd[:, s], mhalf[:, s], ALU.pow).then_inc(ln_rstd, 1)

            def add_bias(k, bias):
                pool.wait_ge(ln_xT, 2 * k)
                pool.wait_ge(ln_out, 2 * k)
                nc.gpsimd.tensor_tensor(xres[:], xres[:], over(bias[:], B), ALU.add).then_inc(resb, 1)

            heads(A, NH, 16)
            rsqrt(0, 0)
            rsqrt(0, 1)
            pool.wait_ge(ld_x, 16 * 7)
            add_bias(1, bvB)
            rsqrt(1, 0)
            rsqrt(1, 1)
            rsqrt(2, 0)
            rsqrt(2, 1)
            pool.wait_ge(ld_d, 16 * 10)
            add_bias(3, boD)
            nc.gpsimd.memset(vs[:, :, :, :, 8:9], 1.0).then_inc(fixed, 1)
            pool.wait_ge(f_up, E0)
            pool.wait_ge(fixed, 12)
            nc.gpsimd.memset(late[64:MROW], 0.0).then_inc(fixed, 1)
            pool.wait_ge(fixed, 13)
            nc.gpsimd.memset(late[MROW:MROW + PARTS, 1], 1.0).then_inc(fixed, 1)
            pool.wait_ge(fixed, 14)
            heads(D, PAIRS, 8)
            rsqrt(3, 0)
            rsqrt(3, 1)
            pool.wait_ge(D.lo, 2)
            pool.wait_ge(D.kept, 16 * 6)
            pool.wait_ge(ln_rstd, 8)
            nc.gpsimd.memset(qz[0:64, :, :, 1, :], 0.0).then_inc(e_zero, 1)
            pool.wait_ge(e_zero, 1)
            nc.gpsimd.memset(qz[64:128, :, :, 0, :], 0.0).then_inc(e_zero, 1)
            pool.wait_ge(e_zero, 2)
            pool.wait_ge(D.st, 4 * PAIRS)
            nc.gpsimd.memset(vE[:, :, :, :, XD:XD + 1], 1.0).then_inc(e_zero, 1)
            pool.wait_ge(e_zero, 3)
            add_bias(4, boE)
            rsqrt(4, 0)
            rsqrt(4, 1)
            rsqrt(5, 0)
            rsqrt(5, 1)

        @block.tensor
        def _(pe):
            mm = nc.tensor.matmul

            def scores(a, n, slot, g, causal):
                if not early(4 * n + g, 2):
                    pe.wait_ge(a.max, 4 * n + g - 1)
                o = bank(BANK_S + g % 2)
                if causal:
                    mm(tiles(o, 4, P), identb[:], over(causS[:], 4), start=True, stop=False)
                for k in range(4):
                    c, b = divmod(4 * g + k, B)
                    last = mm(o[:, k * P:(k + 1) * P], queries_of[slot][0:MROW, c, b * P:(b + 1) * P],
                              keys_of[slot][0:MROW, c, b * P:(b + 1) * P], start=not causal, stop=not causal or k == 3)
                last.then_inc(a.s, 1)

            def scores_t(a, n, slot, g, causal):
                if not early(4 * n + g, 2):
                    pe.wait_ge(a.exp, 4 * n + g - 1)
                o = bank(BANK_T + g % 2)
                if causal:
                    mm(tiles(o, 4, P), identb[:], over(causT[:], 4), start=True, stop=False)
                for k in range(4):
                    c, b = divmod(4 * g + k, B)
                    last = mm(o[:, k * P:(k + 1) * P], keys_of[slot][0:MROW + PARTS, c, b * P:(b + 1) * P],
                              queries_of[slot][0:MROW + PARTS, c, b * P:(b + 1) * P],
                              start=not causal, stop=not causal or k == 3)
                last.then_inc(a.st, 1)

            def head_maxima(a, n, slot):
                pe.wait_ge(a.msplit, n + 1)
                if not early(n, 1):
                    pe.wait_ge(a.mc, n)
                mm(maxima_bank[0:PARTS * 16, :], mparts[:, slot % 2].rearrange("p a b -> p (a b)"), identb[:], start=True, stop=True).then_inc(a.mt, 1)

            def head_values(a, n, slot, pair):
                pe.wait_ge(a.vs, n + 1)
                pe.wait_ge(a.exp, 4 * n + 4)
                if not early(n, 2):
                    pe.wait_ge(a.ot, n - 1)
                for tile in range(16):
                    c, b = divmod(tile, B)
                    col = (c * 2 + b // 4) * P
                    last = mm(bank(BANK_O + slot % 2)[32 * (b % 4):32 * (b % 4) + 32, col:col + P],
                              vs[:, slot % 2, c if pair else 0, b, :], probs[:, slot % 2, tile, :], start=True, stop=True)
                last.then_inc(a.pv, 1)

            def head_token(a, n):
                pe.wait_ge(a.ot, n + 1)
                if not early(n, 1):
                    pe.wait_ge(a.norm, n)
                for k in range(4):
                    last = nc.tensor.transpose(bank(BANK_M1)[:, k * P:(k + 1) * P], outT[:, k * P:(k + 1) * P], ident)
                last.then_inc(a.to, 1)

            def heads(a, count, pair, causal):
                def step(n, slot, turn):
                    ahead, after_ahead, before = ((slot + k) % RING for k in (1, 2, -1))
                    if not late_head(n + 2, count):
                        pe.wait_ge(a.stack[after_ahead], (a.turns + turn + (slot + 2) // RING) * 64)
                        scores(a, n + 2, after_ahead, 0, causal)
                        scores(a, n + 2, after_ahead, 1, causal)
                    if not late_head(n, count):
                        pe.wait_ge(a.mrow[slot], (a.turns + turn) * 16)
                        scores_t(a, n, slot, 0, causal)
                        scores_t(a, n, slot, 1, causal)
                    if not late_head(n + 1, count):
                        head_maxima(a, n + 1, ahead)
                    if not early(n, 1):
                        head_values(a, n - 1, before, pair)
                    if not late_head(n + 2, count):
                        scores(a, n + 2, after_ahead, 2, causal)
                        scores(a, n + 2, after_ahead, 3, causal)
                    if not late_head(n, count):
                        scores_t(a, n, slot, 2, causal)
                        scores_t(a, n, slot, 3, causal)
                    if not early(n, 1):
                        head_token(a, n - 1)

                for h in range(2):
                    pe.wait_ge(a.stack[h], (a.turns + 1) * 64)
                    for g in range(4):
                        scores(a, h, h, g, causal)
                head_maxima(a, 0, 0)
                for n in range(RING):
                    step(n, n, 1)
                if count > 2 * RING:
                    with pe.Fori(1, count // RING - 1) as i:
                        for u in range(RING):
                            step(i * RING + u, u, i + 1)
                for n in range(count - RING, count + 1):
                    step(n, n % RING, n // RING + 1)

            def finish(a, chunks, w):
                pe.wait_ge(a.norm, NH if chunks == 2 else PAIRS)
                per = 4 // chunks
                banks = (BANK_S, BANK_S + 1, BANK_T, BANK_T + 1)
                for g in range(B // per):
                    for k in range(per):
                        for c in range(chunks):
                            o = bank(banks[g])[:, (k * chunks + c) * P:(k * chunks + c + 1) * P]
                            last = nc.tensor.transpose(o, oall[:, g * per + k, c * P:(c + 1) * P], ident)
                    last.then_inc(a.post, 1)
                for half in range(2):
                    pe.wait_ge(a.postc, (half + 1) * B // per // 2)
                    for k in range(4):
                        b = 4 * half + k
                        for c in range(chunks):
                            last = mm(bank(BANK_O + half)[:, k * P:(k + 1) * P], oT[:, b, c, :],
                                      w[:, c, :] if chunks == 2 else w[:],
                                      start=c == 0, stop=c == chunks - 1)
                    last.then_inc(a.y, 1)

            def to_feature(k):
                for half in range(2):
                    pe.wait_ge(ln_out, 2 * k + half + 1)
                    for j in range(4):
                        last = nc.tensor.transpose(bank(BANK_M0 + half)[:, j * P:(j + 1) * P],
                                                   xres[:, 4 * half + j, :], ident)
                    last.then_inc(ln_tp, 1)

            pe.wait_ge(ld_a, 48)
            for t in range(4):
                for half in range(2):
                    last = mm(bank(2 * t + half), wqk0[:, t, :], xT[:, half * HALF:(half + 1) * HALF],
                              start=True, stop=True)
                last.then_inc(A.qk, 1)
            pe.wait_ge(ld_b, 16 * 7)
            pe.wait_ge(A.mul, 2)
            for g in range(4):
                for k in range(2):
                    b = 2 * g + k
                    last = mm(bank(g)[:, k * 256:(k + 1) * 256], xT[:, b * P:(b + 1) * P], wv0[:], start=True, stop=True)
                last.then_inc(A.vps, 1)
            pe.wait_ge(ld_x, 16 * 7)
            pe.wait_ge(A.mul, 4)
            for half in range(2):
                mm(bank(4 + half)[:, 0:480], wkB[:], ctxT[:, half * 480:(half + 1) * 480],
                   start=True, stop=True).then_inc(bkv, 1)
            for half in range(2):
                for k in range(4):
                    b = 4 * half + k
                    last = mm(bank(6 + half)[0:L, k * P:(k + 1) * P], ctxT[:, b * L:(b + 1) * L], wvB[:],
                              start=True, stop=True)
                last.then_inc(bkv, 1)
            pe.wait_ge(A.vall, 4)
            pe.wait_ge(bkvc, 4)
            pe.wait_ge(fixed, 11)
            pe.wait_ge(tables, 4)
            heads(A, NH, pair=False, causal=False)
            finish(A, 2, wproj0)
            to_feature(0)

            for half in range(2):
                pe.wait_ge(ln_xT, half + 1)
                mm(bank(BANK_S + half), wqB[:], xT[:, half * HALF:(half + 1) * HALF], start=True, stop=True).then_inc(b_q, 1)
            kb = before[:, 0:960]
            for half in range(2):
                pe.wait_ge(b_qc, half + 1)
                for k in range(4):
                    b = 4 * half + k
                    last = mm(bank(BANK_T + half)[:, k * L:(k + 1) * L], qB[:, b, :], kb[:, b * L:(b + 1) * L],
                              start=True, stop=True)
                last.then_inc(b_s, 1)
            pe.wait_ge(b_max, 2)
            pe.wait_ge(b_msplit, 1)
            mm(maxima_bank[0:PARTS * B, :], bparts, identb[:], start=True, stop=True).then_inc(b_mt, 1)
            pe.wait_ge(b_mrow, 16)
            for half in range(2):
                o = bank(BANK_S + half)
                mm(o[0:L, :], onesb[0:PARTS, 0:L], mrow[:, 0, half * 512:(half + 1) * 512], start=True, stop=False)
                for k in range(4):
                    b = 4 * half + k
                    last = mm(o[0:L, k * P:(k + 1) * P], kb[:, b * L:(b + 1) * L], qB[:, b, :], start=False, stop=k == 3)
                last.then_inc(b_st, 1)
            for g, (lo, hi) in enumerate(((0, 3), (3, 6), (6, 8))):
                o = bank((BANK_T, BANK_T + 1, BANK_O + 1)[g])
                pe.wait_ge(b_exp, 1 if hi <= 4 else 2)
                for b in range(lo, hi):
                    last = mm(o[:, (b - lo) * 129:(b - lo + 1) * 129], probs[0:L, 0, b, :], vB[0:L, b, 0:129],
                              start=True, stop=True)
                last.then_inc(b_pv, 1)
            to_feature(1)

            for b in range(B):
                pe.wait_ge(ln_xT, 2 + b // 4 + 1)
                last = mm(bank(BANK_S)[:, b * E0:(b + 1) * E0], xT[:, b * P:(b + 1) * P], rw0[:], start=True, stop=True)
            last.then_inc(f_log, 1)
            pe.wait_ge(f_one, 2)
            mm(bank(BANK_S + 1)[:, 0:B * E0], trib[:], smb[:, 0, :], start=True, stop=False)
            mm(bank(BANK_S + 1)[:, 0:B * E0], onesb[:], smb[:, 1, :], start=False, stop=True).then_inc(f_cnt, 1)
            pe.wait_ge(f_slot, 1)
            for b in range(B):
                last = mm(bank(BANK_T + b // 4)[:, b % 4 * P:(b % 4 + 1) * P],
                          sm[:, 9, b:b + 1].to_broadcast([P, P]), ident, start=True, stop=True)
                if b % 4 == 3:
                    last.then_inc(f_srow, 1)
            pe.wait_ge(f_part, 1)
            pe.wait_ge(f_mid, 1)
            pe.wait_ge(f_hi, 1)
            for b in range(B):
                pe.wait_ge(f_sel, b + 1)
                for half in range(2):
                    for p in range(PARTS):
                        last = mm(bank(BANK_O + half), xpart[:, p, b, :], sel[:, b, half * HALF:(half + 1) * HALF],
                                  start=b == 0 and p == 0, stop=b == B - 1 and p == PARTS - 1)
                if b == B - 1:
                    last.then_inc(f_xin, 1)
            pe.wait_ge(f_xinc, 2)
            pe.wait_ge(ld_f, 16 * 3)
            for e in range(E0 + 1):
                if e < E0:
                    if e >= 2:
                        pe.wait_ge(f_gelu, e - 1)
                    for f in range(F0):
                        last = mm(bank(BANK_S + e % 2)[:, f * P:(f + 1) * P], w1a[:, e, f * P:(f + 1) * P],
                                  xin[:, e * P:(e + 1) * P], start=True, stop=True)
                    last.then_inc(f_up, 1)
                if e > 0:
                    x = e - 1
                    pe.wait_ge(f_gelu, x + 1)
                    for f in range(F0):
                        last = mm(bank(BANK_M0 + x // 4)[:, x % 4 * P:(x % 4 + 1) * P], hid0[:, x % 2, f * P:(f + 1) * P],
                                  w2a[:, x, f, :], start=f == 0, stop=f == F0 - 1)
                    last.then_inc(f_dn, 1)
            pe.wait_ge(f_epart, 2)
            pe.wait_ge(f_selT, E0)
            for b in range(B):
                o = bank(BANK_O + b // 4)[:, b % 4 * P:(b % 4 + 1) * P]
                for e in range(E0):
                    for p in range(PARTS):
                        last = mm(o, selT[:, e, b * P:(b + 1) * P], epart[:, p, e, :],
                                  start=e == 0 and p == 0, stop=e == E0 - 1 and p == PARTS - 1)
                if b % 4 == 3:
                    last.then_inc(f_y, 1)
            pe.wait_ge(f_ehi, 2)
            to_feature(2)

            pe.wait_ge(f_r, 2)
            for t in range(2):
                for half in range(2):
                    pe.wait_ge(ln_xT, 4 + half + 1)
                    last = mm(bank(2 + 2 * t + half), wqkD[:, t, :], xT[:, half * HALF:(half + 1) * HALF],
                              start=True, stop=True)
                last.then_inc(D.qk, 1)
            for half in range(2):
                for k in range(4):
                    b = 4 * half + k
                    last = mm(bank(6 + half)[:, k * P:(k + 1) * P], xT[:, b * P:(b + 1) * P], wvD[:], start=True, stop=True)
                last.then_inc(D.vps, 1)
            pe.wait_ge(D.vall, 2)
            pe.wait_ge(D.mul, 2)
            heads(D, PAIRS, pair=True, causal=True)
            finish(D, 1, woD)
            to_feature(3)

            def project(n, slot, turn):
                pe.wait_ge(e_w[slot], turn * 48)
                if not early(n, 1):
                    pe.wait_ge(e_mc, n)
                if not early(n, 1):
                    pe.wait_ge(e_vc, n * 2)
                for half in range(2):
                    mm(bank(BANK_M0 + half), wE[:, slot, 0, :], xT[:, half * HALF:(half + 1) * HALF],
                       start=True, stop=True).then_inc(e_q, 1)
                for half in range(2):
                    pe.wait_ge(e_qc, n * 4 + 2 * half + 2)
                    mm(bank(BANK_M0 + half)[:, 0:480], wE[0:CD, slot, 1, :], ctxT[:, half * 480:(half + 1) * 480],
                       start=True, stop=True).then_inc(e_k, 1)
                for half in range(2):
                    pe.wait_ge(e_kc, n * 2 + half + 1)
                    for k in range(4):
                        b = 4 * half + k
                        last = mm(bank(BANK_M0 + half)[0:L, k * P:(k + 1) * P], ctxT[:, b * L:(b + 1) * L],
                                  wE[0:CD, slot, 2, :], start=True, stop=True)
                    last.then_inc(e_v, 1)

            def pair_scores(n, slot):
                for g in range(4):
                    if not early(4 * n + g, 2):
                        pe.wait_ge(e_max, n * 4 + g - 1)
                    if g == 0 and not early(n, 2):
                        pe.wait_ge(e_norm, 3 * (n - 1))
                    for k in range(4):
                        b, j = 2 * g + k // 2, k % 2
                        last = mm(bank(BANK_S + g % 2)[:, k * L:(k + 1) * L], qz[:, slot, b, j, :],
                                  kE[:, slot, b * L:(b + 1) * L], start=True, stop=True)
                    last.then_inc(e_s, 1)

            def pair_scores_t(n, slot, turn):
                pe.wait_ge(e_mrow[slot], turn * 16)
                for g in range(4):
                    if g >= 2:
                        pe.wait_ge(e_exp, n * 4 + g - 1)
                    elif not early(n, 1):
                        pe.wait_ge(e_oc, n * 2 + g - 1)
                    o = bank(BANK_T + g % 2)
                    mm(o[0:L, :], onesb[0:PARTS, 0:L], mrow[:, slot, g * 512:(g + 1) * 512], start=True, stop=False)
                    for k in range(2):
                        b = 2 * g + k
                        last = mm(o[0:L, k * 256:(k + 1) * 256], kE[:, slot, b * L:(b + 1) * L],
                                  qz[:, slot, b, :, :].rearrange("p a b -> p (a b)"), start=False, stop=k == 1)
                    last.then_inc(e_st, 1)

            def pair_maxima(n, slot):
                pe.wait_ge(e_msplit, n + 1)
                pe.wait_ge(e_vc, n * 2 + 2)
                mm(maxima_bank[0:PARTS * 16, :], mparts[:, slot].rearrange("p a b -> p (a b)"), identb[:], start=True, stop=True).then_inc(e_mt, 1)

            def pair_values(n, slot):
                for g, (lo, hi, at) in enumerate(OUT_TILES):
                    if not early(n, 1):
                        pe.wait_ge(e_norm, 3 * (n - 1) + g + 1)
                    pe.wait_ge(e_exp, n * 4 + (hi + 3) // 4)
                    for tile in range(lo, hi):
                        last = mm(bank(at)[:, (tile - lo) * (XD + 1):(tile - lo + 1) * (XD + 1)], probs[0:L, slot, tile, :],
                                  vE[:, slot, tile // 2, tile % 2, :], start=True, stop=True)
                    last.then_inc(e_pv, 1)

            def pair_outputs(n):
                for half in range(2):
                    pe.wait_ge(e_norm, 3 * n + 3)
                    for k in range(4):
                        tile = 2 * (4 * half + k)
                        last = nc.tensor.transpose(bank(BANK_T + half)[:, k * P:(k + 1) * P],
                                                   outE[:, tile:tile + 2, :].rearrange("p a b -> p (a b)"), ident)
                    last.then_inc(e_tp, 1)

            def pair_step(n, slot, turn, last=False):
                if not last:
                    project(n + 1, 1 - slot, turn + slot)
                if not early(n, 1):
                    pair_outputs(n - 1)
                if not last:
                    pe.wait_ge(e_vc, (n + 2) * 2)
                    pair_scores(n + 1, 1 - slot)
                pair_scores_t(n, slot, turn)
                if not last:
                    pair_maxima(n + 1, 1 - slot)
                pair_values(n, slot)

            pe.wait_ge(ln_xT, 8)
            project(0, 0, 1)
            pe.wait_ge(e_vc, 2)
            pair_scores(0, 0)
            pair_maxima(0, 0)
            pair_step(0, 0, 1)
            pair_step(1, 1, 1)
            with pe.Fori(1, PAIRS // 2 - 1) as i:
                for u in range(2):
                    pair_step(i * 2 + u, u, i + 1)
            pair_step(PAIRS - 2, 0, PAIRS // 2)
            pair_step(PAIRS - 1, 1, PAIRS // 2, last=True)
            pair_outputs(PAIRS - 1)
            pe.wait_ge(e_oc, 2 * PAIRS)
            pe.wait_ge(e_wo, 16)
            for half in range(2):
                for k in range(4):
                    b = 4 * half + k
                    for p in range(PAIRS):
                        last = mm(bank(BANK_O + half)[:, k * P:(k + 1) * P], otall[:, p, b * P:(b + 1) * P], woE[:, p, :],
                                  start=p == 0, stop=p == PAIRS - 1)
                last.then_inc(e_y, 1)
            to_feature(4)

            for b in range(B):
                pe.wait_ge(ln_xT, 8 + b // 4 + 1)
                last = mm(bank(BANK_S)[:, b * E1:(b + 1) * E1], xT[:, b * P:(b + 1) * P], rw1[:], start=True, stop=True)
            last.then_inc(g_log, 1)

            def up(e, slot, turn, first=False):
                pe.wait_ge(g_w1[slot], turn * 32)
                for f in range(F1):
                    for half in range(2):
                        u = 2 * f + half
                        if not first:
                            pe.wait_ge(g_gelu, e * 4 + u - 3)
                        mm(bank(BANK_S + u), w1s[:, slot, f * P:(f + 1) * P], xT[:, half * HALF:(half + 1) * HALF],
                           start=True, stop=True).then_inc(g_up, 1)

            def down(e, slot, turn, first=False):
                banks = (BANK_M0, BANK_O)[slot]
                pe.wait_ge(g_w2[slot], turn * 16)
                pe.wait_ge(g_gelu, e * 4 + 4)
                for half in range(2):
                    if not first:
                        pe.wait_ge(g_acc, e * 2 + half - 1)
                    for k in range(4):
                        b = 4 * half + k
                        for f in range(F1):
                            last = mm(bank(banks + half)[:, k * P:(k + 1) * P], hid1[:, slot, f, b * P:(b + 1) * P],
                                      w2s[:, slot, f, :], start=f == 0, stop=f == F1 - 1)
                    last.then_inc(g_dn, 1)

            pe.wait_ge(g_c, 1)
            for half in range(2):
                for k in range(4):
                    b = 4 * half + k
                    last = nc.tensor.transpose(bank(BANK_O + half)[0:E1, k * P:(k + 1) * P], sm[:, 11, b * E1:(b + 1) * E1],
                                               ident)
                last.then_inc(g_ct, 1)
            up(0, 0, 1, first=True)
            pe.wait_ge(g_ctc, 2)
            for half in range(2):
                for k in range(4):
                    b = 4 * half + k
                    last = mm(bank(BANK_O + half)[:, k * P:(k + 1) * P], oT[0:E1, b, 0, :], b2s[:], start=True, stop=True)
                last.then_inc(g_b2, 1)
            up(1, 1, 1)
            down(0, 0, 1, first=True)
            up(2, 0, 2)
            pe.wait_ge(g_acc, 2)
            down(1, 1, 1, first=True)
            with pe.Fori(1, E1 // 2 - 1) as i:
                for u in range(2):
                    up(i * 2 + u + 1, 1 - u, i + 1 + u)
                    down(i * 2 + u, u, i + 1)
            up(E1 - 1, 1, E1 // 2)
            down(E1 - 2, 0, E1 // 2)
            down(E1 - 1, 1, E1 // 2)

        @block.scalar
        def _(act):
            ach = Chain(act, achain)

            def fn(o, i, f, **kw):
                return nc.scalar.activation(o, i, f, **kw)

            def parts_hi_mid(a, n, src):
                act.wait_ge(a.full, n + 1)
                fn(part[:, n, 0, :], src, ACT.Copy).then_inc(a.hi, 1)

            def part_mid(a, n, src):
                act.wait_ge(a.rest, n + 1)
                fn(part[:, n, 1, :], src, ACT.Copy).then_inc(a.mid, 1)

            def heads(a, count):
                def exponentials(n, slot, g):
                    act.wait_ge(a.st, 4 * n + g + 1)
                    if g == 0 and not early(n, 2):
                        act.wait_ge(a.pv, n - 1)
                    fn(probs[:, slot % 2, 4 * g:4 * g + 4, :], tiles(bank(BANK_T + g % 2), 4, P), ACT.Exp).then_inc(a.exp, 1)

                def copy_maxima(n, slot, moved):
                    act.wait_ge(a.mt, n + 1)
                    if not early(n, 2):
                        act.wait_ge(a.mrow[(slot - 2) % RING], (a.turns + moved) * 16)
                    fn(mT[:, slot % 2, :], maxima_bank[0:PARTS * 16, :], ACT.Copy).then_inc(a.mc, 1)

                def copy_outputs(n, slot):
                    act.wait_ge(a.pv, n + 1)
                    if not early(n, 1):
                        act.wait_ge(a.to, n)
                    fn(outT[:], bank(BANK_O + slot % 2), ACT.Copy).then_inc(a.ot, 1)

                def step(n, slot, turn):
                    if not late_head(n, count):
                        exponentials(n, slot, 0)
                        exponentials(n, slot, 1)
                    if not late_head(n + 1, count):
                        copy_maxima(n + 1, (slot + 1) % RING, turn if slot > 0 else turn - 1)
                    if not early(n, 1):
                        copy_outputs(n - 1, (slot - 1) % RING)
                    if not late_head(n, count):
                        exponentials(n, slot, 2)
                        exponentials(n, slot, 3)

                copy_maxima(0, 0, None)
                for n in range(RING):
                    step(n, n, 1)
                if count > 2 * RING:
                    with act.Fori(1, count // RING - 1) as i:
                        for u in range(RING):
                            step(i * RING + u, u, i + 1)
                for n in range(count - RING, count + 1):
                    step(n, n % RING, n // RING + 1)

            def finish(a, chunks):
                per = 4 // chunks
                banks = (BANK_S, BANK_S + 1, BANK_T, BANK_T + 1)
                for g in range(B // per):
                    act.wait_ge(a.post, g + 1)
                    o = oT[:, g * per:(g + 1) * per, 0:chunks, :]
                    fn(o, bank(banks[g]).rearrange("p (a b c) -> p a b c", b=chunks, c=P), ACT.Copy).then_inc(a.postc, 1)

            def feature_copies(k):
                for half in range(2):
                    act.wait_ge(ln_tp, 2 * k + half + 1)
                    fn(xT[:, half * HALF:(half + 1) * HALF], bank(BANK_M0 + half), ACT.Copy).then_inc(ln_xT, 1)

            act.wait_ge(ld_a, 48)
            for dst, c in ((identb, C_ID), (trib, C_TRI), (causS, C_CS), (causT, C_CT)):
                fn(dst[:], con[:, c:c + P], ACT.Copy).then_inc(tables, 1)
            act.wait_ge(lam_sum, 1)
            fn(lams[:, 2:4], lams[:, 0:2], ACT.Exp).then_inc(lam_exp, 1)
            for g in range(2):
                act.wait_ge(A.vps, g + 1)
                fn(vall[:, 2 * g:2 * g + 2, :], bank(g).rearrange("p (a b) -> p a b", a=2), ACT.Copy).then_inc(A.vall, 1)
            for n in range(2):
                parts_hi_mid(A, n, rope[:, 2 * n, :])
            for g in range(2, 4):
                act.wait_ge(A.vps, g + 1)
                fn(vall[:, 2 * g:2 * g + 2, :], bank(g).rearrange("p (a b) -> p a b", a=2), ACT.Copy).then_inc(A.vall, 1)
            for n in range(2):
                part_mid(A, n, rope[:, 2 * n + 1, :])
            for half in range(2):
                act.wait_ge(bkv, half + 1)
                fn(kTB[:, half, :], bank(4 + half)[:, 0:480], ACT.Identity, bias=bkB[:, 0:1]).then_inc(bkvc, 1)
            act.wait_ge(fixed, 9)
            for half in range(2):
                act.wait_ge(bkv, 2 + half + 1)
                fn(vB[0:L, 4 * half:4 * half + 4, 0:P], tiles(bank(6 + half)[0:L, :], 4, P), ACT.Copy).then_inc(bkvc, 1)
            for n in range(2, 4):
                parts_hi_mid(A, n, rope[:, 2 * n, :])
            for n in range(2, 4):
                part_mid(A, n, rope[:, 2 * n + 1, :])
            heads(A, NH)
            finish(A, 2)
            feature_copies(0)

            act.wait_ge(b_mt, 1)
            fn(mT[0:PARTS * B, 0, :], maxima_bank[0:PARTS * B, :], ACT.Copy).then_inc(b_mc, 1)
            for half in range(2):
                act.wait_ge(b_st, half + 1)
                fn(probs[0:L, 0, 4 * half:4 * half + 4, :], tiles(bank(BANK_S + half)[0:L, :], 4, P), ACT.Exp).then_inc(b_exp, 1)
            feature_copies(1)

            act.wait_ge(f_sub, 1)
            fn(sm[:, 1, 0:64], sm[:, 0, 0:64], ACT.Exp).then_inc(f_exp, 1)
            fn(xpart[:, 0, :, :], xres[:], ACT.Copy).then_inc(f_hi, 1)
            for half in range(2):
                act.wait_ge(f_srow, half + 1)
                fn(slotrow[:, half * HALF:(half + 1) * HALF], bank(BANK_T + half), ACT.Copy).then_inc(f_srowc, 1)
            act.wait_ge(f_rest, 1)
            fn(xpart[:, 1, :, :], racc[:], ACT.Copy).then_inc(f_mid, 1)
            act.wait_ge(f_xin, 1)
            for half in range(2):
                fn(xin[:, half * HALF:(half + 1) * HALF], bank(BANK_O + half), ACT.Copy).then_inc(f_xinc, 1)
            for e in range(E0):
                act.wait_ge(f_up, e + 1)
                if e >= 2:
                    act.wait_ge(f_dn, e - 1)
                fn(hid0[:, e % 2, :], bank(BANK_S + e % 2), ACT.Gelu_apprx_tanh).then_inc(f_gelu, 1)
            for half in range(2):
                act.wait_ge(f_dn, 4 * half + 4)
                fn(epart[:, 0, 4 * half:4 * half + 4, :], tiles(bank(BANK_M0 + half), 4, P), ACT.Copy).then_inc(f_ehi, 1)
            for half in range(2):
                act.wait_ge(f_erest, half + 1)
                fn(epart[:, 1, 4 * half:4 * half + 4, :], eout[:, 4 * half:4 * half + 4, :], ACT.Copy).then_inc(f_emid, 1)
            feature_copies(2)

            for n in range(2):
                parts_hi_mid(D, n, rope[:, 2 * n, :])
            for n in range(2):
                part_mid(D, n, rope[:, 2 * n + 1, :])
            heads(D, PAIRS)
            finish(D, 1)
            feature_copies(3)

            def copies(n, slot):
                for half in range(2):
                    act.wait_ge(e_q, n * 2 + half + 1)
                    for j in range(2):
                        fn(qz[64 * j:64 * j + 64, slot, 4 * half:4 * half + 4, j, :],
                           tiles(bank(BANK_M0 + half)[64 * j:64 * j + 64, :], 4, P), ACT.Copy, scale=XD ** -0.5
                           ).then_inc(e_qc, 1)
                for half in range(2):
                    act.wait_ge(e_k, n * 2 + half + 1)
                    fn(kE[:, slot, half * 480:(half + 1) * 480], bank(BANK_M0 + half)[:, 0:480], ACT.Copy).then_inc(e_kc, 1)
                for half in range(2):
                    act.wait_ge(e_v, n * 2 + half + 1)
                    fn(vE[:, slot, 4 * half:4 * half + 4, :, 0:XD],
                       bank(BANK_M0 + half)[0:L, :].rearrange("p (b j n) -> p b j n", b=4, j=2), ACT.Copy).then_inc(e_vc, 1)

            def pair_exps(n, slot):
                for g in range(4):
                    act.wait_ge(e_st, n * 4 + g + 1)
                    if g == 0 and not early(n, 2):
                        act.wait_ge(e_pv, 3 * (n - 1))
                    fn(probs[0:L, slot, 4 * g:4 * g + 4, :], tiles(bank(BANK_T + g % 2)[0:L, :], 4, P),
                       ACT.Exp).then_inc(e_exp, 1)

            def pair_outputs(n):
                for half in range(2):
                    act.wait_ge(e_tp, n * 2 + half + 1)
                    fn(otall[:, bass.ds(n, 1), half * HALF:(half + 1) * HALF].rearrange("p a b -> p (a b)"),
                       bank(BANK_T + half), ACT.Copy).then_inc(e_oc, 1)

            def pair_maxima(n, slot, turn):
                act.wait_ge(e_mt, n + 1)
                if not early(n, 2):
                    act.wait_ge(e_mrow[slot], turn * 16)
                fn(mT[:, slot, :], maxima_bank[0:PARTS * 16, :], ACT.Copy).then_inc(e_mc, 1)

            def pair_step(n, slot, turn, last=False):
                if not last:
                    if not early(n, 1):
                        act.wait_ge(e_pv, 3 * n)
                    copies(n + 1, 1 - slot)
                if not early(n, 1):
                    pair_outputs(n - 1)
                pair_exps(n, slot)
                if not last:
                    pair_maxima(n + 1, 1 - slot, turn + slot - 1)

            act.wait_ge(e_zero, 3)
            copies(0, 0)
            pair_maxima(0, 0, None)
            pair_step(0, 0, 1)
            pair_step(1, 1, 1)
            with act.Fori(1, PAIRS // 2 - 1) as i:
                for u in range(2):
                    pair_step(i * 2 + u, u, i + 1)
            pair_step(PAIRS - 2, 0, PAIRS // 2)
            pair_step(PAIRS - 1, 1, PAIRS // 2, last=True)
            pair_outputs(PAIRS - 1)
            feature_copies(4)

            act.wait_ge(g_sub, 1)
            fn(sm[:, 1, :], sm[:, 0, :], ACT.Exp).then_inc(g_exp, 1)
            for half in range(2):
                act.wait_ge(g_ct, half + 1)
                fn(oT[0:E1, 4 * half:4 * half + 4, 0, :], tiles(bank(BANK_O + half)[0:E1, :], 4, P), ACT.Copy).then_inc(g_ctc, 1)

            def gelus(e, slot, first=False):
                for f in range(F1):
                    for half in range(2):
                        u = 2 * f + half
                        act.wait_ge(g_up, e * 4 + u + 1)
                        if u == 0 and not first:
                            act.wait_ge(g_dn, e * 2 - 2)
                        fn(hid1[:, slot, f, half * HALF:(half + 1) * HALF], bank(BANK_S + u), ACT.Gelu,
                           bias=b1s[:, slot, f:f + 1]).then_inc(g_gelu, 1)

            for e in range(2):
                act.wait_ge(g_w1[e], 32)
                gelus(e, e, first=True)
            with act.Fori(1, E1 // 2) as i:
                for u in range(2):
                    act.wait_ge(g_w1[u], (i + 1) * 32)
                    gelus(i * 2 + u, u)

        @block.vector
        def _(dve):
            dch = Chain(dve, dchain)
            tt, ts, stt = nc.vector.tensor_tensor, nc.vector.tensor_scalar, nc.vector.scalar_tensor_tensor

            def link(ins):
                dch(ins)
                dch.wait()

            def split_maxima(src, parts, width):
                link(nc.vector.tensor_copy(parts[:, 0, :], src))
                link(tt(mres[:, 0:width], src, parts[:, 0, :], ALU.subtract))
                link(nc.vector.tensor_copy(parts[:, 1, :], mres[:, 0:width]))
                return tt(parts[:, 2, :], mres[:, 0:width], parts[:, 1, :], ALU.subtract)

            SPLIT = 3

            def heads(a, count, finish_head, links):
                def maxima(n, slot, g):
                    dve.wait_ge(a.s, 4 * n + g + 1)
                    nc.vector.tensor_reduce(negm[:, slot % 2, 4 * g:4 * g + 4], tiles(bank(BANK_S + g % 2), 4, P),
                                            AX.X, ALU.max, negate=True).then_inc(a.max, 1)

                def split(n, slot):
                    dve.wait_ge(a.max, 4 * n + 4)
                    if not early(n, 2):
                        dve.wait_ge(a.mt, n - 1)
                    split_maxima(negm[:, slot % 2, :], mparts[:, slot % 2], 16).then_inc(a.msplit, 1)

                def step(n, slot):
                    ahead = (slot + 2) % RING
                    if not late_head(n + 2, count):
                        maxima(n + 2, ahead, 0)
                        maxima(n + 2, ahead, 1)
                    if not early(n, 2):
                        finish_head(n - 2)
                    if not late_head(n + 2, count):
                        maxima(n + 2, ahead, 2)
                        maxima(n + 2, ahead, 3)
                        split(n + 2, ahead)

                for h in range(2):
                    for g in range(4):
                        maxima(h, h, g)
                    split(h, h)
                for n in range(RING):
                    step(n, n)
                if count > 2 * RING:
                    with dve.Fori(1, count // RING - 1) as i:
                        dch.enter(i, 1, RING * (SPLIT + links))
                        for u in range(RING):
                            step(i * RING + u, u)
                        dch.leave(count // RING - 2)
                for n in range(count - RING, count + 2):
                    step(n, n % RING)

            def finish_a(n):
                o = bank(BANK_M1).rearrange("p (c b w) -> p c b w", c=2, w=32)
                dve.wait_ge(A.to, n + 1)
                link(nc.vector.reciprocal(rz[:].rearrange("p (c b) -> p c b", c=2), o[:, :, :, 16]))
                link(ts(rz[:, B:2 * B], rz[:, B:2 * B], lams[:, 5:6], None, ALU.mult))
                dch(tt(ot1[:], o[:, 0, :, 0:16], along(rz[:, 0:B], 16), ALU.mult))
                link(tt(ot2[:], o[:, 1, :, 0:16], along(rz[:, B:2 * B], 16), ALU.mult))
                tt(oall[:, :, bass.ds(n * 16, 16)], ot1[:], ot2[:], ALU.add).then_inc(A.norm, 1)

            def finish_d(n):
                o = bank(BANK_M1).rearrange("p (c b w) -> p c b w", c=2, w=32)
                dve.wait_ge(D.to, n + 1)
                link(nc.vector.reciprocal(rz[:].rearrange("p (c b) -> p c b", c=2), o[:, :, :, 8]))
                dch(tt(oall[:, :, bass.ds(n * 16, 8)], o[:, 0, :, 0:8], along(rz[:, 0:B], 8), ALU.mult))
                tt(oall[:, :, bass.ds(n * 16 + 8, 8)], o[:, 1, :, 0:8], along(rz[:, B:2 * B], 8), ALU.mult).then_inc(D.norm, 1)

            def layernorm(k, half):
                s = range(4 * half, 4 * half + 4)
                for b in s:
                    dch(nc.vector.bn_stats(bst[:, b, :], racc[:, b, :]))
                dch.wait()
                for b in s:
                    last = nc.vector.bn_aggr(mv[:, b, :], bst[:, b, :])
                    if b < s[-1]:
                        dch(last)
                last.then_inc(ln_var, 1)
                dve.wait_ge(ln_rstd, 2 * k + half + 1)
                for b in s:
                    last = ts(xres[:, b, :], racc[:, b, :], mv[:, b, 0:1], rstd[:, b:b + 1], ALU.subtract, ALU.mult)
                    if b < s[-1]:
                        dch(last)
                last.then_inc(ln_out, 1)

            def half_of(ap, half):
                return ap[:, 4 * half:4 * half + 4, :]

            dve.wait_ge(ld_b, 16 * 7)
            link(tt(lamin[:, 0:2, :], lamin[:, 0:2, :], lamin[:, 2:4, :], ALU.mult))
            nc.vector.tensor_reduce(lams[:, 0:2], lamin[:, 0:2, :], AX.X, ALU.add).then_inc(lam_sum, 1)
            dve.wait_ge(ld_a, 48)

            def rotary(n, t0, cos, sin):
                mine, other = (t0, t0 + 2) if n % 2 == 0 else (t0 + 2, t0)
                for k, (at, table) in enumerate(((mine, cos), (other, sin))):
                    last = tt(rope[:, 2 * n + k, :].rearrange("p (a b) -> p a b", b=P),
                              bank(at, 2).rearrange("p (a b) -> p a b", b=P), over(con[:, table:table + P], B), ALU.mult)
                    if k == 0:
                        dch(last)
                last.then_inc(A.mul, 1)

            def rest_part(a, n):
                dve.wait_ge(a.hi, n + 1)
                tt(rope[:, 2 * n + 1, :], rope[:, 2 * n, :], part[:, n, 0, :], ALU.subtract).then_inc(a.rest, 1)

            def low_part(a, n):
                dve.wait_ge(a.mid, n + 1)
                tt(part[:, n, 2, :], rope[:, 2 * n + 1, :], part[:, n, 1, :], ALU.subtract).then_inc(a.lo, 1)

            for n in range(4):
                dve.wait_ge(A.qk, 2 if n < 2 else 4)
                rotary(n, 0 if n < 2 else 4, *((C_COSQ, C_SINQ) if n < 2 else (C_COSK, C_SINK)))
            dve.wait_ge(lam_exp, 1)
            link(tt(lams[:, 4:5], lams[:, 3:4], lams[:, 2:3], ALU.subtract))
            link(ts(lams[:, 5:6], lams[:, 4:5], -(0.8 - 0.6), None, ALU.add))
            for pair in ((0, 1), (2, 3)):
                for n in pair:
                    rest_part(A, n)
                for n in pair:
                    low_part(A, n)
            heads(A, NH, finish_a, 4)
            for half in range(2):
                dve.wait_ge(A.y, half + 1)
                link(tt(half_of(racc, half), tiles(bank(BANK_O + half), 4, P), half_of(xres, half), ALU.add))
                layernorm(0, half)

            for half in range(2):
                dve.wait_ge(b_q, half + 1)
                ts(qB[:, 4 * half:4 * half + 4, :], tiles(bank(BANK_S + half), 4, P), bqB[:, 0:1], float(P) ** -0.5,
                   ALU.add, ALU.mult).then_inc(b_qc, 1)
            for half in range(2):
                dve.wait_ge(b_s, half + 1)
                nc.vector.tensor_reduce(negm[:, 0, 4 * half:4 * half + 4], tiles(bank(BANK_T + half), 4, L), AX.X, ALU.max,
                                        negate=True).then_inc(b_max, 1)
            dve.wait_ge(b_max, 2)
            split_maxima(negm[:, 0, 0:B], bparts.rearrange("p (a b) -> p a b", a=PARTS), B).then_inc(b_msplit, 1)
            dve.wait_ge(resb, 1)
            for g, (lo, hi) in enumerate(((0, 3), (3, 6), (6, 8))):
                o = tiles(bank((BANK_T, BANK_T + 1, BANK_O + 1)[g]), hi - lo, 129)
                dve.wait_ge(b_pv, g + 1)
                link(nc.vector.reciprocal(rz[:, lo:hi], o[:, :, P]))
                for b in range(lo, hi):
                    dch(stt(racc[:, b, :], o[:, b - lo, 0:P], rz[:, b:b + 1], xres[:, b, :], ALU.mult, ALU.add))
                if g == 1:
                    dch.wait()
                    layernorm(1, 0)
            dch.wait()
            layernorm(1, 1)

            def by_token(n):
                return sm[:, n, 0:B * E0].rearrange("p (b e) -> p b e", e=E0)

            def by_expert(ap):
                return ap.rearrange("p (e b) -> p b e", b=B)

            logits = tiles(bank(BANK_S), B, E0)
            dve.wait_ge(f_log, 1)
            link(nc.vector.tensor_reduce(sm[:, 5, 0:B], logits, AX.X, ALU.max))
            tt(by_token(0), logits, along(sm[:, 5, 0:B], E0), ALU.subtract).then_inc(f_sub, 1)
            link(tt(by_token(2), logits, along(sm[:, 5, 0:B], E0), ALU.is_equal))
            link(nc.vector.tensor_tensor_scan(sm[:, 3, 0:64], con[:, C_R8:C_R8 + 64], sm[:, 2, 0:64], 0.0, ALU.mult, ALU.add))
            link(stt(by_expert(sm[:, 4, 0:64]), by_token(3), 1.0, by_token(2), ALU.is_equal, ALU.mult))
            link(nc.vector.tensor_tensor_scan(sm[:, 7, 0:64], con[:, C_R8:C_R8 + 64], sm[:, 4, 0:64], 0.0, ALU.mult, ALU.add))
            nc.vector.tensor_copy(smb[:, 0, :], sm[:, 4, 0:64]).then_inc(f_one, 1)
            tt(smb[:, 1, :], sm[:, 7, 0:64], sm[:, 4, 0:64], ALU.subtract).then_inc(f_one, 1)
            dve.wait_ge(f_exp, 1)
            link(nc.vector.tensor_reduce(sm[:, 6, 0:B], by_token(1), AX.X, ALU.add))
            link(nc.vector.reciprocal(sm[:, 6, 0:B], sm[:, 6, 0:B]))
            dve.wait_ge(f_cnt, 1)
            count = bank(BANK_S + 1)[:, 0:64]
            link(tt(sm[:, 7, 0:64], count, sm[:, 4, 0:64], ALU.mult))
            link(nc.vector.tensor_reduce(sm[:, 8, 0:B], by_expert(sm[:, 7, 0:64]), AX.X, ALU.add))
            link(ts(sm[:, 10, 0:B], sm[:, 8, 0:B], float(P), None, ALU.is_le))
            link(tt(sm[:, 7, 0:64], sm[:, 4, 0:64], con[:, C_EOFF:C_EOFF + 64], ALU.mult))
            link(nc.vector.tensor_reduce(sm[:, 9, 0:B], by_expert(sm[:, 7, 0:64]), AX.X, ALU.add))
            link(tt(sm[:, 9, 0:B], sm[:, 9, 0:B], sm[:, 8, 0:B], ALU.add))
            link(tt(sm[:, 9, 0:B], sm[:, 9, 0:B], sm[:, 10, 0:B], ALU.mult))
            ts(sm[:, 9, 0:B], sm[:, 9, 0:B], -1.0, None, ALU.add).then_inc(f_slot, 1)
            dve.wait_ge(f_hi, 1)
            tt(racc[:], xres[:], xpart[:, 0, :, :], ALU.subtract).then_inc(f_rest, 1)
            dve.wait_ge(f_mid, 1)
            tt(xpart[:, 2, :, :], racc[:], xpart[:, 1, :, :], ALU.subtract).then_inc(f_part, 1)
            dve.wait_ge(f_slot, 1)
            for b in range(B):
                ts(sel[:, b, :], con[:, C_IOTA:C_IOTA + T], sm[:, 9, b:b + 1], None, ALU.is_equal).then_inc(f_sel, 1)
            dve.wait_ge(f_srowc, 2)
            for e in range(E0):
                ts(selT[:, e, :], slotrow[:], con[:, C_SLOT + e:C_SLOT + e + 1], None, ALU.is_equal).then_inc(f_selT, 1)
            for half in range(2):
                dve.wait_ge(f_ehi, half + 1)
                tt(half_of(eout, half), tiles(bank(BANK_M0 + half), 4, P), epart[:, 0, 4 * half:4 * half + 4, :],
                   ALU.subtract).then_inc(f_erest, 1)
            for half in range(2):
                dve.wait_ge(f_emid, half + 1)
                tt(epart[:, 2, 4 * half:4 * half + 4, :], half_of(eout, half), epart[:, 1, 4 * half:4 * half + 4, :],
                   ALU.subtract).then_inc(f_epart, 1)
            for half in range(2):
                dve.wait_ge(f_y, half + 1)
                for k in range(4):
                    b = 4 * half + k
                    last = stt(racc[:, b, :], bank(BANK_O + half)[:, k * P:(k + 1) * P], sm[:, 6, b:b + 1], xres[:, b, :],
                               ALU.mult, ALU.add)
                    if k < 3:
                        dch(last)
                last.then_inc(f_r, 1)
                dve.wait_ge(f_r, half + 1)
                layernorm(2, half)

            dve.wait_ge(ld_d, 16 * 10)
            for n in range(2):
                dve.wait_ge(D.qk, n + 1)
                ts(rope[:, 2 * n, :], bank(2 + 2 * n, 2), bqkD[:, n:n + 1], HD ** -0.5 if n == 0 else 1.0,
                   ALU.add, ALU.mult).then_inc(D.mul, 1)
                dve.wait_ge(D.mul, n + 1)
                nc.vector.tensor_copy(lams[:, 6:7], lams[:, 5:6]).then_inc(D.full, 1)
            for half in range(2):
                dve.wait_ge(D.vps, half + 1)
                tt(vall[:, 4 * half:4 * half + 4, 0:P], tiles(bank(6 + half), 4, P), over(bvD[:], 4), ALU.add).then_inc(D.vall, 1)
            rest_part(D, 0)
            rest_part(D, 1)
            low_part(D, 0)
            low_part(D, 1)
            heads(D, PAIRS, finish_d, 2)
            dve.wait_ge(resb, 2)
            for half in range(2):
                dve.wait_ge(D.y, half + 1)
                link(tt(half_of(racc, half), tiles(bank(BANK_O + half), 4, P), half_of(xres, half), ALU.add))
                layernorm(3, half)

            def pair_maxima(n, slot):
                for g in range(4):
                    dve.wait_ge(e_s, n * 4 + g + 1)
                    nc.vector.tensor_reduce(negm[:, slot, 4 * g:4 * g + 4], tiles(bank(BANK_S + g % 2), 4, L), AX.X, ALU.max,
                                            negate=True).then_inc(e_max, 1)
                dve.wait_ge(e_max, n * 4 + 4)
                if not early(n, 2):
                    dve.wait_ge(e_mt, n - 1)
                split_maxima(negm[:, slot, :], mparts[:, slot], 16).then_inc(e_msplit, 1)

            def pair_norm(n):
                for g, (lo, hi, at) in enumerate(OUT_TILES):
                    o = tiles(bank(at), hi - lo, XD + 1)
                    dve.wait_ge(e_pv, 3 * n + g + 1)
                    link(nc.vector.reciprocal(rz[:, lo:hi], o[:, :, XD]))
                    if g == 0 and not early(n, 1):
                        dve.wait_ge(e_tp, 2 * n)
                    tt(outE[:, lo:hi, :], o[:, :, 0:XD], along(rz[:, lo:hi], XD), ALU.mult).then_inc(e_norm, 1)

            def pair_step(n, slot):
                if not early(n, 1):
                    pair_norm(n - 1)
                pair_maxima(n + 1, 1 - slot)

            pair_maxima(0, 0)
            pair_step(0, 0)
            pair_step(1, 1)
            with dve.Fori(1, PAIRS // 2 - 1) as i:
                dch.enter(i, 1, 2 * (SPLIT + 3))
                for u in range(2):
                    pair_step(i * 2 + u, u)
                dch.leave(PAIRS // 2 - 2)
            pair_step(PAIRS - 2, 0)
            pair_norm(PAIRS - 2)
            pair_norm(PAIRS - 1)
            dve.wait_ge(resb, 3)
            for half in range(2):
                dve.wait_ge(e_y, half + 1)
                link(tt(half_of(racc, half), tiles(bank(BANK_O + half), 4, P), half_of(xres, half), ALU.add))
                layernorm(4, half)

            def b16(n):
                return sm[:, n, :].rearrange("p (b e) -> p b e", e=E1)

            dve.wait_ge(g_log, 1)
            link(tt(b16(5), tiles(bank(BANK_S), B, E1), over(rb1[:], B), ALU.add))
            top = sm[:, 9, 0:B * 8].rearrange("p (b k) -> p b k", k=8)
            for b in range(B):
                dch(nc.vector.max(top[:, b, :], b16(5)[:, b, :]))
            dch.wait()
            tt(b16(0), b16(5), top[:, :, 0:1].to_broadcast([P, B, E1]), ALU.subtract).then_inc(g_sub, 1)
            fourth = top[:, :, TOPK - 1:TOPK].to_broadcast([P, B, E1])
            dch(tt(b16(2), b16(5), fourth, ALU.is_gt))
            link(tt(b16(3), b16(5), fourth, ALU.is_equal))
            dch(nc.vector.tensor_reduce(sm[:, 6, 0:B], b16(2), AX.X, ALU.add))
            link(nc.vector.tensor_tensor_scan(sm[:, 4, :], con[:, C_R16:C_R16 + B * E1], sm[:, 3, :], 0.0, ALU.mult, ALU.add))
            link(ts(sm[:, 6, 0:B], sm[:, 6, 0:B], -1.0, float(TOPK), ALU.mult, ALU.add))
            link(tt(b16(4), b16(4), along(sm[:, 6, 0:B], E1), ALU.is_le))
            link(tt(b16(3), b16(3), b16(4), ALU.mult))
            link(tt(b16(7), b16(2), b16(3), ALU.add))
            dve.wait_ge(g_exp, 1)
            link(tt(b16(7), b16(7), b16(1), ALU.mult))
            link(nc.vector.tensor_reduce(sm[:, 8, 0:B], b16(7), AX.X, ALU.add))
            link(nc.vector.reciprocal(sm[:, 8, 0:B], sm[:, 8, 0:B]))
            tt(b16(11), b16(7), along(sm[:, 8, 0:B], E1), ALU.mult).then_inc(g_c, 1)
            for half in range(2):
                dve.wait_ge(g_b2, half + 1)
                tt(half_of(racc, half), tiles(bank(BANK_O + half), 4, P), half_of(xres, half), ALU.add).then_inc(g_acc, 1)

            def accumulate(e, slot):
                banks = (BANK_M0, BANK_O)[slot]
                for half in range(2):
                    dve.wait_ge(g_dn, e * 2 + half + 1)
                    dve.wait_ge(g_acc, e * 2 + half + 1)
                    for k in range(4):
                        b = 4 * half + k
                        last = stt(racc[:, b, :], bank(banks + half)[:, k * P:(k + 1) * P],
                                   sm[:, 11, bass.ds(b * E1 + e, 1)], racc[:, b, :], ALU.mult, ALU.add)
                        if k < 3:
                            dch(last)
                    last.then_inc(g_acc, 1)

            accumulate(0, 0)
            accumulate(1, 1)
            with dve.Fori(1, E1 // 2) as i:
                dch.enter(i, 1, 12)
                for u in range(2):
                    accumulate(i * 2 + u, u)
                dch.leave(E1 // 2 - 1)
            for half in range(2):
                dve.wait_ge(g_acc, 2 * E1 + half + 1)
                dch.wait()
                layernorm(5, half)


def kernel(**inputs):
    import concourse.bacc as bacc
    from concourse.bass_utils import run_bass_kernel_spmd

    a = {k: np.asarray(v) for k, v in inputs.items()}
    wqkv0 = a["L0_attn_W_qkv"]
    w1 = a["L1_attn_Wqkv"]
    bq1 = a["L1_attn_bqkv"]

    def pair_order(w):
        n = w.shape[1]
        return w.reshape(PAIRS, 2, n, HD).transpose(2, 0, 3, 1).reshape(n, P)

    wkv = a["L1_xattn_w_kv"]
    arrays = {
        "con": constant_table(),
        "xT": a["x"].reshape(T, P).T,
        "x": a["x"].transpose(1, 0, 2),
        "ctxT": a["ctx_768"].reshape(B * L, CD).T,
        "wqk0": wqkv0[:4 * P].reshape(4, P, P).transpose(2, 0, 1),
        "wv0": wqkv0[4 * P:].reshape(2, NH, HD, P).transpose(3, 1, 0, 2).reshape(P, 2 * P),
        "wproj0": a["L0_attn_W_proj"].reshape(P, 2, P).transpose(2, 1, 0),
        "lq1": a["L0_attn_lambda_q1"].reshape(1, HD), "lq2": a["L0_attn_lambda_q2"].reshape(1, HD),
        "lk1": a["L0_attn_lambda_k1"].reshape(1, HD), "lk2": a["L0_attn_lambda_k2"].reshape(1, HD),
        "wqB": a["L0_xattn_Wq"], "wkB": a["L0_xattn_Wk"], "wvB": a["L0_xattn_Wv"],
        "bqB": a["L0_xattn_bq"].reshape(P, 1), "bkB": a["L0_xattn_bk"].reshape(P, 1), "bvB": a["L0_xattn_bv"].reshape(1, P),
        "rw0": a["L0_ffn_router_w"],
        "w1a": a["L0_ffn_w1"].transpose(1, 0, 2),
        "w2a": a["L0_ffn_w2"].reshape(E0, F0, P, P).transpose(2, 0, 1, 3),
        "wqkD": np.stack([pair_order(w1[:, :, 0:HD]), pair_order(w1[:, :, HD:2 * HD])], 1),
        "wvD": w1[:, :, 2 * HD:].transpose(1, 0, 2).reshape(P, P),
        "bqkD": np.stack([pair_order(bq1[:, None, 0:HD])[0], pair_order(bq1[:, None, HD:2 * HD])[0]], 1),
        "bvD": bq1[:, 2 * HD:].reshape(1, P),
        "woD": a["L1_attn_Wout"], "boD": a["L1_attn_bout"].reshape(1, P),
        "wqE": a["L1_xattn_w_q"], "wkE": wkv[:, :NH * XD], "wvE": wkv[:, NH * XD:],
        "woE": a["L1_xattn_w_out"].reshape(PAIRS, P, P).transpose(1, 0, 2), "boE": a["L1_xattn_b_out"].reshape(1, P),
        "rw1": a["L1_ffn_router_w"], "rb1": a["L1_ffn_router_b"].reshape(1, E1), "b2s": a["L1_ffn_b2"],
        "w1b": a["L1_ffn_w1"], "b1": a["L1_ffn_b1"].reshape(E1, F1, P).transpose(0, 2, 1),
        "w2b": a["L1_ffn_w2"].reshape(E1, F1, P, P).transpose(0, 2, 1, 3),
    }
    nc = bacc.Bacc("TRN2", target_bir_lowering=False, num_devices=1)
    feed, d = {}, {}
    for name, v in arrays.items():
        v = np.ascontiguousarray(v)
        feed[f"in_{name}"] = v
        d[name] = nc.dram_tensor(f"in_{name}", v.shape, mybir.dt.from_np(v.dtype), kind="ExternalInput").ap()
    out = nc.dram_tensor("out", (P, B, P), F32, kind="ExternalOutput").ap()
    decoder_kernel(nc, d, out)
    r = run_bass_kernel_spmd(nc, [feed], core_ids=[0])
    return r.results[0]["out"].transpose(1, 0, 2)
```

```python
from contextlib import ExitStack

import numpy as np

import concourse.bass as bass
from concourse import mybir

F32 = mybir.dt.float32
BF16 = mybir.dt.bfloat16
ALU = mybir.AluOpType
ACT = mybir.ActivationFunctionType
AX = mybir.AxisListType

P = 128
B = 8
T = B * P
HALF = T // 2
L = 120
CD = 96
NH = 16
HD = 8
XD = 64
PAIRS = NH // 2
E0 = 8
F0 = 512 // P
E1 = 16
TOPK = 4
F1 = 256 // P
PARTS = 3
ROWS = PARTS * PARTS * HD
MROW = 96
EPS = 1e-5
RING = 4
BIG = -1e30
BANK_M0, BANK_M1, BANK_S, BANK_T, BANK_O = 0, 1, 2, 4, 6
BANK_PART = (BANK_M0, BANK_M1, BANK_O, BANK_O + 1)

C_ID, C_TRI, C_COSQ, C_SINQ, C_COSK, C_SINK, C_CS, C_CT = (P * n for n in range(8))
C_IOTA = 8 * P
C_R8 = C_IOTA + T
C_R16 = C_R8 + B * E0
C_EOFF = C_R16 + B * E1
C_SLOT = C_EOFF + B * E0
C_ALL = C_SLOT + E0


def constant_table():
    t = np.zeros((P, C_ALL), np.float32)
    n = np.arange(P)
    t[:, C_ID:C_ID + P] = np.eye(P)
    t[:, C_TRI:C_TRI + P] = n[:, None] <= n[None, :]
    inv = (1.0 / np.float32(10000.0) ** (np.arange(0, 2 * HD, 2, dtype=np.float32) / np.float32(2 * HD)))
    angle = (n.astype(np.float32)[None, :] * inv.astype(np.float32)[:, None]).astype(np.float32)
    cos, sin = np.tile(np.cos(angle), (NH, 1)), np.tile(np.sin(angle), (NH, 1))
    scale = HD ** -0.5
    t[:, C_COSQ:C_COSQ + P], t[:, C_SINQ:C_SINQ + P] = cos * scale, sin * scale
    t[:, C_COSK:C_COSK + P], t[:, C_SINK:C_SINK + P] = cos, sin
    t[:, C_CS:C_CS + P] = np.where(n[None, :] > n[:, None], BIG, 0.0)
    t[:, C_CT:C_CT + P] = np.where(n[:, None] > n[None, :], BIG, 0.0)
    t[:, C_IOTA:C_IOTA + T] = np.arange(T)[None, :]
    t[:, C_R8:C_R8 + B * E0] = (np.arange(B * E0) % 8 != 0)[None, :]
    t[:, C_R16:C_R16 + B * E1] = (np.arange(B * E1) % E1 != 0)[None, :]
    t[:, C_EOFF:C_EOFF + B * E0] = (np.arange(B * E0) // B * P)[None, :]
    t[:, C_SLOT:C_SLOT + E0] = np.arange(E0)[None, :] * P + n[:, None]
    return t


class Chain:

    def __init__(self, eng, sem):
        self.eng, self.sem, self.n = eng, sem, 0

    def __call__(self, ins):
        ins.then_inc(self.sem, 1)
        self.n = self.n + 1

    def wait(self):
        self.eng.wait_ge(self.sem, self.n)

    def enter(self, i, first, stride):
        self.entered, self.stride = self.n, stride
        self.n = (i - first) * stride + self.entered

    def leave(self, times):
        self.n = self.entered + times * self.stride


def decoder_kernel(nc, d, out):
    with ExitStack() as ctx:
        def sb(name, shape, dt=F32):
            return ctx.enter_context(nc.sbuf_tensor(name, shape, dt))

        def sem(name):
            return ctx.enter_context(nc.semaphore(name))

        ps = ctx.enter_context(nc.psum_tensor("ps", [P, 8, 512], F32))
        con = sb("con", [P, C_ALL])
        identb, trib, onesb, causS, causT = (sb(n, [P, P], BF16) for n in ("identb", "trib", "onesb", "causS", "causT"))
        one = sb("one", [P, 1])
        xres = sb("xres", [P, B, P])
        racc = sb("racc", [P, B, P])
        xT = sb("xT", [P, T])
        ctxT = sb("ctxT", [CD, B * L])
        wqk0 = sb("wqk0", [P, 4, P])
        wv0 = sb("wv0", [P, 2 * P])
        wproj0 = sb("wproj0", [P, 2, P])
        lamin = sb("lamin", [P, 4, HD])
        lams = sb("lams", [P, 8])
        wqB, wkB, wvB = sb("wqB", [P, P]), sb("wkB", [CD, P]), sb("wvB", [CD, P])
        bqB, bkB, bvB = sb("bqB", [P, 1]), sb("bkB", [P, 1]), sb("bvB", [P, P])
        rw0 = sb("rw0", [P, E0])
        w1a = sb("w1a", [P, E0, F0 * P])
        w2a = sb("w2a", [P, E0, F0, P])
        before = w2a[:].rearrange("p e f n -> p (e f n)")
        kTB = before[:, 0:960].rearrange("p (a b) -> p a b", a=2)
        vB = before[:, 1024:1024 + B * 132].rearrange("p (b n) -> p b n", b=B)
        wqkD, wvD, woD = sb("wqkD", [P, 2, P]), sb("wvD", [P, P]), sb("woD", [P, P])
        bqkD, bvD, boD = sb("bqkD", [P, 2]), sb("bvD", [P, P]), sb("boD", [P, P])
        boE = sb("boE", [P, P])
        rw1, rb1, b2s = sb("rw1", [P, E1]), sb("rb1", [P, E1]), sb("b2s", [E1, P])
        stq, stk = sb("stq", [P, 2, 2, T], BF16), sb("stk", [P, 2, 2, T], BF16)
        late = w1a[:].rearrange("p e f -> p (e f)").bitcast(BF16).rearrange("p (k s c t) -> p k s c t", k=2, s=2, c=2)
        queries_of = [stq[:, 0], stq[:, 1], late[:, 0, 0], late[:, 0, 1]]
        keys_of = [stk[:, 0], stk[:, 1], late[:, 1, 0], late[:, 1, 1]]
        probs = sb("probs", [P, 2, 16, P])
        outT = sb("outT", [P, 512])
        vall = sb("vall", [P, B, 2 * P])
        vs = sb("vs", [P, 2, 2, B, 32])
        oall = sb("oall", [P, B, 2 * P])
        oT = sb("oT", [P, B, 2, P])
        negm = sb("negm", [P, 2, 16])
        mparts = sb("mparts", [P, 2, PARTS, 16], BF16)
        mres, zero = sb("mres", [P, 16]), sb("zero", [P, 16])
        mT = sb("mT", [PARTS * 16, 2, P], BF16)
        rz = sb("rz", [P, 16])
        rzE = sb("rzE", [P, 2, 16])
        ot = sb("ot", [P, 2, 2 * B, 16])
        bst, mv = sb("bst", [P, B, 6]), sb("mv", [P, B, 2])
        rstd, mhalf = sb("rstd", [P, B]), sb("mhalf", [P, B])
        sm = sb("sm", [P, 12, 128])
        smb = sb("smb", [P, 2, B * E0], BF16)
        arena = sb("arena", [P, 14976])

        def area(at, *shape, dt=F32, rows=P):
            n = int(np.prod(shape)) * (2 if dt == BF16 else 4) // 4
            a = arena[0:rows, at:at + n]
            if dt == BF16:
                a = a.bitcast(BF16)
            names = "abcd"[:len(shape)]
            return a.rearrange(f"p ({' '.join(names)}) -> p {' '.join(names)}",
                               **dict(zip(names[1:], shape[1:]))) if len(shape) > 1 else a

        rope = area(0, 8, T)
        part = area(8192, 4, PARTS, T, dt=BF16)
        sel = area(0, B, T, dt=BF16)
        selT = area(4096, E0, T, dt=BF16)
        xpart = area(8192, PARTS, B, P, dt=BF16)
        epart = area(9728, PARTS, E0, P, dt=BF16)
        xin = area(11264, T)
        hid0 = area(12288, 2, 512)
        eout = area(13312, E0, P)
        slotrow = probs[:, 0, 0:8, :].rearrange("p a b -> p (a b)")
        qB = area(0, B, P)
        otall = area(0, PAIRS, T)
        qz = area(8192, 2, B, 2, P)
        kE = area(12288, 2, B * L)
        wE = area(14208, 2, 3, P)
        vE = w1a[0:L].rearrange("p e f -> p (e f)")[:, 0:2 * T].rearrange("p (s b n) -> p s b n", s=2, b=B)
        ptE = w2a[0:L].rearrange("p e f n -> p (e f n)").rearrange("p (s t n) -> p s t n", s=2, t=16)
        hid1 = area(0, 2, F1, T)
        free = w1a[:].rearrange("p e f -> p (e f)")[:, 2 * T:]
        w1s = free[:, 0:512].rearrange("p (s n) -> p s n", s=2)
        w2s = free[:, 512:1024].rearrange("p (s f n) -> p s f n", s=2, f=F1)
        b1s = free[:, 1024:1028].rearrange("p (s f) -> p s f", s=2)

        ROW = 2 * T
        HEAD = PARTS * HD * ROW
        stackA = nc.dram_tensor("stackA", [2 * NH * HEAD], BF16, kind="Internal")
        stackD = nc.dram_tensor("stackD", [2 * PAIRS * HEAD], BF16, kind="Internal")

        ident = con[:, C_ID:C_ID + P]
        fill = onesb[:].unsqueeze(1).to_broadcast([P, 4, P])

        def bank(n, k=1):
            return ps[:, n, :] if k == 1 else ps[:, n:n + k, :].rearrange("p a b -> p (a b)")

        def tiles(ap, n, w):
            return ap[:, 0:n * w].rearrange("p (a b) -> p a b", b=w)

        maxima_bank = bank(BANK_M0)[:, 0:P]

        def over(ap, n):
            return ap.unsqueeze(1).to_broadcast([ap.shape[0], n, ap.shape[1]])

        def half_of(ap, half):
            return ap[:, 4 * half:4 * half + 4, :]

        def early(n, k):
            return isinstance(n, int) and n < k

        def late_head(n, count):
            return isinstance(n, int) and n >= count

        def along(ap, n):
            return ap.unsqueeze(2).to_broadcast([ap.shape[0], ap.shape[1], n])

        ld_a, ld_h, ld_b, ld_c, ld_l, ld_x, ld_r, ld_f, ld_d = (sem(f"ld_{n}") for n in "ahbclxrfd")
        zeros = sem("zeros")
        fixed = sem("fixed")
        tables = sem("tables")
        dchain, achain, pchain = sem("dchain"), sem("achain"), sem("pchain")

        stack, mrow_in = ([sem(f"{n}{k}") for k in range(RING)] for n in ("stack", "mrow_in"))

        class Heads:

            def __init__(self, n, turns):
                self.qk = sem(n + "_qk")
                self.mul = sem(n + "_mul")
                self.full = sem(n + "_full")
                self.hi, self.mid, self.lo = sem(n + "_hi"), sem(n + "_mid"), sem(n + "_lo")
                self.rest = sem(n + "_rest")
                self.kept = sem(n + "_kept")
                self.vps, self.vall = sem(n + "_vps"), sem(n + "_vall")
                self.stack, self.mrow, self.turns = stack, mrow_in, turns
                self.s = sem(n + "_s")
                self.max = sem(n + "_max")
                self.msplit = sem(n + "_msplit")
                self.mt = sem(n + "_mt")
                self.mc = sem(n + "_mc")
                self.st = sem(n + "_st")
                self.exp = sem(n + "_exp")
                self.vs = sem(n + "_vs")
                self.pv = sem(n + "_pv")
                self.ot = sem(n + "_ot")
                self.to = sem(n + "_to")
                self.div = sem(n + "_div")
                self.norm = sem(n + "_norm") if turns == 0 else self.div
                self.post = sem(n + "_post")
                self.postc = sem(n + "_postc")
                self.y = sem(n + "_y")

        A, D = Heads("a", 0), Heads("d", NH // RING)
        ln_var, ln_rstd, ln_out, ln_tp, ln_xT = (sem("ln_" + n) for n in ("var", "rstd", "out", "tp", "xT"))
        resb = sem("resb")
        bkv, bkvc = sem("b_kv"), sem("b_kvc")
        b_q, b_qc, b_s, b_max, b_sub, b_exp, b_pt, b_ptc, b_pv = (
            sem("b_" + n) for n in ("q", "qc", "s", "max", "sub", "exp", "pt", "ptc", "pv"))
        lam_sum, lam_exp, lam_done = sem("lam_sum"), sem("lam_exp"), sem("lam_done")
        f_log, f_sub, f_exp, f_one, f_cnt, f_slot, f_srow, f_srowc, f_sel, f_selT, f_hi, f_rest, f_mid, f_part = (
            sem("f_" + n) for n in ("log", "sub", "exp", "one", "cnt", "slot", "srow", "srowc", "sel", "selT", "hi",
                                    "rest", "mid", "part"))
        f_xin, f_xinc, f_up, f_gelu, f_dn, f_ehi, f_erest, f_emid, f_epart, f_y, f_r = (
            sem("f_" + n) for n in ("xin", "xinc", "up", "gelu", "dn", "ehi", "erest", "emid", "epart", "y", "r"))
        e_w = [sem("e_w0"), sem("e_w1")]
        (e_q, e_k, e_v, e_qa, e_qd, e_kc, e_vc, e_s, e_max, e_sub, e_exp, e_rz, e_norm, e_pt, e_ptc, e_pv, e_oc,
         e_zero, e_wo, e_y) = (
            sem("e_" + n) for n in ("q", "k", "v", "qa", "qd", "kc", "vc", "s", "max", "sub", "exp", "rz", "norm", "pt",
                                    "ptc", "pv", "oc", "zero", "wo", "y"))
        woE = oT[:, 0:4, :, :].rearrange("p a b c -> p (a b) c")
        g_w1, g_w2 = ([sem(f"g_{n}_{k}") for k in range(2)] for n in ("w1", "w2"))
        g_log, g_sub, g_exp, g_c, g_ct, g_ctc, g_b2, g_up, g_gelu, g_dn, g_acc, g_out = (
            sem("g_" + n) for n in ("log", "sub", "exp", "c", "ct", "ctc", "b2", "up", "gelu", "dn", "acc", "out"))

        block = ctx.enter_context(nc.Block())

        @block.sync
        def _(sp):
            def load(dst, src, signal):
                sp.dma_start(dst, src).then_inc(signal, 16)

            load(wqk0[:], d["wqk0"], ld_a)
            load(xT[:, 0:HALF], d["xT"][:, 0:HALF], ld_a)
            load(xT[:, HALF:T], d["xT"][:, HALF:T], ld_h)
            load(con[:, 0:C_IOTA], d["con"][:, 0:C_IOTA], ld_c)
            load(wv0[:], d["wv0"], ld_b)
            load(ctxT[:], d["ctxT"], ld_x)
            for dst, n in ((wqB, "wqB"), (wkB, "wkB"), (wvB, "wvB"), (bqB, "bqB"), (bkB, "bkB")):
                load(dst[:], d[n], ld_x)
            load(bvB[:], d["bvB"].to_broadcast([P, P]), ld_x)
            for n, name in enumerate(("lq1", "lq2", "lk1", "lk2")):
                load(lamin[:, n, :], d[name].to_broadcast([P, HD]), ld_l)
            load(xres[:], d["x"], ld_l)
            load(wproj0[:], d["wproj0"], ld_l)
            load(con[:, C_IOTA:C_ALL], d["con"][:, C_IOTA:C_ALL], ld_r)
            load(rw0[:], d["rw0"], ld_r)
            for dst, n in ((wqkD, "wqkD"), (wvD, "wvD"), (woD, "woD"), (bqkD, "bqkD"), (rw1, "rw1"), (b2s, "b2s")):
                load(dst[:], d[n], ld_d)
            for dst, n, w in ((bvD, "bvD", P), (boD, "boD", P), (boE, "boE", P), (rb1, "rb1", E1)):
                load(dst[:], d[n].to_broadcast([P, w]), ld_d)

            def keep(a, n, p, dst):
                sp.wait_ge((a.hi, a.mid, a.lo)[p], n + 1)
                sp.dma_start(dst, part[:, n, p, :]).then_inc(a.kept, 16)

            def load_stacks(a, h, slot, base, count):
                at = h * HEAD
                sp.dma_start(keys_of[slot][0:ROWS], bass.AP(
                    base, at + count * HEAD, [[0, PARTS], [ROW, PARTS * HD], [1, ROW]])).then_inc(a.stack[slot], 16)
                sp.dma_start(queries_of[slot][0:ROWS], bass.AP(
                    base, at, [[ROW, PARTS * HD], [0, PARTS], [1, ROW]])).then_inc(a.stack[slot], 16)

            def move_maxima(a, made, slot):
                sp.wait_ge(a.mc, made)
                sp.dma_start(queries_of[slot][MROW:MROW + PARTS], mT[:, slot % 2, :]).then_inc(a.mrow[slot], 16)

            def heads(a, count, base):
                sp.wait_ge(a.kept, 16 * (12 if count == NH else 6))
                sp.wait_ge(zeros, 3)
                sp.wait_ge(fixed, 3 if count == NH else 11)
                load_stacks(a, 0, 0, base, count)
                load_stacks(a, 1, 1, base, count)
                sp.wait_ge(zeros, 4)
                load_stacks(a, 2, 2, base, count)
                move_maxima(a, 1, 0)
                load_stacks(a, RING - 1, RING - 1, base, count)
                with sp.Fori(0, count // RING - 1) as i:
                    later = [sp.snap(i * RING + (u + RING)) for u in range(RING)]
                    made = [sp.snap(i * RING + (u + 2)) for u in range(RING)]
                    used = [sp.snap(i * (4 * RING) + 4 * (u + 1)) for u in range(RING)]
                    for u in range(RING):
                        move_maxima(a, made[u], (u + 1) % RING)
                        sp.wait_ge(a.st, used[u])
                        load_stacks(a, later[u], u, base, count)
                for u in range(RING - 1):
                    move_maxima(a, count - RING + u + 2, u + 1)

            for n, p in ((0, 0), (1, 0), (0, 1), (2, 0), (1, 1), (0, 2), (3, 0), (2, 1), (1, 2), (3, 1), (2, 2), (3, 2)):
                t, c = divmod(n, 2)
                keep(A, n, p, bass.AP(
                    stackA, t * NH * HEAD + p * HD * ROW + c * T, [[HEAD, NH], [ROW, HD], [1, T]]) if t == 0 else bass.AP(
                    stackA, t * NH * HEAD + p * ROW + c * T, [[PARTS * ROW, NH * HD], [1, T]]))
            heads(A, NH, stackA)
            sp.wait_ge(A.st, 4 * NH)
            load(w1a[:], d["w1a"], ld_f)
            sp.wait_ge(b_pv, 3)
            load(w2a[:], d["w2a"], ld_f)
            for p in range(PARTS):
                for t in range(2):
                    keep(D, t, p, bass.AP(
                        stackD, p * HD * ROW, [[HEAD, PAIRS], [T, 2 * HD], [1, T]]) if t == 0 else bass.AP(
                        stackD, PAIRS * HEAD + p * ROW, [[PARTS * ROW, PAIRS * HD], [T, 2], [1, T]]))
            heads(D, PAIRS, stackD)

            def weights(pair, slot):
                for n, name in enumerate(("wqE", "wkE", "wvE")):
                    rows = P if n == 0 else CD
                    sp.dma_start(wE[0:rows, slot, n, :], d[name][0:rows, bass.ds(pair * P, P)]).then_inc(e_w[slot], 16)

            sp.wait_ge(D.kept, 16 * 6)
            weights(0, 0)
            weights(1, 1)
            sp.wait_ge(D.y, 2)
            sp.dma_start(woE, d["woE"]).then_inc(e_wo, 16)
            with sp.Fori(0, PAIRS // 2 - 1) as i:
                pair = [sp.snap(i * 2 + (u + 2)) for u in range(2)]
                projected = [sp.snap(i * 4 + 2 * (u + 1)) for u in range(2)]
                for u in range(2):
                    sp.wait_ge(e_q, projected[u])
                    sp.wait_ge(e_v, projected[u])
                    weights(pair[u], u)

            def up_weights(e, slot):
                sp.dma_start(w1s[:, slot, :], d["w1b"][bass.ds(e, 1), :, :]).then_inc(g_w1[slot], 16)
                sp.dma_start(b1s[:, slot, :], d["b1"][bass.ds(e, 1), :, :]).then_inc(g_w1[slot], 16)

            def down_weights(e, slot):
                sp.dma_start(w2s[:, slot, :, :], d["w2b"][bass.ds(e, 1), :, :, :]).then_inc(g_w2[slot], 16)

            for e in range(2):
                up_weights(e, e)
                down_weights(e, e)
            with sp.Fori(0, E1 // 2 - 1) as i:
                nxt = [sp.snap(i * 2 + (u + 2)) for u in range(2)]
                done = [sp.snap(i * 8 + 4 * (u + 1)) for u in range(2)]
                used = [sp.snap(i * 4 + 2 * (u + 1)) for u in range(2)]
                for u in range(2):
                    sp.wait_ge(g_gelu, done[u])
                    up_weights(nxt[u], u)
                    sp.wait_ge(g_dn, used[u])
                    down_weights(nxt[u], u)
            for half in range(2):
                sp.wait_ge(ln_out, 2 * 5 + half + 1)
                sp.dma_start(out[:, 4 * half:4 * half + 4, :], xres[:, 4 * half:4 * half + 4, :]).then_inc(g_out, 16)
            sp.wait_ge(g_out, 32)

        @block.gpsimd
        def _(pool):
            for n, (tile, value) in enumerate((
                    (onesb[:], 1.0), (stk[MROW:MROW + PARTS, :, :, :], 1.0), (late[MROW:MROW + PARTS, 1], 1.0),
                     (one[:], 1.0), (mhalf[:], -0.5), (vB[:, :, P:P + 1], 1.0), (vs[:], 0.0),
                    (vs[:, :, :, :, 16:17], 1.0))):
                nc.gpsimd.memset(tile, value).then_inc(fixed, 1)
                pool.wait_ge(fixed, n + 1)
            pch = Chain(pool, pchain)

            for n in range(4):
                pool.wait_ge(A.mul, n + 1)
                op = ALU.subtract if n % 2 == 0 else ALU.add
                nc.gpsimd.tensor_tensor(rope[:, 2 * n, :], rope[:, 2 * n, :], rope[:, 2 * n + 1, :], op).then_inc(A.full, 1)

            def values(a, h, slot, width):
                if width == 16:
                    return nc.gpsimd.tensor_copy(vs[:, slot, 0, :, 0:16], vall[:, :, bass.ds(h * 16, 16)])
                return nc.gpsimd.tensor_copy(
                    vs[:, slot, :, :, 0:8].rearrange("p c b d -> p b c d"),
                    vall[:, :, bass.ds(h * 16, 16)].rearrange("p b (c d) -> p b c d", c=2))

            def split_maxima(a, n, slot):
                pool.wait_ge(a.max, 4 * n + 4)
                if not early(n, 2):
                    pool.wait_ge(a.mt, n - 1)
                m, parts = negm[:, slot, :], mparts[:, slot]
                pch(nc.gpsimd.tensor_tensor(parts[:, 0, :], m, zero[:], ALU.add))
                pch.wait()
                pch(nc.gpsimd.tensor_tensor(mres[:], m, parts[:, 0, :], ALU.subtract))
                pch.wait()
                pch(nc.gpsimd.tensor_tensor(parts[:, 1, :], mres[:], zero[:], ALU.add))
                pch.wait()
                nc.gpsimd.tensor_tensor(parts[:, 2, :], mres[:], parts[:, 1, :], ALU.subtract).then_inc(a.msplit, 1)

            def add_outputs(a, n, slot):
                pool.wait_ge(a.div, n + 1)
                second = ot[:, slot, B:2 * B, :]
                pch(nc.gpsimd.tensor_tensor(second, second, along(lams[:, 5:6].to_broadcast([P, B]), 16), ALU.mult))
                pch.wait()
                nc.gpsimd.tensor_tensor(oall[:, :, bass.ds(n * 16, 16)], ot[:, slot, 0:B, :], second, ALU.add
                                        ).then_inc(a.norm, 1)

            def heads(a, count, width):
                def step(n, slot):
                    if not late_head(n, count):
                        if not early(n, 2):
                            pool.wait_ge(a.pv, n - 1)
                        values(a, n, slot, width).then_inc(a.vs, 1)
                    if a is A and not early(n, 2):
                        add_outputs(a, n - 2, slot)
                    if not late_head(n + 2, count):
                        split_maxima(a, n + 2, slot)

                pool.wait_ge(a.vall, 4 if width == 16 else 2)
                pool.wait_ge(zeros, 1)
                split_maxima(a, 0, 0)
                split_maxima(a, 1, 1)
                step(0, 0)
                step(1, 1)
                with pool.Fori(1, count // 2 - 1) as i:
                    pch.enter(i, 1, 2 * (3 + (a is A)))
                    for u in range(2):
                        step(i * 2 + u, u)
                    pch.leave(count // 2 - 2)
                for n in range(count - 2, count + (2 if a is A else 0)):
                    step(n, n % 2)

            def rsqrt(k, half):
                s = slice(4 * half, 4 * half + 4)
                pool.wait_ge(ln_var, 2 * k + half + 1)
                pch(nc.gpsimd.tensor_scalar(rstd[:, s], mv[:, s, 1], EPS, None, ALU.add))
                pch.wait()
                nc.gpsimd.tensor_tensor(rstd[:, s], rstd[:, s], mhalf[:, s], ALU.pow).then_inc(ln_rstd, 1)

            def add_bias(k, bias):
                pool.wait_ge(ln_xT, 2 * k)
                pool.wait_ge(ln_out, 2 * k)
                nc.gpsimd.tensor_tensor(xres[:], xres[:], over(bias[:], B), ALU.add).then_inc(resb, 1)

            heads(A, NH, 16)
            rsqrt(0, 0)
            rsqrt(0, 1)
            pool.wait_ge(ld_x, 16 * 7)
            add_bias(1, bvB)
            rsqrt(1, 0)
            rsqrt(1, 1)
            pool.wait_ge(A.norm, NH)
            nc.gpsimd.memset(vs[:, :, :, :, 8:9], 1.0).then_inc(fixed, 1)
            pool.wait_ge(f_up, E0)
            pool.wait_ge(fixed, 9)
            nc.gpsimd.memset(w1a[64:MROW], 0.0).then_inc(fixed, 1)
            pool.wait_ge(fixed, 10)
            nc.gpsimd.memset(late[MROW:MROW + PARTS, 1], 1.0).then_inc(fixed, 1)
            pool.wait_ge(fixed, 11)
            rsqrt(2, 0)
            rsqrt(2, 1)
            pool.wait_ge(ld_d, 16 * 10)
            add_bias(3, boD)
            heads(D, PAIRS, 8)
            rsqrt(3, 0)
            rsqrt(3, 1)
            pool.wait_ge(D.lo, 2)
            pool.wait_ge(D.kept, 16 * 6)
            pool.wait_ge(ln_rstd, 8)
            nc.gpsimd.memset(qz[0:64, :, :, 1, :], 0.0).then_inc(e_zero, 1)
            pool.wait_ge(e_zero, 1)
            nc.gpsimd.memset(qz[64:128, :, :, 0, :], 0.0).then_inc(e_zero, 1)
            pool.wait_ge(e_zero, 2)
            add_bias(4, boE)

            def pair_norm(n, slot):
                for g in range(4):
                    pool.wait_ge(e_rz, n * 4 + g + 1)
                    weights = probs[:, slot, 4 * g:4 * g + 4, 0:L]
                    nc.gpsimd.tensor_tensor(weights, weights, along(rzE[:, slot, 4 * g:4 * g + 4], L), ALU.mult
                                            ).then_inc(e_norm, 1)

            with pool.Fori(0, PAIRS // 2) as i:
                for u in range(2):
                    pair_norm(i * 2 + u, u)
            rsqrt(4, 0)
            rsqrt(4, 1)
            rsqrt(5, 0)
            rsqrt(5, 1)

        @block.tensor
        def _(pe):
            mm = nc.tensor.matmul

            def keep_busy(count, at):
                for _ in range(count):
                    mm(bank(at), onesb[:], fill, start=True, stop=True)

            def scores(a, n, slot, g, causal):
                if not early(4 * n + g, 2):
                    pe.wait_ge(a.max, 4 * n + g - 1)
                o = bank(BANK_S + g % 2)
                if causal:
                    mm(tiles(o, 4, P), identb[:], over(causS[:], 4), start=True, stop=False)
                for k in range(4):
                    c, b = divmod(4 * g + k, B)
                    last = mm(o[:, k * P:(k + 1) * P], queries_of[slot][0:MROW, c, b * P:(b + 1) * P],
                              keys_of[slot][0:MROW, c, b * P:(b + 1) * P], start=not causal, stop=not causal or k == 3)
                last.then_inc(a.s, 1)

            def scores_t(a, n, slot, g, causal):
                if not early(4 * n + g, 2):
                    pe.wait_ge(a.exp, 4 * n + g - 1)
                o = bank(BANK_T + g % 2)
                if causal:
                    mm(tiles(o, 4, P), identb[:], over(causT[:], 4), start=True, stop=False)
                for k in range(4):
                    c, b = divmod(4 * g + k, B)
                    last = mm(o[:, k * P:(k + 1) * P], keys_of[slot][0:MROW + PARTS, c, b * P:(b + 1) * P],
                              queries_of[slot][0:MROW + PARTS, c, b * P:(b + 1) * P],
                              start=not causal, stop=not causal or k == 3)
                last.then_inc(a.st, 1)

            def head_maxima(a, n, slot):
                pe.wait_ge(a.msplit, n + 1)
                if not early(n, 1):
                    pe.wait_ge(a.mc, n)
                mm(maxima_bank[0:PARTS * 16, :], mparts[:, slot % 2].rearrange("p a b -> p (a b)"), identb[:],
                   start=True, stop=True).then_inc(a.mt, 1)

            def head_values(a, n, slot, pair, c):
                if c == 0:
                    pe.wait_ge(a.vs, n + 1)
                    pe.wait_ge(a.exp, 4 * n + 4)
                    if not early(n, 2):
                        pe.wait_ge(a.ot, n - 1)
                for b in range(B):
                    col = (c * 2 + b // 4) * P
                    last = mm(bank(BANK_O + slot % 2)[32 * (b % 4):32 * (b % 4) + 32, col:col + P],
                              vs[:, slot % 2, c if pair else 0, b, :], probs[:, slot % 2, c * B + b, :],
                              start=True, stop=True)
                if c == 1:
                    last.then_inc(a.pv, 1)

            def head_token(a, n):
                pe.wait_ge(a.ot, n + 1)
                if not early(n, 1):
                    pe.wait_ge(a.div, n)
                for k in range(4):
                    last = nc.tensor.transpose(bank(BANK_M1)[:, k * P:(k + 1) * P], outT[:, k * P:(k + 1) * P], ident)
                last.then_inc(a.to, 1)

            def heads(a, count, pair, causal):
                def step(n, slot, turn):
                    ahead, second, third, before = ((slot + k) % RING for k in (1, 2, 3, -1))
                    if not late_head(n, count):
                        pe.wait_ge(a.mrow[slot], (a.turns + turn) * 16)
                        scores_t(a, n, slot, 0, causal)
                        scores_t(a, n, slot, 1, causal)
                    if not late_head(n + 2, count):
                        scores(a, n + 2, second, 2, causal)
                    if not late_head(n + 1, count):
                        head_maxima(a, n + 1, ahead)
                    if not early(n, 1):
                        head_values(a, n - 1, before, pair, 0)
                    if not late_head(n + 2, count):
                        scores(a, n + 2, second, 3, causal)
                    if not early(n, 1):
                        head_values(a, n - 1, before, pair, 1)
                    if not late_head(n, count):
                        scores_t(a, n, slot, 2, causal)
                        scores_t(a, n, slot, 3, causal)
                    if not late_head(n + 3, count):
                        pe.wait_ge(a.stack[third], (a.turns + turn + (slot + 3) // RING) * 32)
                        scores(a, n + 3, third, 0, causal)
                        scores(a, n + 3, third, 1, causal)
                    if not early(n, 1):
                        head_token(a, n - 1)

                for h in range(2):
                    pe.wait_ge(a.stack[h], (a.turns + 1) * 32)
                    for g in range(4):
                        scores(a, h, h, g, causal)
                        if h == 1 and g == 1:
                            head_maxima(a, 0, 0)
                pe.wait_ge(a.stack[2], (a.turns + 1) * 32)
                scores(a, 2, 2, 0, causal)
                scores(a, 2, 2, 1, causal)
                for n in range(RING):
                    step(n, n, 1)
                if count > 2 * RING:
                    with pe.Fori(1, count // RING - 1) as i:
                        for u in range(RING):
                            step(i * RING + u, u, i + 1)
                for n in range(count - RING, count + 1):
                    step(n, n % RING, n // RING + 1)

            def finish(a, chunks, w):
                keep_busy(5, BANK_T)
                pe.wait_ge(a.norm, NH if chunks == 2 else PAIRS)
                per = 4 // chunks
                banks = (BANK_S, BANK_S + 1, BANK_T, BANK_T + 1)
                for g in range(B // per):
                    for k in range(per):
                        for c in range(chunks):
                            o = bank(banks[g])[:, (k * chunks + c) * P:(k * chunks + c + 1) * P]
                            last = nc.tensor.transpose(o, oall[:, g * per + k, c * P:(c + 1) * P], ident)
                    last.then_inc(a.post, 1)
                for half in range(2):
                    pe.wait_ge(a.postc, (half + 1) * B // per // 2)
                    for k in range(4):
                        b = 4 * half + k
                        for c in range(chunks):
                            last = mm(bank(BANK_O + half)[:, k * P:(k + 1) * P], oT[:, b, c, :],
                                      w[:, c, :] if chunks == 2 else w[:],
                                      start=c == 0, stop=c == chunks - 1)
                    last.then_inc(a.y, 1)

            def to_feature_half(k, half):
                pe.wait_ge(ln_out, 2 * k + half + 1)
                for j in range(4):
                    last = nc.tensor.transpose(bank(BANK_M0 + half)[:, j * P:(j + 1) * P], xres[:, 4 * half + j, :], ident)
                last.then_inc(ln_tp, 1)

            def to_feature(k):
                for half in range(2):
                    to_feature_half(k, half)

            pe.wait_ge(fixed, 1)
            keep_busy(9, BANK_M0)
            pe.wait_ge(ld_a, 32)
            for t in range(4):
                for half in range(2):
                    if t == 0 and half == 1:
                        pe.wait_ge(ld_h, 16)
                    last = mm(bank(2 * t + half), wqk0[:, t, :], xT[:, half * HALF:(half + 1) * HALF],
                              start=True, stop=True)
                last.then_inc(A.qk, 1)
            pe.wait_ge(ld_b, 16)
            pe.wait_ge(A.mul, 2)
            for g in range(4):
                for k in range(2):
                    b = 2 * g + k
                    last = mm(bank(g)[:, k * 256:(k + 1) * 256], xT[:, b * P:(b + 1) * P], wv0[:], start=True, stop=True)
                last.then_inc(A.vps, 1)
            pe.wait_ge(ld_x, 16 * 7)
            pe.wait_ge(A.mul, 4)
            for half in range(2):
                mm(bank(4 + half)[:, 0:480], wkB[:], ctxT[:, half * 480:(half + 1) * 480],
                   start=True, stop=True).then_inc(bkv, 1)
            for half in range(2):
                for k in range(4):
                    b = 4 * half + k
                    last = mm(bank(6 + half)[0:L, k * P:(k + 1) * P], ctxT[:, b * L:(b + 1) * L], wvB[:],
                              start=True, stop=True)
                last.then_inc(bkv, 1)
            pe.wait_ge(A.vall, 4)
            pe.wait_ge(fixed, 8)
            keep_busy(26, BANK_M0)
            pe.wait_ge(bkvc, 4)
            pe.wait_ge(fixed, 8)
            pe.wait_ge(tables, 4)
            heads(A, NH, pair=False, causal=False)
            finish(A, 2, wproj0)
            keep_busy(10, BANK_T)
            to_feature(0)

            for half in range(2):
                pe.wait_ge(ln_xT, half + 1)
                mm(bank(BANK_S + half), wqB[:], xT[:, half * HALF:(half + 1) * HALF], start=True, stop=True).then_inc(b_q, 1)
            kb = before[:, 0:960]
            for half in range(2):
                pe.wait_ge(b_qc, half + 1)
                for k in range(4):
                    b = 4 * half + k
                    last = mm(bank(BANK_T + half)[:, k * L:(k + 1) * L], qB[:, b, :], kb[:, b * L:(b + 1) * L],
                              start=True, stop=True)
                last.then_inc(b_s, 1)
            for half in range(2):
                pe.wait_ge(b_exp, half + 1)
                for k in range(4):
                    last = nc.tensor.transpose(bank(BANK_S + half)[0:L, k * P:(k + 1) * P], probs[:, 0, 4 * half + k, 0:L],
                                               ident)
                last.then_inc(b_pt, 1)
            for g, (lo, hi) in enumerate(((0, 3), (3, 6), (6, 8))):
                o = bank((BANK_T, BANK_T + 1, BANK_O + 1)[g])
                pe.wait_ge(b_ptc, 1 if hi <= 4 else 2)
                for b in range(lo, hi):
                    last = mm(o[:, (b - lo) * 129:(b - lo + 1) * 129], probs[0:L, 1, b, :], vB[0:L, b, 0:129],
                              start=True, stop=True)
                last.then_inc(b_pv, 1)
            keep_busy(10, BANK_M1)
            to_feature(1)

            pe.wait_ge(ld_r, 16 * 2)
            for b in range(B):
                pe.wait_ge(ln_xT, 2 + b // 4 + 1)
                last = mm(bank(BANK_S)[:, b * E0:(b + 1) * E0], xT[:, b * P:(b + 1) * P], rw0[:], start=True, stop=True)
            last.then_inc(f_log, 1)
            keep_busy(4, BANK_M0)
            pe.wait_ge(f_one, 2)
            mm(bank(BANK_S + 1)[:, 0:B * E0], trib[:], smb[:, 0, :], start=True, stop=False)
            mm(bank(BANK_S + 1)[:, 0:B * E0], onesb[:], smb[:, 1, :], start=False, stop=True).then_inc(f_cnt, 1)
            pe.wait_ge(f_slot, 1)
            keep_busy(5, BANK_M0)
            pe.wait_ge(f_part, 2)
            pe.wait_ge(f_mid, 2)
            pe.wait_ge(f_hi, 2)
            for b in range(B):
                pe.wait_ge(f_sel, b + 1)
                for half in range(2):
                    for p in range(PARTS):
                        last = mm(bank(BANK_O + half), xpart[:, p, b, :], sel[:, b, half * HALF:(half + 1) * HALF],
                                  start=b == 0 and p == 0, stop=b == B - 1 and p == PARTS - 1)
                if b == B - 1:
                    last.then_inc(f_xin, 1)
            for b in range(B):
                last = mm(bank(BANK_T + b // 4)[:, b % 4 * P:(b % 4 + 1) * P],
                          sm[:, 9, b:b + 1].to_broadcast([P, P]), ident, start=True, stop=True)
                if b % 4 == 3:
                    last.then_inc(f_srow, 1)
            pe.wait_ge(ld_f, 16 * 2)
            for e in range(E0 + 1):
                if e < E0:
                    pe.wait_ge(f_xinc, e // 4 + 1)
                    if e >= 2:
                        pe.wait_ge(f_gelu, e - 1)
                    for f in range(F0):
                        last = mm(bank(BANK_S + e % 2)[:, f * P:(f + 1) * P], w1a[:, e, f * P:(f + 1) * P],
                                  xin[:, e * P:(e + 1) * P], start=True, stop=True)
                    last.then_inc(f_up, 1)
                if e > 0:
                    x = e - 1
                    pe.wait_ge(f_gelu, x + 1)
                    for f in range(F0):
                        last = mm(bank(BANK_PART[x // 2])[:, x % 2 * P:(x % 2 + 1) * P], hid0[:, x % 2, f * P:(f + 1) * P],
                                  w2a[:, x, f, :], start=f == 0, stop=f == F0 - 1)
                    last.then_inc(f_dn, 1)
            pe.wait_ge(f_selT, E0)
            for b in range(B):
                o = bank(BANK_T + b // 4)[:, b % 4 * P:(b % 4 + 1) * P]
                for e in range(E0):
                    if b == 0 and e % 2 == 0:
                        pe.wait_ge(f_epart, e // 2 + 1)
                    for p in range(PARTS):
                        last = mm(o, selT[:, e, b * P:(b + 1) * P], epart[:, p, e, :],
                                  start=e == 0 and p == 0, stop=e == E0 - 1 and p == PARTS - 1)
                if b % 4 == 3:
                    last.then_inc(f_y, 1)
            keep_busy(10, BANK_S)
            to_feature(2)

            pe.wait_ge(f_r, 2)
            for t in range(2):
                for half in range(2):
                    pe.wait_ge(ln_xT, 4 + half + 1)
                    last = mm(bank(2 + 2 * t + half), wqkD[:, t, :], xT[:, half * HALF:(half + 1) * HALF],
                              start=True, stop=True)
                last.then_inc(D.qk, 1)
            for half in range(2):
                for k in range(4):
                    b = 4 * half + k
                    last = mm(bank(6 + half)[:, k * P:(k + 1) * P], xT[:, b * P:(b + 1) * P], wvD[:], start=True, stop=True)
                last.then_inc(D.vps, 1)
            keep_busy(40, BANK_M0)
            pe.wait_ge(D.vall, 2)
            pe.wait_ge(D.full, 2)
            heads(D, PAIRS, pair=True, causal=True)
            finish(D, 1, woD)

            def project_queries(n, slot):
                if not early(n, 1):
                    pe.wait_ge(e_vc, n * 2)
                for half in range(2):
                    mm(bank(BANK_M0 + half), wE[:, slot, 0, :], xT[:, half * HALF:(half + 1) * HALF],
                       start=True, stop=True).then_inc(e_q, 1)

            def project_keys(n, slot):
                for half in range(2):
                    if not early(n, 1):
                        pe.wait_ge(e_qa, n * 2 + half + 1)
                        pe.wait_ge(e_qd, n * 2 + half + 1)
                    mm(bank(BANK_M0 + half)[:, 0:480], wE[0:CD, slot, 1, :], ctxT[:, half * 480:(half + 1) * 480],
                       start=True, stop=True).then_inc(e_k, 1)

            def project_values(n, slot):
                for half in range(2):
                    pe.wait_ge(e_kc, n * 2 + half + 1)
                    for k in range(4):
                        b = 4 * half + k
                        last = mm(bank(BANK_M0 + half)[0:L, k * P:(k + 1) * P], ctxT[:, b * L:(b + 1) * L],
                                  wE[0:CD, slot, 2, :], start=True, stop=True)
                    last.then_inc(e_v, 1)

            def pair_scores(n, slot, g):
                pe.wait_ge(e_kc, n * 2 + (2 if g >= 2 else 1))
                if not early(4 * n + g, 2):
                    pe.wait_ge(e_sub, n * 4 + g - 1)
                for k in range(4):
                    b, j = 2 * g + k // 2, k % 2
                    last = mm(bank(BANK_S + g % 2)[:, k * L:(k + 1) * L], qz[:, slot, b, j, :],
                              kE[:, slot, b * L:(b + 1) * L], start=True, stop=True)
                last.then_inc(e_s, 1)

            def pair_weights(n, slot, g):
                pe.wait_ge(e_norm, n * 4 + g + 1)
                if not early(4 * n + g, 2):
                    pe.wait_ge(e_ptc, n * 4 + g - 1)
                for k in range(4):
                    last = nc.tensor.transpose(bank(BANK_T + g % 2)[0:L, k * P:(k + 1) * P],
                                               probs[:, slot, 4 * g + k, 0:L], ident)
                last.then_inc(e_pt, 1)

            def pair_values(n, slot):
                pe.wait_ge(e_vc, n * 2 + 2)
                for half in range(2):
                    pe.wait_ge(e_ptc, n * 4 + 2 * half + 2)
                    if not early(n, 1):
                        pe.wait_ge(e_oc, n * 2 + half - 1)
                    for b in range(4 * half, 4 * half + 4):
                        for j in range(2):
                            last = mm(bank(BANK_O + half)[64 * j:64 * j + 64, b % 4 * P:(b % 4 + 1) * P],
                                      vE[:, slot, b, 64 * j:64 * j + 64], ptE[:, slot, 2 * b + j, :], start=True, stop=True)
                    last.then_inc(e_pv, 1)

            def pair_step(n, slot, turn, last=False):
                if last:
                    for g in range(4):
                        pair_weights(n, slot, g)
                else:
                    pe.wait_ge(e_w[1 - slot], (turn + slot) * 48)
                    project_queries(n + 1, 1 - slot)
                    project_keys(n + 1, 1 - slot)
                    pair_scores(n + 1, 1 - slot, 0)
                    pair_scores(n + 1, 1 - slot, 1)
                    project_values(n + 1, 1 - slot)
                    pair_scores(n + 1, 1 - slot, 2)
                    pair_weights(n, slot, 0)
                    pair_scores(n + 1, 1 - slot, 3)
                    pair_weights(n, slot, 1)
                    pair_weights(n, slot, 2)
                    pair_weights(n, slot, 3)
                pair_values(n, slot)

            pe.wait_ge(e_w[0], 48)
            project_keys(0, 0)
            project_values(0, 0)
            pe.wait_ge(e_vc, 2)
            to_feature(3)
            pe.wait_ge(ln_xT, 8)
            project_queries(0, 0)
            pe.wait_ge(e_qa, 2)
            pe.wait_ge(e_qd, 2)
            for g in range(4):
                pair_scores(0, 0, g)
            pair_step(0, 0, 1)
            pair_step(1, 1, 1)
            with pe.Fori(1, PAIRS // 2 - 1) as i:
                for u in range(2):
                    pair_step(i * 2 + u, u, i + 1)
            pair_step(PAIRS - 2, 0, PAIRS // 2)
            pair_step(PAIRS - 1, 1, PAIRS // 2, last=True)
            pe.wait_ge(e_oc, 2 * PAIRS)
            pe.wait_ge(e_wo, 16)
            for half in range(2):
                for k in range(4):
                    b = 4 * half + k
                    for p in range(PAIRS):
                        last = mm(bank(BANK_O + half)[:, k * P:(k + 1) * P], otall[:, p, b * P:(b + 1) * P], woE[:, p, :],
                                  start=p == 0, stop=p == PAIRS - 1)
                last.then_inc(e_y, 1)

            def up_half(e, slot, turn, half):
                pe.wait_ge(g_w1[slot], turn * 32)
                for f in range(F1):
                    u = F1 * half + f
                    if not early(e, 1):
                        pe.wait_ge(g_gelu, e * 4 + u - 3)
                    mm(bank(BANK_S + u), w1s[:, slot, f * P:(f + 1) * P], xT[:, half * HALF:(half + 1) * HALF],
                       start=True, stop=True).then_inc(g_up, 1)

            def up(e, slot, turn):
                for half in range(2):
                    up_half(e, slot, turn, half)

            def down(e, slot, turn, first=False):
                banks = (BANK_M0, BANK_O)[slot]
                pe.wait_ge(g_w2[slot], turn * 16)
                for half in range(2):
                    pe.wait_ge(g_gelu, e * 4 + 2 * half + 2)
                    if not first:
                        pe.wait_ge(g_acc, e * 2 + half - 1)
                    for k in range(4):
                        b = 4 * half + k
                        for f in range(F1):
                            last = mm(bank(banks + half)[:, k * P:(k + 1) * P], hid1[:, slot, f, b * P:(b + 1) * P],
                                      w2s[:, slot, f, :], start=f == 0, stop=f == F1 - 1)
                    last.then_inc(g_dn, 1)

            keep_busy(10, BANK_T)
            for half in range(2):
                to_feature_half(4, half)
                pe.wait_ge(ln_xT, 8 + half + 1)
                up_half(0, 0, 1, half)
            for b in range(B):
                last = mm(bank(BANK_O)[:, b * E1:(b + 1) * E1], xT[:, b * P:(b + 1) * P], rw1[:], start=True, stop=True)
            last.then_inc(g_log, 1)
            down(0, 0, 1, first=True)
            up(1, 1, 1)
            pe.wait_ge(g_c, 1)
            for half in range(2):
                for k in range(4):
                    b = 4 * half + k
                    last = nc.tensor.transpose(bank(BANK_O + half)[0:E1, k * P:(k + 1) * P], sm[:, 11, b * E1:(b + 1) * E1],
                                               ident)
                last.then_inc(g_ct, 1)
            up(2, 0, 2)
            pe.wait_ge(g_ctc, 2)
            for half in range(2):
                for k in range(4):
                    b = 4 * half + k
                    last = mm(bank(BANK_O + half)[:, k * P:(k + 1) * P], oT[0:E1, b, 0, :], b2s[:], start=True, stop=True)
                last.then_inc(g_b2, 1)
            pe.wait_ge(g_acc, 2)
            down(1, 1, 1, first=True)
            with pe.Fori(1, E1 // 2 - 1) as i:
                for u in range(2):
                    up(i * 2 + u + 1, 1 - u, i + 1 + u)
                    down(i * 2 + u, u, i + 1)
            up(E1 - 1, 1, E1 // 2)
            down(E1 - 2, 0, E1 // 2)
            down(E1 - 1, 1, E1 // 2)

        @block.scalar
        def _(act):
            ach = Chain(act, achain)

            def fn(o, i, f, **kw):
                return nc.scalar.activation(o, i, f, **kw)

            def part_hi(a, n, src):
                act.wait_ge(a.full, n + 1)
                fn(part[:, n, 0, :], src, ACT.Copy).then_inc(a.hi, 1)

            def part_mid(a, n, src):
                act.wait_ge(a.rest, n + 1)
                fn(part[:, n, 1, :], src, ACT.Copy).then_inc(a.mid, 1)

            def heads(a, count):
                def exponentials(n, slot, g):
                    act.wait_ge(a.st, 4 * n + g + 1)
                    if g == 0 and not early(n, 2):
                        act.wait_ge(a.pv, n - 1)
                    fn(probs[:, slot % 2, 4 * g:4 * g + 4, :], tiles(bank(BANK_T + g % 2), 4, P), ACT.Exp).then_inc(a.exp, 1)

                def copy_maxima(n, slot, moved):
                    act.wait_ge(a.mt, n + 1)
                    if not early(n, 2):
                        act.wait_ge(a.mrow[(slot - 2) % RING], (a.turns + moved) * 16)
                    fn(mT[:, slot % 2, :], maxima_bank[0:PARTS * 16, :], ACT.Copy).then_inc(a.mc, 1)

                def copy_outputs(n, slot):
                    act.wait_ge(a.pv, n + 1)
                    if not early(n, 1):
                        act.wait_ge(a.to, n)
                    fn(outT[:], bank(BANK_O + slot % 2), ACT.Copy).then_inc(a.ot, 1)

                def step(n, slot, turn):
                    if not late_head(n, count):
                        exponentials(n, slot, 0)
                    if not late_head(n + 1, count):
                        copy_maxima(n + 1, (slot + 1) % RING, turn if slot > 0 else turn - 1)
                    if not late_head(n, count):
                        exponentials(n, slot, 1)
                    if not early(n, 1):
                        copy_outputs(n - 1, (slot - 1) % RING)
                    if not late_head(n, count):
                        exponentials(n, slot, 2)
                        exponentials(n, slot, 3)

                copy_maxima(0, 0, None)
                for n in range(RING):
                    step(n, n, 1)
                if count > 2 * RING:
                    with act.Fori(1, count // RING - 1) as i:
                        for u in range(RING):
                            step(i * RING + u, u, i + 1)
                for n in range(count - RING, count + 1):
                    step(n, n % RING, n // RING + 1)

            def finish(a, chunks):
                per = 4 // chunks
                banks = (BANK_S, BANK_S + 1, BANK_T, BANK_T + 1)
                for g in range(B // per):
                    act.wait_ge(a.post, g + 1)
                    o = oT[:, g * per:(g + 1) * per, 0:chunks, :]
                    fn(o, bank(banks[g]).rearrange("p (a b c) -> p a b c", b=chunks, c=P), ACT.Copy).then_inc(a.postc, 1)

            def feature_copy(k, half):
                act.wait_ge(ln_tp, 2 * k + half + 1)
                fn(xT[:, half * HALF:(half + 1) * HALF], bank(BANK_M0 + half), ACT.Copy).then_inc(ln_xT, 1)

            def feature_copies(k):
                for half in range(2):
                    feature_copy(k, half)

            def table_of(f):
                ach(fn(lams[:, 7:8], one[:], f))
                ach.wait()

            act.wait_ge(ld_c, 16)
            for dst, c in ((identb, C_ID), (trib, C_TRI), (causS, C_CS), (causT, C_CT)):
                fn(dst[:], con[:, c:c + P], ACT.Copy).then_inc(tables, 1)
            def values(g):
                act.wait_ge(A.vps, g + 1)
                fn(vall[:, 2 * g:2 * g + 2, :], bank(g).rearrange("p (a b) -> p a b", a=2), ACT.Copy).then_inc(A.vall, 1)

            part_hi(A, 0, rope[:, 0, :])
            part_hi(A, 1, rope[:, 2, :])
            part_mid(A, 0, rope[:, 1, :])
            values(0)
            values(1)
            part_hi(A, 2, rope[:, 4, :])
            part_mid(A, 1, rope[:, 3, :])
            part_hi(A, 3, rope[:, 6, :])
            part_mid(A, 2, rope[:, 5, :])
            part_mid(A, 3, rope[:, 7, :])
            values(2)
            values(3)
            for half in range(2):
                act.wait_ge(bkv, half + 1)
                fn(kTB[:, half, :], bank(4 + half)[:, 0:480], ACT.Identity, bias=bkB[:, 0:1]).then_inc(bkvc, 1)
            act.wait_ge(fixed, 6)
            for half in range(2):
                act.wait_ge(bkv, 2 + half + 1)
                fn(vB[0:L, 4 * half:4 * half + 4, 0:P], tiles(bank(6 + half)[0:L, :], 4, P), ACT.Copy).then_inc(bkvc, 1)
            act.wait_ge(lam_sum, 1)
            fn(lams[:, 2:4], lams[:, 0:2], ACT.Exp).then_inc(lam_exp, 1)
            heads(A, NH)
            finish(A, 2)
            feature_copies(0)

            for half in range(2):
                act.wait_ge(b_sub, half + 1)
                tile = probs[:, 0, 4 * half:4 * half + 4, 0:L]
                fn(tile, tile, ACT.Exp).then_inc(b_exp, 1)
            for half in range(2):
                act.wait_ge(b_pt, half + 1)
                fn(probs[0:L, 1, 4 * half:4 * half + 4, :], tiles(bank(BANK_S + half)[0:L, :], 4, P), ACT.Copy).then_inc(b_ptc, 1)
            for half in range(2):
                act.wait_ge(ln_out, 2 + half + 1)
                fn(half_of(xpart[:, 0], half), half_of(xres, half), ACT.Copy).then_inc(f_hi, 1)
                feature_copy(1, half)
            for half in range(2):
                act.wait_ge(f_rest, half + 1)
                fn(half_of(xpart[:, 1], half), half_of(racc, half), ACT.Copy).then_inc(f_mid, 1)

            act.wait_ge(f_sub, 1)
            fn(sm[:, 1, 0:64], sm[:, 0, 0:64], ACT.Exp).then_inc(f_exp, 1)
            table_of(ACT.Gelu_apprx_tanh)
            act.wait_ge(f_xin, 1)
            for half in range(2):
                fn(xin[:, half * HALF:(half + 1) * HALF], bank(BANK_O + half), ACT.Copy).then_inc(f_xinc, 1)
            for half in range(2):
                act.wait_ge(f_srow, half + 1)
                fn(slotrow[:, half * HALF:(half + 1) * HALF], bank(BANK_T + half), ACT.Copy).then_inc(f_srowc, 1)

            def hi_part(q):
                act.wait_ge(f_dn, 2 * q + 2)
                fn(epart[:, 0, 2 * q:2 * q + 2, :], tiles(bank(BANK_PART[q]), 2, P), ACT.Copy).then_inc(f_ehi, 1)

            def mid_part(q):
                act.wait_ge(f_erest, q + 1)
                fn(epart[:, 1, 2 * q:2 * q + 2, :], eout[:, 2 * q:2 * q + 2, :], ACT.Copy).then_inc(f_emid, 1)

            for e in range(E0):
                act.wait_ge(f_up, e + 1)
                if e >= 2:
                    act.wait_ge(f_dn, e - 1)
                fn(hid0[:, e % 2, :], bank(BANK_S + e % 2), ACT.Gelu_apprx_tanh).then_inc(f_gelu, 1)
                if e in (3, 5, 7):
                    hi_part((e - 3) // 2)
                if e in (4, 6):
                    mid_part((e - 4) // 2)
            mid_part(2)
            hi_part(3)
            mid_part(3)
            table_of(ACT.Exp)
            feature_copies(2)

            for n in range(2):
                part_hi(D, n, rope[:, 2 * n, :])
            for n in range(2):
                part_mid(D, n, rope[:, 2 * n + 1, :])
            heads(D, PAIRS)
            finish(D, 1)

            def copy_queries(n, slot):
                for half in range(2):
                    act.wait_ge(e_q, n * 2 + half + 1)
                    fn(qz[0:64, slot, 4 * half:4 * half + 4, 0, :], tiles(bank(BANK_M0 + half)[0:64, :], 4, P),
                       ACT.Copy, scale=XD ** -0.5).then_inc(e_qa, 1)

            def copy_keys_values(n, slot):
                for half in range(2):
                    act.wait_ge(e_k, n * 2 + half + 1)
                    fn(kE[:, slot, half * 480:(half + 1) * 480], bank(BANK_M0 + half)[:, 0:480], ACT.Copy).then_inc(e_kc, 1)
                for half in range(2):
                    act.wait_ge(e_v, n * 2 + half + 1)
                    fn(vE[:, slot, 4 * half:4 * half + 4, :], tiles(bank(BANK_M0 + half)[0:L, :], 4, P),
                       ACT.Copy).then_inc(e_vc, 1)

            def copies(n, slot):
                copy_queries(n, slot)
                copy_keys_values(n, slot)

            def pair_exps(n, slot, g):
                act.wait_ge(e_sub, n * 4 + g + 1)
                tile = probs[:, slot, 4 * g:4 * g + 4, 0:L]
                fn(tile, tile, ACT.Exp).then_inc(e_exp, 1)

            def pair_weights(n, slot, g):
                act.wait_ge(e_pt, n * 4 + g + 1)
                if g == 0 and not early(n, 2):
                    act.wait_ge(e_pv, 2 * (n - 1))
                fn(ptE[:, slot, 4 * g:4 * g + 4, :], tiles(bank(BANK_T + g % 2)[0:L, :], 4, P), ACT.Copy).then_inc(e_ptc, 1)

            def pair_outputs(n):
                for half in range(2):
                    act.wait_ge(e_pv, n * 2 + half + 1)
                    fn(otall[:, bass.ds(n, 1), half * HALF:(half + 1) * HALF].rearrange("p a b -> p (a b)"),
                       bank(BANK_O + half), ACT.Copy).then_inc(e_oc, 1)

            def pair_step(n, slot, last=False):
                if last:
                    for g in range(4):
                        pair_weights(n, slot, g)
                else:
                    if not early(n, 1):
                        act.wait_ge(e_pv, 2 * n)
                    copies(n + 1, 1 - slot)
                    pair_exps(n + 1, 1 - slot, 0)
                    pair_exps(n + 1, 1 - slot, 1)
                    pair_weights(n, slot, 0)
                    pair_exps(n + 1, 1 - slot, 2)
                    pair_weights(n, slot, 1)
                    pair_exps(n + 1, 1 - slot, 3)
                    pair_weights(n, slot, 2)
                    pair_weights(n, slot, 3)
                pair_outputs(n)

            copy_keys_values(0, 0)
            feature_copies(3)
            act.wait_ge(e_zero, 2)
            copy_queries(0, 0)
            for g in range(4):
                pair_exps(0, 0, g)
            pair_step(0, 0)
            pair_step(1, 1)
            with act.Fori(1, PAIRS // 2 - 1) as i:
                for u in range(2):
                    pair_step(i * 2 + u, u)
            pair_step(PAIRS - 2, 0)
            pair_step(PAIRS - 1, 1, last=True)
            table_of(ACT.Gelu)
            feature_copies(4)

            def gelus(e, slot, first=False):
                for half in range(2):
                    for f in range(F1):
                        u = F1 * half + f
                        act.wait_ge(g_up, e * 4 + u + 1)
                        if u == 0 and not first:
                            act.wait_ge(g_dn, e * 2 - 2)
                        fn(hid1[:, slot, f, half * HALF:(half + 1) * HALF], bank(BANK_S + u), ACT.Gelu,
                           bias=b1s[:, slot, f:f + 1]).then_inc(g_gelu, 1)

            for e in range(2):
                act.wait_ge(g_w1[e], 32)
                gelus(e, e, first=True)
                if e == 0:
                    act.wait_ge(g_sub, 1)
                    fn(sm[:, 1, :], sm[:, 0, :], ACT.Exp).then_inc(g_exp, 1)
            for half in range(2):
                act.wait_ge(g_ct, half + 1)
                fn(oT[0:E1, 4 * half:4 * half + 4, 0, :], tiles(bank(BANK_O + half)[0:E1, :], 4, P), ACT.Copy).then_inc(g_ctc, 1)
            with act.Fori(1, E1 // 2) as i:
                for u in range(2):
                    act.wait_ge(g_w1[u], (i + 1) * 32)
                    gelus(i * 2 + u, u)

        @block.vector
        def _(dve):
            dch = Chain(dve, dchain)
            tt, ts, stt = nc.vector.tensor_tensor, nc.vector.tensor_scalar, nc.vector.scalar_tensor_tensor

            def link(ins):
                dch(ins)
                dch.wait()

            def heads(a, count, finish_head):
                def maxima(n, slot, g):
                    dve.wait_ge(a.s, 4 * n + g + 1)
                    if g == 0 and not early(n, 2):
                        dve.wait_ge(a.msplit, n - 1)
                    nc.vector.tensor_reduce(negm[:, slot % 2, 4 * g:4 * g + 4], tiles(bank(BANK_S + g % 2), 4, P),
                                            AX.X, ALU.max, negate=True).then_inc(a.max, 1)

                def step(n, slot):
                    ahead = (slot + 2) % RING
                    if not late_head(n + 2, count):
                        maxima(n + 2, ahead, 0)
                        maxima(n + 2, ahead, 1)
                    if not early(n, 2):
                        finish_head(n - 2, slot % 2)
                    if not late_head(n + 2, count):
                        maxima(n + 2, ahead, 2)
                        maxima(n + 2, ahead, 3)

                for h in range(2):
                    for g in range(4):
                        maxima(h, h, g)
                for n in range(RING):
                    step(n, n)
                if count > 2 * RING:
                    with dve.Fori(1, count // RING - 1) as i:
                        dch.enter(i, 1, RING)
                        for u in range(RING):
                            step(i * RING + u, u)
                        dch.leave(count // RING - 2)
                for n in range(count - RING, count + 2):
                    step(n, n % RING)

            def finish_a(n, slot):
                dve.wait_ge(A.to, n + 1)
                if not early(n, 2):
                    dve.wait_ge(A.norm, n - 1)
                o = tiles(bank(BANK_M1), 16, 32)
                link(nc.vector.reciprocal(rz[:], o[:, :, 16]))
                tt(ot[:, slot], o[:, :, 0:16], along(rz[:], 16), ALU.mult).then_inc(A.div, 1)

            def finish_d(n, slot):
                dve.wait_ge(D.to, n + 1)
                o = tiles(bank(BANK_M1), 16, 32)
                link(nc.vector.reciprocal(rz[:], o[:, :, 8]))
                tt(oall[:, :, bass.ds(n * 16, 16)].rearrange("p b (c d) -> p c b d", c=2),
                   o[:, :, 0:8].rearrange("p (c b) d -> p c b d", c=2),
                   along(rz[:], 8).rearrange("p (c b) d -> p c b d", c=2), ALU.mult).then_inc(D.div, 1)

            def ln_stats(k, half):
                s = range(4 * half, 4 * half + 4)
                for b in s:
                    dch(nc.vector.bn_stats(bst[:, b, :], racc[:, b, :]))
                dch.wait()
                for b in s:
                    last = nc.vector.bn_aggr(mv[:, b, :], bst[:, b, :])
                    if b < s[-1]:
                        dch(last)
                last.then_inc(ln_var, 1)

            def ln_apply(k, half):
                s = range(4 * half, 4 * half + 4)
                dve.wait_ge(ln_rstd, 2 * k + half + 1)
                for b in s:
                    last = ts(xres[:, b, :], racc[:, b, :], mv[:, b, 0:1], rstd[:, b:b + 1], ALU.subtract, ALU.mult)
                    if b < s[-1]:
                        dch(last)
                last.then_inc(ln_out, 1)

            nc.vector.memset(zero[:], 0.0).then_inc(zeros, 1)
            for tile in (stq, stk):
                nc.vector.memset(tile[64:MROW].rearrange("p s c t -> p (s c t)").bitcast(F32), 0.0).then_inc(zeros, 1)
            dve.wait_ge(ld_c, 16)

            def rotary(n, t0, cos, sin):
                mine, other = (t0, t0 + 2) if n % 2 == 0 else (t0 + 2, t0)
                for k, (at, table) in enumerate(((mine, cos), (other, sin))):
                    last = tt(rope[:, 2 * n + k, :].rearrange("p (a b) -> p a b", b=P),
                              bank(at, 2).rearrange("p (a b) -> p a b", b=P), over(con[:, table:table + P], B), ALU.mult)
                    if k == 0:
                        dch(last)
                last.then_inc(A.mul, 1)

            def rest_part(a, n):
                dve.wait_ge(a.hi, n + 1)
                tt(rope[:, 2 * n + 1, :], rope[:, 2 * n, :], part[:, n, 0, :], ALU.subtract).then_inc(a.rest, 1)

            def low_part(a, n):
                dve.wait_ge(a.mid, n + 1)
                tt(part[:, n, 2, :], rope[:, 2 * n + 1, :], part[:, n, 1, :], ALU.subtract).then_inc(a.lo, 1)

            def rotate(n):
                dve.wait_ge(A.qk, 2 if n < 2 else 4)
                rotary(n, 0 if n < 2 else 4, *((C_COSQ, C_SINQ) if n < 2 else (C_COSK, C_SINK)))

            rotate(0)
            rotate(1)
            rotate(2)
            rest_part(A, 0)
            rotate(3)
            rest_part(A, 1)
            low_part(A, 0)
            rest_part(A, 2)
            low_part(A, 1)
            rest_part(A, 3)
            low_part(A, 2)
            low_part(A, 3)
            nc.vector.memset(w1a[64:MROW], 0.0).then_inc(zeros, 1)
            dve.wait_ge(ld_l, 16 * 6)
            link(tt(lamin[:, 0:2, :], lamin[:, 0:2, :], lamin[:, 2:4, :], ALU.mult))
            nc.vector.tensor_reduce(lams[:, 0:2], lamin[:, 0:2, :], AX.X, ALU.add).then_inc(lam_sum, 1)
            dve.wait_ge(lam_exp, 1)
            link(tt(lams[:, 4:5], lams[:, 3:4], lams[:, 2:3], ALU.subtract))
            link(ts(lams[:, 5:6], lams[:, 4:5], -(0.8 - 0.6), None, ALU.add))
            heads(A, NH, finish_a)
            for half in range(2):
                dve.wait_ge(A.y, half + 1)
                link(tt(half_of(racc, half), tiles(bank(BANK_O + half), 4, P), half_of(xres, half), ALU.add))
                ln_stats(0, half)
            ln_apply(0, 0)
            ln_apply(0, 1)

            for half in range(2):
                dve.wait_ge(b_q, half + 1)
                ts(qB[:, 4 * half:4 * half + 4, :], tiles(bank(BANK_S + half), 4, P), bqB[:, 0:1], float(P) ** -0.5,
                   ALU.add, ALU.mult).then_inc(b_qc, 1)
            for half in range(2):
                dve.wait_ge(b_s, half + 1)
                s = tiles(bank(BANK_T + half), 4, L)
                nc.vector.tensor_reduce(negm[:, 0, 4 * half:4 * half + 4], s, AX.X, ALU.max).then_inc(b_max, 1)
                dve.wait_ge(b_max, half + 1)
                tt(probs[:, 0, 4 * half:4 * half + 4, 0:L], s, along(negm[:, 0, 4 * half:4 * half + 4], L), ALU.subtract
                   ).then_inc(b_sub, 1)
            dve.wait_ge(resb, 1)
            for g, (lo, hi) in enumerate(((0, 3), (3, 6), (6, 8))):
                o = tiles(bank((BANK_T, BANK_T + 1, BANK_O + 1)[g]), hi - lo, 129)
                dve.wait_ge(b_pv, g + 1)
                link(nc.vector.reciprocal(rz[:, lo:hi], o[:, :, P]))
                for b in range(lo, hi):
                    dch(stt(racc[:, b, :], o[:, b - lo, 0:P], rz[:, b:b + 1], xres[:, b, :], ALU.mult, ALU.add))
                if g == 1:
                    dch.wait()
                    ln_stats(1, 0)
            dch.wait()
            ln_stats(1, 1)
            ln_apply(1, 0)
            ln_apply(1, 1)
            dve.wait_ge(ln_out, 4)
            for half in range(2):
                dve.wait_ge(f_hi, half + 1)
                tt(half_of(racc, half), half_of(xres, half), half_of(xpart[:, 0], half), ALU.subtract).then_inc(f_rest, 1)
            for half in range(2):
                dve.wait_ge(f_mid, half + 1)
                tt(half_of(xpart[:, 2], half), half_of(racc, half), half_of(xpart[:, 1], half), ALU.subtract
                   ).then_inc(f_part, 1)

            def by_token(n):
                return sm[:, n, 0:B * E0].rearrange("p (b e) -> p b e", e=E0)

            def by_expert(ap):
                return ap.rearrange("p (e b) -> p b e", b=B)

            logits = tiles(bank(BANK_S), B, E0)
            dve.wait_ge(f_log, 1)
            link(nc.vector.tensor_reduce(sm[:, 5, 0:B], logits, AX.X, ALU.max))
            tt(by_token(0), logits, along(sm[:, 5, 0:B], E0), ALU.subtract).then_inc(f_sub, 1)
            link(tt(by_token(2), logits, along(sm[:, 5, 0:B], E0), ALU.is_equal))
            link(nc.vector.tensor_tensor_scan(sm[:, 3, 0:64], con[:, C_R8:C_R8 + 64], sm[:, 2, 0:64], 0.0, ALU.mult, ALU.add))
            link(stt(by_expert(sm[:, 4, 0:64]), by_token(3), 1.0, by_token(2), ALU.is_equal, ALU.mult))
            link(nc.vector.tensor_tensor_scan(sm[:, 7, 0:64], con[:, C_R8:C_R8 + 64], sm[:, 4, 0:64], 0.0, ALU.mult, ALU.add))
            nc.vector.tensor_copy(smb[:, 0, :], sm[:, 4, 0:64]).then_inc(f_one, 1)
            tt(smb[:, 1, :], sm[:, 7, 0:64], sm[:, 4, 0:64], ALU.subtract).then_inc(f_one, 1)
            dve.wait_ge(f_exp, 1)
            link(nc.vector.tensor_reduce(sm[:, 6, 0:B], by_token(1), AX.X, ALU.add))
            link(nc.vector.reciprocal(sm[:, 6, 0:B], sm[:, 6, 0:B]))
            dve.wait_ge(f_cnt, 1)
            count = bank(BANK_S + 1)[:, 0:64]
            link(tt(sm[:, 7, 0:64], count, sm[:, 4, 0:64], ALU.mult))
            link(nc.vector.tensor_reduce(sm[:, 8, 0:B], by_expert(sm[:, 7, 0:64]), AX.X, ALU.add))
            link(ts(sm[:, 10, 0:B], sm[:, 8, 0:B], float(P), None, ALU.is_le))
            link(tt(sm[:, 7, 0:64], sm[:, 4, 0:64], con[:, C_EOFF:C_EOFF + 64], ALU.mult))
            link(nc.vector.tensor_reduce(sm[:, 9, 0:B], by_expert(sm[:, 7, 0:64]), AX.X, ALU.add))
            link(tt(sm[:, 9, 0:B], sm[:, 9, 0:B], sm[:, 8, 0:B], ALU.add))
            link(tt(sm[:, 9, 0:B], sm[:, 9, 0:B], sm[:, 10, 0:B], ALU.mult))
            ts(sm[:, 9, 0:B], sm[:, 9, 0:B], -1.0, None, ALU.add).then_inc(f_slot, 1)
            dve.wait_ge(f_slot, 1)
            for b in range(B):
                ts(sel[:, b, :], con[:, C_IOTA:C_IOTA + T], sm[:, 9, b:b + 1], None, ALU.is_equal).then_inc(f_sel, 1)
            dve.wait_ge(f_srowc, 2)
            for e in range(E0):
                ts(selT[:, e, :], slotrow[:], con[:, C_SLOT + e:C_SLOT + e + 1], None, ALU.is_equal).then_inc(f_selT, 1)
            for q in range(E0 // 2):
                two = slice(2 * q, 2 * q + 2)
                dve.wait_ge(f_ehi, q + 1)
                tt(eout[:, two, :], tiles(bank(BANK_PART[q]), 2, P), epart[:, 0, two, :], ALU.subtract).then_inc(f_erest, 1)
                dve.wait_ge(f_emid, q + 1)
                tt(epart[:, 2, two, :], eout[:, two, :], epart[:, 1, two, :], ALU.subtract).then_inc(f_epart, 1)
            for half in range(2):
                dve.wait_ge(f_y, half + 1)
                for k in range(4):
                    b = 4 * half + k
                    last = stt(racc[:, b, :], bank(BANK_T + half)[:, k * P:(k + 1) * P], sm[:, 6, b:b + 1], xres[:, b, :],
                               ALU.mult, ALU.add)
                    if k < 3:
                        dch(last)
                last.then_inc(f_r, 1)
                dve.wait_ge(f_r, half + 1)
                ln_stats(2, half)
            ln_apply(2, 0)
            ln_apply(2, 1)

            dve.wait_ge(ld_d, 16 * 10)
            for n in range(2):
                dve.wait_ge(D.qk, n + 1)
                ts(rope[:, 2 * n, :], bank(2 + 2 * n, 2), bqkD[:, n:n + 1], HD ** -0.5 if n == 0 else 1.0,
                   ALU.add, ALU.mult).then_inc(D.full, 1)
            rest_part(D, 0)
            rest_part(D, 1)
            low_part(D, 0)
            low_part(D, 1)
            for half in range(2):
                dve.wait_ge(D.vps, half + 1)
                tt(vall[:, 4 * half:4 * half + 4, 0:P], tiles(bank(6 + half), 4, P), over(bvD[:], 4), ALU.add).then_inc(D.vall, 1)
            heads(D, PAIRS, finish_d)
            dve.wait_ge(resb, 2)
            for half in range(2):
                dve.wait_ge(D.y, half + 1)
                link(tt(half_of(racc, half), tiles(bank(BANK_O + half), 4, P), half_of(xres, half), ALU.add))
                ln_stats(3, half)
            ln_apply(3, 0)
            ln_apply(3, 1)

            def pair_queries(n, slot):
                if not early(n, 2):
                    dve.wait_ge(e_s, 4 * (n - 1))
                for half in range(2):
                    dve.wait_ge(e_q, n * 2 + half + 1)
                    ts(qz[64:P, slot, 4 * half:4 * half + 4, 1, :], tiles(bank(BANK_M0 + half)[64:P, :], 4, P), XD ** -0.5,
                       None, ALU.mult).then_inc(e_qd, 1)

            def pair_maxima(n, slot):
                if not early(n, 2):
                    dve.wait_ge(e_pt, 4 * (n - 1))
                for g in range(4):
                    dve.wait_ge(e_s, n * 4 + g + 1)
                    s = tiles(bank(BANK_S + g % 2), 4, L)
                    nc.vector.tensor_reduce(negm[:, slot, 4 * g:4 * g + 4], s, AX.X, ALU.max).then_inc(e_max, 1)
                    dve.wait_ge(e_max, n * 4 + g + 1)
                    tt(probs[:, slot, 4 * g:4 * g + 4, 0:L], s, along(negm[:, slot, 4 * g:4 * g + 4], L),
                       ALU.subtract).then_inc(e_sub, 1)

            def pair_sums(n, slot):
                if not early(n, 2):
                    dve.wait_ge(e_norm, 4 * (n - 1))
                for g in range(4):
                    r = rzE[:, slot, 4 * g:4 * g + 4]
                    dve.wait_ge(e_exp, n * 4 + g + 1)
                    link(nc.vector.tensor_reduce(r, probs[:, slot, 4 * g:4 * g + 4, 0:L], AX.X, ALU.add))
                    nc.vector.reciprocal(r, r).then_inc(e_rz, 1)

            dve.wait_ge(e_zero, 2)
            pair_queries(0, 0)
            pair_maxima(0, 0)
            pair_queries(1, 1)
            pair_sums(0, 0)
            pair_maxima(1, 1)
            pair_sums(1, 1)
            with dve.Fori(1, PAIRS // 2) as i:
                dch.enter(i, 1, 2 * 4)
                for u in range(2):
                    pair_queries(i * 2 + u, u)
                    pair_maxima(i * 2 + u, u)
                    pair_sums(i * 2 + u, u)
                dch.leave(PAIRS // 2 - 1)
            dve.wait_ge(resb, 3)
            for half in range(2):
                dve.wait_ge(e_y, half + 1)
                link(tt(half_of(racc, half), tiles(bank(BANK_O + half), 4, P), half_of(xres, half), ALU.add))
                ln_stats(4, half)
            ln_apply(4, 0)
            ln_apply(4, 1)

            def b16(n):
                return sm[:, n, :].rearrange("p (b e) -> p b e", e=E1)

            dve.wait_ge(g_log, 1)
            link(tt(b16(5), tiles(bank(BANK_O), B, E1), over(rb1[:], B), ALU.add))
            top = sm[:, 9, 0:B * 8].rearrange("p (b k) -> p b k", k=8)
            for b in range(B):
                dch(nc.vector.max(top[:, b, :], b16(5)[:, b, :]))
            dch.wait()
            tt(b16(0), b16(5), top[:, :, 0:1].to_broadcast([P, B, E1]), ALU.subtract).then_inc(g_sub, 1)
            fourth = top[:, :, TOPK - 1:TOPK].to_broadcast([P, B, E1])
            dch(tt(b16(2), b16(5), fourth, ALU.is_gt))
            link(tt(b16(3), b16(5), fourth, ALU.is_equal))
            dch(nc.vector.tensor_reduce(sm[:, 6, 0:B], b16(2), AX.X, ALU.add))
            link(nc.vector.tensor_tensor_scan(sm[:, 4, :], con[:, C_R16:C_R16 + B * E1], sm[:, 3, :], 0.0, ALU.mult, ALU.add))
            link(ts(sm[:, 6, 0:B], sm[:, 6, 0:B], -1.0, float(TOPK), ALU.mult, ALU.add))
            link(tt(b16(4), b16(4), along(sm[:, 6, 0:B], E1), ALU.is_le))
            link(tt(b16(3), b16(3), b16(4), ALU.mult))
            link(tt(b16(7), b16(2), b16(3), ALU.add))
            dve.wait_ge(g_exp, 1)
            link(tt(b16(7), b16(7), b16(1), ALU.mult))
            link(nc.vector.tensor_reduce(sm[:, 8, 0:B], b16(7), AX.X, ALU.add))
            link(nc.vector.reciprocal(sm[:, 8, 0:B], sm[:, 8, 0:B]))
            tt(b16(11), b16(7), along(sm[:, 8, 0:B], E1), ALU.mult).then_inc(g_c, 1)
            for half in range(2):
                dve.wait_ge(g_b2, half + 1)
                tt(half_of(racc, half), tiles(bank(BANK_O + half), 4, P), half_of(xres, half), ALU.add).then_inc(g_acc, 1)

            def accumulate(e, slot, half):
                banks = (BANK_M0, BANK_O)[slot]
                dve.wait_ge(g_dn, e * 2 + half + 1)
                dve.wait_ge(g_acc, e * 2 + half + 1)
                for k in range(4):
                    b = 4 * half + k
                    last = stt(racc[:, b, :], bank(banks + half)[:, k * P:(k + 1) * P],
                               sm[:, 11, bass.ds(b * E1 + e, 1)], racc[:, b, :], ALU.mult, ALU.add)
                    if k < 3:
                        dch(last)
                last.then_inc(g_acc, 1)

            for e in range(2):
                for half in range(2):
                    accumulate(e, e, half)
            with dve.Fori(1, E1 // 2 - 1) as i:
                dch.enter(i, 1, 12)
                for u in range(2):
                    for half in range(2):
                        accumulate(i * 2 + u, u, half)
                dch.leave(E1 // 2 - 2)
            for half in range(2):
                accumulate(E1 - 2, 0, half)
            for half in range(2):
                accumulate(E1 - 1, 1, half)
                dve.wait_ge(g_acc, 2 * E1 + half + 1)
                dch.wait()
                ln_stats(5, half)
            ln_apply(5, 0)
            ln_apply(5, 1)


def kernel(**inputs):
    import concourse.bacc as bacc
    from concourse.bass_utils import run_bass_kernel_spmd

    a = {k: np.asarray(v) for k, v in inputs.items()}
    wqkv0 = a["L0_attn_W_qkv"]
    w1 = a["L1_attn_Wqkv"]
    bq1 = a["L1_attn_bqkv"]

    def pair_order(w):
        n = w.shape[1]
        return w.reshape(PAIRS, 2, n, HD).transpose(2, 0, 3, 1).reshape(n, P)

    wkv = a["L1_xattn_w_kv"]
    arrays = {
        "con": constant_table(),
        "xT": a["x"].reshape(T, P).T,
        "x": a["x"].transpose(1, 0, 2),
        "ctxT": a["ctx_768"].reshape(B * L, CD).T,
        "wqk0": wqkv0[:4 * P].reshape(4, P, P).transpose(2, 0, 1),
        "wv0": wqkv0[4 * P:].reshape(2, NH, HD, P).transpose(3, 1, 0, 2).reshape(P, 2 * P),
        "wproj0": a["L0_attn_W_proj"].reshape(P, 2, P).transpose(2, 1, 0),
        "lq1": a["L0_attn_lambda_q1"].reshape(1, HD), "lq2": a["L0_attn_lambda_q2"].reshape(1, HD),
        "lk1": a["L0_attn_lambda_k1"].reshape(1, HD), "lk2": a["L0_attn_lambda_k2"].reshape(1, HD),
        "wqB": a["L0_xattn_Wq"], "wkB": a["L0_xattn_Wk"], "wvB": a["L0_xattn_Wv"],
        "bqB": a["L0_xattn_bq"].reshape(P, 1), "bkB": a["L0_xattn_bk"].reshape(P, 1), "bvB": a["L0_xattn_bv"].reshape(1, P),
        "rw0": a["L0_ffn_router_w"],
        "w1a": a["L0_ffn_w1"].transpose(1, 0, 2),
        "w2a": a["L0_ffn_w2"].reshape(E0, F0, P, P).transpose(2, 0, 1, 3),
        "wqkD": np.stack([pair_order(w1[:, :, 0:HD]), pair_order(w1[:, :, HD:2 * HD])], 1),
        "wvD": w1[:, :, 2 * HD:].transpose(1, 0, 2).reshape(P, P),
        "bqkD": np.stack([pair_order(bq1[:, None, 0:HD])[0], pair_order(bq1[:, None, HD:2 * HD])[0]], 1),
        "bvD": bq1[:, 2 * HD:].reshape(1, P),
        "woD": a["L1_attn_Wout"], "boD": a["L1_attn_bout"].reshape(1, P),
        "wqE": a["L1_xattn_w_q"], "wkE": wkv[:, :NH * XD], "wvE": wkv[:, NH * XD:],
        "woE": a["L1_xattn_w_out"].reshape(PAIRS, P, P).transpose(1, 0, 2), "boE": a["L1_xattn_b_out"].reshape(1, P),
        "rw1": a["L1_ffn_router_w"], "rb1": a["L1_ffn_router_b"].reshape(1, E1), "b2s": a["L1_ffn_b2"],
        "w1b": a["L1_ffn_w1"], "b1": a["L1_ffn_b1"].reshape(E1, F1, P).transpose(0, 2, 1),
        "w2b": a["L1_ffn_w2"].reshape(E1, F1, P, P).transpose(0, 2, 1, 3),
    }
    nc = bacc.Bacc("TRN2", target_bir_lowering=False, num_devices=1)
    feed, d = {}, {}
    for name, v in arrays.items():
        v = np.ascontiguousarray(v)
        feed[f"in_{name}"] = v
        d[name] = nc.dram_tensor(f"in_{name}", v.shape, mybir.dt.from_np(v.dtype), kind="ExternalInput").ap()
    out = nc.dram_tensor("out", (P, B, P), F32, kind="ExternalOutput").ap()
    decoder_kernel(nc, d, out)
    r = run_bass_kernel_spmd(nc, [feed], core_ids=[0])
    return r.results[0]["out"].transpose(1, 0, 2)
```
